# Optimizing a Trainium2 kernel written in Bass

```python
import numpy as np
import jax
import jax.numpy as jnp

def _softmax(x, axis=-1):
    return jax.nn.softmax(x, axis=axis)

def _gelu(x):
    return jax.nn.gelu(x, approximate=True)

def _silu(x):
    return jax.nn.silu(x)

def _sigmoid(x):
    return jax.nn.sigmoid(x)

def _layernorm(x, axis=-1, eps=1e-05):
    m = jnp.mean(x, axis=axis, keepdims=True)
    v = jnp.var(x, axis=axis, keepdims=True)
    return (x - m) / jnp.sqrt(v + eps)

def _scatter_add(tgt, idx, src, axis=0):
    return tgt.at[idx].add(src)

def _segment_sum(src, seg, n):
    return jax.ops.segment_sum(src, seg, n)
kernel_name = 'mk_seq_preln_d2_jaxref_r4_259061'

def setup_inputs(seed: int=0):
    np.random.seed(seed)
    _w = jnp.asarray

    def _L0_attn_setup():
        import jax, jax.numpy as jnp
        import numpy as np
        from math import sqrt
        D_MODEL = 256
        NUM_HEADS = 16
        MASK_VAL = -100000000.0

        def _proj_heads(x, w, h):
            d = w.shape[0] // h
            w = w.reshape(h, d, w.shape[1])
            return jnp.einsum('bsi,hdi->bhsd', x, w)
        key = jax.random.key(seed)
        k1, k2, k3, k4, k5 = jax.random.split(key, 5)
        scale = 1.0 / sqrt(D_MODEL)
        return {'in_features': jax.random.normal(k1, (2, 512, D_MODEL), dtype=jnp.float32), 'q_proj_weight': jax.random.normal(k2, (D_MODEL, D_MODEL), dtype=jnp.float32) * scale, 'k_proj_weight': jax.random.normal(k3, (D_MODEL, D_MODEL), dtype=jnp.float32) * scale, 'v_proj_weight': jax.random.normal(k4, (D_MODEL, D_MODEL), dtype=jnp.float32) * scale, 'o_proj_weight': jax.random.normal(k5, (D_MODEL, D_MODEL), dtype=jnp.float32) * scale}
    _L0_attn_in = _L0_attn_setup()

    def _L0_ffn_setup():
        import jax, jax.numpy as jnp
        import numpy as np
        TOP_K = 2
        E = 8
        D = 256
        F = 512
        B, S = (2, 256)
        key = jax.random.key(seed)
        ks = jax.random.split(key, 8)
        sc = 0.02
        return {'x_bsD': jax.random.normal(ks[0], (B, S, D), dtype=jnp.float32), 'router_DE': jax.random.normal(ks[1], (D, E), dtype=jnp.float32) * sc, 'w_in_shared_FD': jax.random.normal(ks[2], (F, D), dtype=jnp.float32) * sc, 'w_out_shared_DF': jax.random.normal(ks[3], (D, F), dtype=jnp.float32) * sc, 'w_swiglu_FD': jax.random.normal(ks[4], (F, D), dtype=jnp.float32) * sc, 'w_in_eDF': jax.random.normal(ks[5], (E, D, F), dtype=jnp.float32) * sc, 'w_swiglu_eDF': jax.random.normal(ks[6], (E, D, F), dtype=jnp.float32) * sc, 'w_out_eFD': jax.random.normal(ks[7], (E, F, D), dtype=jnp.float32) * sc}
    _L0_ffn_in = _L0_ffn_setup()

    def _L1_attn_setup():
        import jax, jax.numpy as jnp
        import numpy as np
        B, S, D = (4, 512, 256)
        key = jax.random.key(seed)
        k1, k2 = jax.random.split(key)
        x = jax.random.normal(k1, (B, S, D), dtype=jnp.float32)
        W = jax.random.normal(k2, (2 * D, D), dtype=jnp.float32) * 0.02
        return {'x': x, 'W': W}
    _L1_attn_in = _L1_attn_setup()

    def _L1_ffn_setup():
        import jax, jax.numpy as jnp
        import numpy as np
        EPS = 1e-05

        def _quantize(W):
            gamma = jnp.mean(jnp.abs(W))
            return jnp.clip(jnp.round(W / (gamma + EPS)), -1.0, 1.0)
        key = jax.random.key(seed)
        k_x, k_w1, k_b1, k_w2, k_b2 = jax.random.split(key, 5)
        n_embd = 256
        d_ff = 4 * n_embd
        B, S = (4, 1024)
        bound1 = 1.0 / np.sqrt(n_embd)
        bound2 = 1.0 / np.sqrt(d_ff)
        x = jax.random.normal(k_x, (B, S, n_embd), dtype=jnp.float32)
        W1 = jax.random.uniform(k_w1, (d_ff, n_embd), jnp.float32, -bound1, bound1)
        b1 = jax.random.uniform(k_b1, (d_ff,), jnp.float32, -bound1, bound1)
        W2 = jax.random.uniform(k_w2, (n_embd, d_ff), jnp.float32, -bound2, bound2)
        b2 = jax.random.uniform(k_b2, (n_embd,), jnp.float32, -bound2, bound2)
        return {'x': x, 'W1': W1, 'b1': b1, 'W2': W2, 'b2': b2}
    _L1_ffn_in = _L1_ffn_setup()
    _d = {'L0_attn_in_features': _L0_attn_in['in_features'], 'L0_attn_q_proj_weight': _L0_attn_in['q_proj_weight'], 'L0_attn_k_proj_weight': _L0_attn_in['k_proj_weight'], 'L0_attn_v_proj_weight': _L0_attn_in['v_proj_weight'], 'L0_attn_o_proj_weight': _L0_attn_in['o_proj_weight'], 'L0_ffn_router_DE': _L0_ffn_in['router_DE'], 'L0_ffn_w_in_shared_FD': _L0_ffn_in['w_in_shared_FD'], 'L0_ffn_w_out_shared_DF': _L0_ffn_in['w_out_shared_DF'], 'L0_ffn_w_swiglu_FD': _L0_ffn_in['w_swiglu_FD'], 'L0_ffn_w_in_eDF': _L0_ffn_in['w_in_eDF'], 'L0_ffn_w_swiglu_eDF': _L0_ffn_in['w_swiglu_eDF'], 'L0_ffn_w_out_eFD': _L0_ffn_in['w_out_eFD'], 'L1_attn_W': _L1_attn_in['W'], 'L1_ffn_W1': _L1_ffn_in['W1'], 'L1_ffn_b1': _L1_ffn_in['b1'], 'L1_ffn_W2': _L1_ffn_in['W2'], 'L1_ffn_b2': _L1_ffn_in['b2']}
    _x0 = _d['L0_attn_in_features']
    _d['L0_attn_in_features'] = jax.random.normal(jax.random.fold_in(jax.random.key(seed), 1), (2, 2048, 256), dtype=_x0.dtype)
    del _x0
    return _d

def reference(L0_attn_in_features, L0_attn_q_proj_weight, L0_attn_k_proj_weight, L0_attn_v_proj_weight, L0_attn_o_proj_weight, L0_ffn_router_DE, L0_ffn_w_in_shared_FD, L0_ffn_w_out_shared_DF, L0_ffn_w_swiglu_FD, L0_ffn_w_in_eDF, L0_ffn_w_swiglu_eDF, L0_ffn_w_out_eFD, L1_attn_W, L1_ffn_W1, L1_ffn_b1, L1_ffn_W2, L1_ffn_b2):

    def _L0_attn_ref(in_features, q_proj_weight, k_proj_weight, v_proj_weight, o_proj_weight):
        import jax, jax.numpy as jnp
        import numpy as np
        from math import sqrt
        D_MODEL = 256
        NUM_HEADS = 16
        MASK_VAL = -100000000.0

        def _proj_heads(x, w, h):
            d = w.shape[0] // h
            w = w.reshape(h, d, w.shape[1])
            return jnp.einsum('bsi,hdi->bhsd', x, w)
        h = NUM_HEADS
        b, s, _ = in_features.shape
        q = _proj_heads(in_features, q_proj_weight, h)
        k = _proj_heads(in_features, k_proj_weight, h)
        v = _proj_heads(in_features, v_proj_weight, h)
        d_k = q.shape[-1]
        mask = jnp.triu(jnp.full((s, s), MASK_VAL, dtype=q.dtype), k=1)[None, None]
        scores = jnp.einsum('bhqd,bhkd->bhqk', q, k) / sqrt(d_k) + mask
        attn = jax.nn.softmax(scores, axis=-1)
        out = jnp.einsum('bhqk,bhkd->bhqd', attn, v)
        out = out.transpose(0, 2, 1, 3).reshape(b, s, -1)
        return jnp.einsum('bsv,mv->bsm', out, o_proj_weight)

    def _L0_ffn_ref(x_bsD, router_DE, w_in_shared_FD, w_out_shared_DF, w_swiglu_FD, w_in_eDF, w_swiglu_eDF, w_out_eFD):
        import jax, jax.numpy as jnp
        import numpy as np
        TOP_K = 2
        E = 8
        D = 256
        F = 512
        B, S = (2, 256)
        b, s, d = x_bsD.shape
        x_aD = x_bsD.reshape(-1, d)
        a = x_aD.shape[0]
        scores_aE = x_aD @ router_DE
        topv_aK, topi_aK = jax.lax.top_k(scores_aE, TOP_K)
        masked_aE = jnp.full_like(scores_aE, -jnp.inf)
        masked_aE = masked_aE.at[jnp.arange(a)[:, None], topi_aK].set(topv_aK)
        gates_Ea = jax.nn.sigmoid(masked_aE.astype(jnp.float32)).astype(x_aD.dtype).T
        routed_in_EaD = x_aD[None, :, :] * gates_Ea[:, :, None]
        routed_in_EaD = jax.lax.stop_gradient(routed_in_EaD)
        mid_EaF = jnp.einsum('ead,edf->eaf', routed_in_EaD, w_in_eDF)
        sw_EaF = jnp.einsum('ead,edf->eaf', routed_in_EaD, w_swiglu_eDF)
        h_EaF = jax.nn.silu(mid_EaF) * sw_EaF
        out_EaD = jnp.einsum('eaf,efd->ead', h_EaF, w_out_eFD)
        shared_aF = jax.nn.silu(x_aD @ w_in_shared_FD.T) * (x_aD @ w_swiglu_FD.T)
        shared_out_aD = jax.lax.stop_gradient(shared_aF @ w_out_shared_DF.T)
        out_aD = shared_out_aD + jnp.sum(out_EaD, axis=0)
        return out_aD.reshape(b, s, d)

    def _L1_attn_ref(x, W):
        import jax, jax.numpy as jnp
        import numpy as np
        B, S, D = (4, 512, 256)
        d = x.shape[-1]
        kv = x @ W.T
        K, V = (kv[..., :d], kv[..., d:])
        n = x.shape[-2]
        causal = jnp.tril(jnp.ones((n, n), dtype=bool))
        mask = jnp.where(causal, jnp.float32(0.0), -jnp.inf).astype(x.dtype)
        scores = jnp.einsum('bqd,bkd->bqk', x, K) + mask
        attn = jax.nn.softmax(scores, axis=-1)
        return x + jnp.einsum('bqk,bkd->bqd', attn, V)

    def _L1_ffn_ref(x, W1, b1, W2, b2):
        import jax, jax.numpy as jnp
        import numpy as np
        EPS = 1e-05

        def _quantize(W):
            gamma = jnp.mean(jnp.abs(W))
            return jnp.clip(jnp.round(W / (gamma + EPS)), -1.0, 1.0)
        Wq1 = _quantize(W1)
        Wq2 = _quantize(W2)
        h = jax.nn.relu(jnp.einsum('bsd,fd->bsf', x, Wq1) + b1)
        out = jnp.einsum('bsf,df->bsd', h, Wq2) + b2
        return out
    x = L0_attn_in_features
    x = x + _L0_attn_ref(_layernorm(x, axis=-1), L0_attn_q_proj_weight, L0_attn_k_proj_weight, L0_attn_v_proj_weight, L0_attn_o_proj_weight)
    x = x + _L0_ffn_ref(_layernorm(x, axis=-1), L0_ffn_router_DE, L0_ffn_w_in_shared_FD, L0_ffn_w_out_shared_DF, L0_ffn_w_swiglu_FD, L0_ffn_w_in_eDF, L0_ffn_w_swiglu_eDF, L0_ffn_w_out_eFD)
    x = x + _L1_attn_ref(_layernorm(x, axis=-1), L1_attn_W)
    x = x + _L1_ffn_ref(_layernorm(x, axis=-1), L1_ffn_W1, L1_ffn_b1, L1_ffn_W2, L1_ffn_b2)
    return x

_drawn_inputs = setup_inputs


def setup_inputs(seed=0):
    import zlib

    import numpy as np

    out = dict(_drawn_inputs(seed))
    spreads = {}
    factors = {'L0_ffn_router_DE': 5.489,
     'L0_ffn_w_in_eDF': 4.748,
     'L0_ffn_w_swiglu_eDF': 4.743,
     'L0_ffn_w_out_eFD': 4.723,
     'L1_ffn_b1': 21.719,
     'L1_ffn_b2': 200.0,
     'L0_ffn_w_in_shared_FD': 7.486,
     'L0_ffn_w_out_shared_DF': 7.411,
     'L0_ffn_w_swiglu_FD': 7.387,
     'L1_attn_W': 3.879}
    for name, (base, spread) in spreads.items():
        noise = np.random.default_rng([zlib.crc32(name.encode()), seed]).standard_normal(out[name].shape)
        drawn = base * np.exp(spread * noise) if base else spread * noise
        out[name] = jnp.asarray(drawn.astype(out[name].dtype))
    for name, factor in factors.items():
        out[name] = (out[name] * factor).astype(out[name].dtype)
    return out
```

```python
from contextlib import ExitStack, contextmanager

import concourse.bass as bass
from concourse import mybir

F32 = mybir.dt.float32
F32R = mybir.dt.float32r
BF16 = mybir.dt.bfloat16
I32 = mybir.dt.int32
ALU = mybir.AluOpType
ACT = mybir.ActivationFunctionType
AX = mybir.AxisListType

P = 128
BATCH, SEQ, D = 2, 2048, 256
TOK = BATCH * SEQ
DC = D // P
TILES = TOK // P
TB = 4
BT = TB * P
BLOCKS = TOK // BT
HEADS, DH = 16, D // 16
HG = 4
GROUPS = HEADS // HG
EPS = 1e-5
SHIFT_ROWS = 6 * DH
KROWS = SHIFT_ROWS + 3
UNITS = GROUPS * BATCH
Q_SLOTS, K_SLOTS = (0, 0, 1, 1, 0, 2), (0, 1, 0, 1, 2, 0)
SAFE_SQUARE = 48.0 ** 2


EXPERTS, TOP_K, FF = 8, 2, 512
FC = FF // P
SLOT_TILES = TOP_K * TOK // P + EXPERTS
SLOTS = SLOT_TILES * P


def sem(k, name):
    handle = k["sem_ctx"].enter_context(k["nc"].semaphore(name))
    k["used"].append(handle)
    return handle


def sems(k, stem, names):
    return [sem(k, f"{stem}_{n}") for n in names.split()]


@contextmanager
def semaphores(k):
    with ExitStack() as k["sem_ctx"]:
        k["used"] = []
        yield
        with k["nc"].Block() as block:

            @block.gpsimd
            def _(pool):
                for handle in k["used"]:
                    pool.sem_clear(handle)


def wait_past(eng, sem, value):
    if not isinstance(value, int) or value > 0:
        eng.wait_ge(sem, value)


def hold(eng, k, sem, value):
    eng.wait_ge(sem, value)
    eng.sem_inc(k["passed"], 1)


def is_first(i):
    return isinstance(i, int) and i == 0


def is_last(i, count):
    return isinstance(i, int) and i == count - 1


def at_least(value):
    return max(value, 0) if isinstance(value, int) else value


def over_blocks(eng, count, body):
    for j in range(2):
        body(j, j, 0)
    if count > 4:
        with eng.Fori(1, count // 2 - 1) as n:
            for j in range(2):
                body(2 * n + j, j, n)
    for j in range(2):
        body(count - 2 + j, j, count // 2 - 1)


def mm3(pe, out, lhs, rhs, start, stop):
    (lh, ll), (rh, rl) = lhs, rhs
    pe.matmul(out, lh, rh, start=start, stop=False)
    pe.matmul(out, lh, rl, start=False, stop=False)
    return pe.matmul(out, ll, rh, start=False, stop=stop)


def turner(k, stem, ps):
    ps_ok, hi_ok, lo_ok = sems(k, stem, "ps_ok hi_ok lo_ok")
    return {"ps": ps, "ident": k["ident"], "ps_ok": ps_ok, "hi_ok": hi_ok, "lo_ok": lo_ok}


def turn_block(pe, w, i, rows):
    wait_past(pe, w["lo_ok"], DC * i)
    for t in range(TB):
        for c in range(DC):
            last = pe.transpose(w["ps"][:, c, t * P:(t + 1) * P], rows(t, c), w["ident"][:, :])
    last.then_inc(w["ps_ok"], 1)


def high_parts(act, w, i, out):
    act.wait_ge(w["ps_ok"], i + 1)
    for c in range(DC):
        act.activation(out(c), w["ps"][:, c], ACT.Copy).then_inc(w["hi_ok"], 1)


def low_parts(dve, w, i, out, high):
    for c in range(DC):
        dve.wait_ge(w["hi_ok"], DC * i + c + 1)
        dve.tensor_tensor(out(c), w["ps"][:, c], high(c).bitcast(F32), ALU.subtract).then_inc(w["lo_ok"], 1)


def split_weights(dve, raw, hi, lo, sem, at):
    dve.tensor_copy(hi, raw).then_inc(sem, 1)
    dve.wait_ge(sem, at + 1)
    dve.tensor_tensor(lo, raw, hi.bitcast(F32), ALU.subtract).then_inc(sem, 1)


def phase_constants(k):
    nc = k["nc"]
    made, picked = sems(k, "constants", "made picked")
    with nc.Block() as block:

        @block.gpsimd
        def _(pool):
            pool.memset(k["ident"][:, :], 0.0).then_inc(made, 1)
            pool.memset(k["head_sel"][:, :], 1.0).then_inc(made, 1)
            pool.memset(k["eps"][:, :], EPS).then_inc(made, 1)
            pool.memset(k["causal"][:, :], 0.0).then_inc(made, 1)
            pool.memset(k["V"][:, :, :, :, DH:DH + 1], 1.0).then_inc(made, 1)
            pool.wait_ge(made, 5)
            pool.affine_select(out=k["causal"][:, :], in_=k["causal"][:, :], compare_op=ALU.is_ge, fill=-3.0e38,
                               base=0, pattern=[[-1, P]], channel_multiplier=1).then_inc(picked, 1)
            pool.affine_select(out=k["ident"][:, :], in_=k["ident"][:, :], compare_op=ALU.not_equal, fill=1.0,
                               base=0, pattern=[[-1, P]], channel_multiplier=1).then_inc(picked, 1)
            pool.affine_select(out=k["head_sel"][:, :], in_=k["head_sel"][:, :], compare_op=ALU.is_ge, fill=0.0,
                               base=0, pattern=[[-DH, P // DH]], channel_multiplier=1).then_inc(picked, 1)
            pool.wait_ge(picked, 3)
            pool.affine_select(out=k["head_sel"][:, :], in_=k["head_sel"][:, :], compare_op=ALU.is_ge, fill=0.0,
                               base=DH - 1, pattern=[[DH, P // DH]], channel_multiplier=-1).then_inc(picked, 1)


def layer_norm(k, mem, stem):
    nc = k["nc"]
    norm = {"X": k["X"], "eps": k["eps"], "k": k}
    for name, shape in (("stats", [P, 2, TB, 6]), ("moments", [P, 2, TB, 2]), ("std", [P, 2, TB]), ("rstd", [P, 2, TB])):
        norm[name] = mem.enter_context(nc.sbuf_tensor(f"{stem}_{name}", shape, F32))
    for name in ("stats_ok", "moments_ok", "std_ok", "rstd_ok", "xn_ok"):
        norm[name] = sem(k, f"{stem}_{name}")
    return norm


def norm_measure(dve, w, b, j, first=0):
    for t in range(TB):
        dve.bn_stats(w["stats"][:, j, t, :], w["X"][:, bass.ds(first + TB * b + t, 1), :]).then_inc(w["stats_ok"], 1)
    hold(dve, w["k"], w["stats_ok"], TB * b + TB)
    for t in range(TB):
        dve.bn_aggr(w["moments"][:, j, t, :], w["stats"][:, j, t, :]).then_inc(w["moments_ok"], 1)


def norm_root(act, w, b, j):
    act.wait_ge(w["moments_ok"], TB * b + TB)
    act.activation(w["std"][:, j], w["moments"][:, j, :, 1], ACT.Sqrt, bias=w["eps"][:, 0:1]).then_inc(w["std_ok"], 1)


def norm_apply(dve, w, b, j, out, first=0):
    dve.wait_ge(w["std_ok"], b + 1)
    dve.reciprocal(w["rstd"][:, j], w["std"][:, j]).then_inc(w["rstd_ok"], 1)
    dve.wait_ge(w["rstd_ok"], b + 1)
    for t in range(TB):
        last = dve.tensor_scalar(out(t), w["X"][:, bass.ds(first + TB * b + t, 1), :], w["moments"][:, j, t, 0:1],
                                 w["rstd"][:, j, t:t + 1], ALU.subtract, ALU.mult)
    last.then_inc(w["xn_ok"], 1)


def phase_qkv(k):
    nc, io = k["nc"], k["io"]
    with ExitStack() as mem:
        def sb(name, shape, dt):
            return mem.enter_context(nc.sbuf_tensor(name, shape, dt))

        def ps(name, shape, dt=F32):
            return mem.enter_context(nc.psum_tensor(name, shape, dt))

        w_raw = sb("w_raw", [P, 3, DC, D], F32)
        w_hi = sb("w_hi", [P, 3, DC, D], F32R)
        w_lo = sb("w_lo", [P, 3, DC, D], F32R)
        xn = sb("xn1", [P, 2, TB, D], F32)
        xnT_hi = sb("xn1T_hi", [P, 2, DC, BT], F32R)
        xnT_lo = sb("xn1T_lo", [P, 2, DC, BT], F32R)
        part1 = sb("part1", [P, 2, 4, BT], BF16)
        part2 = sb("part2", [P, 2, 4, BT], BF16)
        part3 = sb("part3", [P, 2, 4, BT], BF16)
        rest = sb("rest", [P, 2, 4, BT], F32)
        square = sb("square", [P, 2, 4, BT], BF16)
        norm_max = sb("norm_max", [P, BLOCKS], F32)
        norm_top = sb("norm_top", [P, 1], F32)
        norm_row = sb("norm_row", [1, P], F32)
        over = sb("over", [1, 2, 8], F32)
        zeros = sb("shift_zeros", [P, HEADS * TOK * 3 // P], BF16)
        ps_t = ps("ps_t", [P, DC, BT])
        ps_qk = ps("ps_qk", [P, 4, BT])
        ps_v = ps("ps_v", [P, 2, D])
        ps_n = ps("ps_n", [P, BT])
        norm = layer_norm(k, mem, "ln1")

        w_in, w_split, zero_ok, zero_out = sems(k, "qkv", "w_in w_split zero_ok zero_out")
        x_in = sems(k, "x_in", "even odd")
        parts_out = sems(k, "parts_out", "even odd")
        t_ok, t_hi_ok, t_lo_ok = sems(k, "qkv", "t_ok t_hi_ok t_lo_ok")
        qk_ok, part1_ok, rest_ok, part2_ok, part3_ok = sems(k, "qkv", "qk_ok part1_ok rest_ok part2_ok part3_ok")
        v_ok, v_used, n_ok, n_used, top_ok, topT_ok, row_ok = sems(k, 
            "qkv", "v_ok v_used n_ok n_used top_ok topT_ok row_ok")

        x_view = io["x"].rearrange("(n p) d -> p n d", p=P)
        with nc.Block() as block:

            @block.sync
            def _(sp):
                sp.dma_start(k["X"][:, 0:TB, :], x_view[:, 0:TB, :]).then_inc(x_in[0], 16)
                for n, name in enumerate("qkv"):
                    sp.dma_start(w_raw[:, n], io["w" + name].rearrange("(c p) n -> p c n", p=P)).then_inc(w_in, 16)
                for b in range(1, BLOCKS):
                    wait_past(sp, x_in[b % 2], 16 * (b // 2))
                    sp.dma_start(k["X"][:, b * TB:(b + 1) * TB, :],
                                 x_view[:, b * TB:(b + 1) * TB, :]).then_inc(x_in[b % 2], 16)
                sp.wait_ge(zero_ok, 1)
                sp.dma_start(io["shift"].rearrange("m g b h t -> (m g b h t)").rearrange("(p n) -> p n", p=P),
                             zeros[:, :]).then_inc(zero_out, 16)
                for b in range(BLOCKS):
                    j = b % 2
                    sp.wait_ge(part3_ok, b + 1)
                    t0 = b * BT % SEQ
                    for n, part in enumerate((part1, part2, part3)):
                        for m in range(2):
                            to = io["qk"][m, n, :, b * BT // SEQ, :, t0:t0 + BT].rearrange(
                                "(c g) r t -> g r c t", c=DC)
                            for g in range(2):
                                sp.dma_start(to[g], part[64 * g:64 * g + 64, j, DC * m:DC * m + DC]).then_inc(
                                    parts_out[j], 16)
                for j in range(2):
                    sp.wait_ge(parts_out[j], 192 * (BLOCKS // 2))
                sp.wait_ge(zero_out, 16)

            @block.gpsimd
            def _(pool):
                pool.memset(zeros[:, :].bitcast(I32), 0).then_inc(zero_ok, 1)

                def body(i, j, n):
                    pool.wait_ge(part2_ok, i + 1)
                    wait_past(pool, parts_out[j], 192 * n)
                    pool.tensor_tensor(part3[:, j], rest[:, j], part2[:, j], ALU.subtract).then_inc(part3_ok, 1)

                over_blocks(pool, BLOCKS, body)

            @block.scalar
            def _(act):
                norm_root(act, norm, 0, 0)

                def body(i, j, n):
                    act.wait_ge(t_ok, i + 1)
                    for c in range(DC):
                        act.activation(xnT_hi[:, j, c], ps_t[:, c], ACT.Copy).then_inc(t_hi_ok, 1)
                    if not (isinstance(i, int) and i == BLOCKS - 1):
                        norm_root(act, norm, i + 1, 1 - j)
                    wait_past(act, parts_out[j], 192 * n)
                    wait_past(act, n_ok, i - 1 if not isinstance(i, int) or i else 0)
                    for c in range(4):
                        act.wait_ge(qk_ok, 4 * i + c + 1)
                        scale = DH ** -0.5 if c < DC else 1.0
                        act.activation(part1[:, j, c], ps_qk[:, c], ACT.Copy, scale=scale)
                        act.activation(square[:, j, c], ps_qk[:, c], ACT.Square, scale=scale).then_inc(part1_ok, 1)
                        if c % 2:
                            g = c // 2
                            act.wait_ge(v_ok, 2 * i + g + 1)
                            for t in range(2):
                                last = act.activation(
                                    k["V"][:, :, bass.ds(TB * i + 2 * g + t, 1), :, 0:DH],
                                    ps_v[:, t].rearrange("p (g h d) -> p g h d", h=HG, d=DH), ACT.Copy)
                            last.then_inc(v_used, 1)

                over_blocks(act, BLOCKS, body)

            @block.vector
            def _(dve):
                dve.memset(ps_n[:, :], 0.0).then_inc(n_used, 1)
                dve.wait_ge(x_in[0], 16)
                norm_measure(dve, norm, 0, 0)
                dve.wait_ge(w_in, 48)
                dve.tensor_copy(w_hi[:, :], w_raw[:, :]).then_inc(w_split, 1)
                dve.wait_ge(w_split, 1)
                dve.tensor_tensor(w_lo[:, :], w_raw[:, :], w_hi[:, :].bitcast(F32), ALU.subtract).then_inc(w_split, 1)
                norm_apply(dve, norm, 0, 0, lambda t: xn[:, 0, t:t + 1, :])

                def rests(i, j, c):
                    dve.wait_ge(part1_ok, 4 * i + c + 1)
                    if c < DC:
                        op = dve.scalar_tensor_tensor(out=rest[:, j, c], in0=ps_qk[:, c], scalar=DH ** -0.5,
                                                      in1=part1[:, j, c], op0=ALU.mult, op1=ALU.subtract)
                    else:
                        op = dve.tensor_tensor(rest[:, j, c], ps_qk[:, c], part1[:, j, c], ALU.subtract)
                    op.then_inc(rest_ok, 1)

                def body(i, j, n):
                    for c in range(DC):
                        dve.wait_ge(t_hi_ok, DC * i + c + 1)
                        dve.tensor_tensor(xnT_lo[:, j, c], ps_t[:, c], xnT_hi[:, j, c].bitcast(F32),
                                          ALU.subtract).then_inc(t_lo_ok, 1)
                    last = isinstance(i, int) and i == BLOCKS - 1
                    if not last:
                        hold(dve, k, x_in[1 - j], 16 * (n + j) + 16)
                        norm_measure(dve, norm, i + 1, 1 - j)
                    wait_past(dve, part3_ok, i - 1 if not isinstance(i, int) or i else 0)
                    rests(i, j, 0)
                    rests(i, j, 1)
                    if not last:
                        norm_apply(dve, norm, i + 1, 1 - j, lambda t: xn[:, 1 - j, t:t + 1, :])
                    rests(i, j, 2)
                    rests(i, j, 3)
                    dve.wait_ge(rest_ok, 4 * i + 4)
                    wait_past(dve, parts_out[j], 192 * n)
                    dve.tensor_copy(part2[:, j], rest[:, j]).then_inc(part2_ok, 1)
                    dve.wait_ge(n_ok, i + 1)
                    dve.tensor_reduce(norm_max[:, bass.ds(i, 1)], ps_n[:, :], AX.X, ALU.max).then_inc(n_used, 1)

                over_blocks(dve, BLOCKS, body)
                dve.wait_ge(n_used, BLOCKS + 1)
                dve.tensor_reduce(norm_top[:, :], norm_max[:, :], AX.X, ALU.max).then_inc(top_ok, 1)
                dve.wait_ge(topT_ok, 1)
                dve.tensor_copy(norm_row[:, :], ps_n[0:1, 0:P]).then_inc(row_ok, 1)
                dve.wait_ge(row_ok, 1)
                row = norm_row[:, :].rearrange("p (m c r) -> p m c r", m=2, c=2)
                dve.tensor_tensor(over[:, :, :], row[:, 0, :, 0:8], row[:, 1, :, 0:8], ALU.mult).then_inc(row_ok, 1)
                dve.wait_ge(row_ok, 2)
                dve.tensor_scalar(over[:, :, :], over[:, :, :], SAFE_SQUARE, None, ALU.is_gt).then_inc(row_ok, 1)
                dve.wait_ge(row_ok, 3)
                dve.tensor_reduce(k["unsafe"][:, :], over[:, :, :], AX.XY, ALU.max).then_inc(row_ok, 1)

            @block.tensor
            def _(pe):
                def turn(i, j):
                    pe.wait_ge(norm["xn_ok"], i + 1)
                    wait_past(pe, t_lo_ok, DC * i)
                    for t in range(TB):
                        for c in range(DC):
                            last = pe.transpose(ps_t[:, c, t * P:(t + 1) * P],
                                                xn[:, j, t, c * P:(c + 1) * P], k["ident"][:, :])
                    last.then_inc(t_ok, 1)

                def body(i, j, n):
                    pe.wait_ge(t_lo_ok, DC * i + DC)
                    for c in range(4):
                        wait_past(pe, rest_ok, 4 * i + c - 3)
                        w, o = c // DC, (c % DC) * P
                        for d in range(DC):
                            last = mm3(pe, ps_qk[:, c], (w_hi[:, w, d, o:o + P], w_lo[:, w, d, o:o + P]),
                                       (xnT_hi[:, j, d], xnT_lo[:, j, d]), d == 0, d == DC - 1)
                        last.then_inc(qk_ok, 1)
                        if c % 2:
                            g = c // 2
                            wait_past(pe, v_used, 2 * i + g)
                            for t in range(2):
                                o = (2 * g + t) * P
                                for d in range(DC):
                                    last = mm3(pe, ps_v[:, t], (xnT_hi[:, j, d, o:o + P], xnT_lo[:, j, d, o:o + P]),
                                               (w_hi[:, 2, d], w_lo[:, 2, d]), d == 0, d == DC - 1)
                            last.then_inc(v_ok, 1)
                    if not (isinstance(i, int) and i == BLOCKS - 1):
                        turn(i + 1, 1 - j)
                    pe.wait_ge(part1_ok, 4 * i + 4)
                    pe.wait_ge(n_used, i + 1)
                    for c in range(4):
                        last = pe.matmul(ps_n[32 * c:32 * c + 8, :], k["head_sel"][:, :], square[:, j, c],
                                         start=True, stop=True)
                    last.then_inc(n_ok, 1)

                pe.wait_ge(w_split, 2)
                turn(0, 0)
                over_blocks(pe, BLOCKS, body)
                pe.wait_ge(top_ok, 1)
                pe.transpose(ps_n[0:1, 0:P], norm_top[:, :], k["ident"][:, :]).then_inc(topT_ok, 1)


def load_stacks(eng, io, u, Q, K, sem):
    for slots, dst, m in ((Q_SLOTS, Q, 0), (K_SLOTS, K, 1)):
        for n, part in enumerate(slots):
            src = io["qk"].rearrange("m n g b r t -> m n (g b) r t")[m, part, bass.ds(u, 1)]
            eng.dma_start(dst[DH * n:DH * n + DH], src.rearrange("o (h d) t -> d (o h) t", d=DH)).then_inc(sem, 16)


def phase_shift(k):
    nc, io = k["nc"], k["io"]
    QT = SEQ // P
    with ExitStack() as mem:
        def sb(name, shape, dt):
            return mem.enter_context(nc.sbuf_tensor(name, shape, dt))

        Q, K = sb("Q_max", [P, HG, SEQ], BF16), sb("K_max", [P, HG, SEQ], BF16)
        mask = sb("wide_mask", [P, 2 * SEQ - P], BF16)
        masked = sb("masked_scores", [P, SEQ], F32)
        top = sb("top", [P, HG * QT], F32)
        neg = sb("neg_top", [HG * QT, P], F32)
        left = sb("left", [HG * QT, 2, P], F32)
        parts = sb("shift_part", [HG * QT, 3, P], BF16)
        ps_s = mem.enter_context(nc.psum_tensor("ps_max", [P, SEQ], F32))
        ps_t = mem.enter_context(nc.psum_tensor("ps_top", [HG * QT, P], F32))
        loaded, scores_ok, mask_ok, masked_ok, top_ok, turned_ok, neg_ok, split_ok, stored, parts_free = sems(k, 
            "shift", "loaded scores_ok mask_ok masked_ok top_ok turned_ok neg_ok split_ok stored parts_free")
        EACH = HG * QT

        with nc.Block() as block:

            def where_unsafe(eng):
                return eng.If(eng.value_load(k["unsafe"][0:1, 0:1], min_val=0, max_val=1) > 0)

            @block.sync
            def _(sp):
                with where_unsafe(sp):
                    load_stacks(sp, io, 0, Q[:, :, :], K[:, :, :], loaded)
                    with sp.Fori(1, UNITS) as u:
                        hold(sp, k, scores_ok, EACH * u)
                        load_stacks(sp, io, u, Q[:, :, :], K[:, :, :], loaded)
                    sp.wait_ge(loaded, 16 * 12 * UNITS)

            @block.gpsimd
            def _(pool):
                with where_unsafe(pool):
                    pool.memset(mask[:, :], 0.0).then_inc(mask_ok, 1)
                    pool.wait_ge(mask_ok, 1)
                    pool.affine_select(out=mask[:, :], in_=mask[:, :], compare_op=ALU.is_ge, fill=-3.0e38,
                                       base=SEQ - P, pattern=[[-1, 2 * SEQ - P]], channel_multiplier=1
                                       ).then_inc(mask_ok, 1)
                    with pool.Fori(0, UNITS) as u:
                        hold(pool, k, split_ok, 3 * u + 3)
                        for n in range(3):
                            pool.dma_start(
                                io["shift"].rearrange("m g b h (t p) -> m (g b) (h t) p", p=P)[n, bass.ds(u, 1)]
                                .rearrange("o r p -> (o r) p"), parts[:, n, :]).then_inc(stored, 16)
                        pool.wait_ge(stored, 48 * u + 48)
                        pool.sem_inc(parts_free, 1)

            @block.vector
            def _(dve):
                with where_unsafe(dve):
                    dve.sem_inc(masked_ok, 1)
                    dve.sem_inc(parts_free, 1)
                    dve.sem_inc(top_ok, 1)
                    dve.wait_ge(mask_ok, 2)
                    with dve.Fori(0, UNITS) as u:
                        for h in range(HG):
                            with dve.Fori(0, QT) as t:
                                at = EACH * u + QT * h + t
                                dve.wait_ge(scores_ok, at + 1)
                                dve.wait_ge(top_ok, at + 1)
                                dve.tensor_tensor(masked[:, :], ps_s[:, :], mask[:, bass.ds(SEQ - P - P * t, SEQ)],
                                                  ALU.add).then_inc(masked_ok, 1)
                                dve.wait_ge(masked_ok, at + 2)
                                dve.tensor_reduce(top[:, bass.ds(QT * h + t, 1)], masked[:, :], AX.X, ALU.max
                                                  ).then_inc(top_ok, 1)
                        dve.wait_ge(turned_ok, u + 1)
                        dve.tensor_scalar(neg[:, :], ps_t[:, :], -1.0, None, ALU.mult).then_inc(neg_ok, 1)
                        dve.wait_ge(neg_ok, 3 * u + 1)
                        dve.wait_ge(parts_free, u + 1)
                        rest = neg[:, :]
                        for n in range(3):
                            dve.tensor_copy(parts[:, n], rest).then_inc(split_ok, 1)
                            if n < 2:
                                dve.wait_ge(split_ok, 3 * u + n + 1)
                                dve.tensor_tensor(left[:, n], rest, parts[:, n], ALU.subtract).then_inc(neg_ok, 1)
                                dve.wait_ge(neg_ok, 3 * u + n + 2)
                                rest = left[:, n]

            @block.tensor
            def _(pe):
                with where_unsafe(pe):
                    with pe.Fori(0, UNITS) as u:
                        hold(pe, k, loaded, 192 * u + 192)
                        for h in range(HG):
                            with pe.Fori(0, QT) as t:
                                at = EACH * u + QT * h + t
                                pe.wait_ge(masked_ok, at + 1)
                                for c in range(0, SEQ, BT):
                                    last = pe.matmul(ps_s[:, c:c + BT], Q[0:SHIFT_ROWS, h, bass.ds(P * t, P)],
                                                     K[0:SHIFT_ROWS, h, c:c + BT], start=True, stop=True)
                                last.then_inc(scores_ok, 1)
                        hold(pe, k, top_ok, EACH * u + EACH + 1)
                        pe.transpose(ps_t[:, :], top[:, :], k["ident"][:, :]).then_inc(turned_ok, 1)


def phase_attention(k):
    nc, io = k["nc"], k["io"]
    SLICES = SEQ // BT
    TILE_LIST = [(q, t, max(0, (t - TB * q) * P)) for q in range(SLICES) for t in range(TB * (q + 1))]
    NT = len(TILE_LIST)
    LAST = [max(g for g, (q, _, _) in enumerate(TILE_LIST) if q == s) for s in range(SLICES)]
    DIAG = [g for g, (q, t, _) in enumerate(TILE_LIST) if t >= TB * q]
    SCORE_BUFS, PROB_BUFS = 3, 4
    LAG = 2
    LOADS = 13

    with ExitStack() as mem:
        def sb(name, shape, dt):
            return mem.enter_context(nc.sbuf_tensor(name, shape, dt))

        Q = sb("Q_stack", [P, 2, HG, SEQ], BF16)
        K = sb("K_stack", [P, 2, HG, SEQ], BF16)
        V = sb("V_unit", [P, 2, SEQ // P, HG, DH + 1], F32)
        probs = sb("probs", [P, PROB_BUFS, HG, BT], F32)
        sums = sb("weighted", [P, 2, BT], F32)
        inv = sb("inv_denominator", [P, 2, TB, HG], F32)
        result = sb("attention_rows", [P, 2, TB, HG, DH], F32)
        zero_rows = sb("zero_slots", [P, D], F32)
        ps_s = mem.enter_context(nc.psum_tensor("ps_s", [P, SCORE_BUFS, 2, BT], F32))
        ps_o = mem.enter_context(nc.psum_tensor("ps_o", [P, 2, BT], F32))

        loaded = sems(k, "unit_loaded", "even odd")
        stored = sems(k, "rows_stored", "even odd")
        cleared = sem(k, "slots_cleared")
        ones_ok, zero_ok, v_ok, scores_ok, exp_ok, mask_ok, pv_ok, sums_ok, turned_ok, inv_ok, result_ok = sems(k, 
            "attention", "ones_ok zero_ok v_ok scores_ok exp_ok mask_ok pv_ok sums_ok turned_ok inv_ok result_ok")

        with nc.Block() as block:

            def load(eng, u, j):
                load_stacks(eng, io, u, Q[:, j], K[:, j], loaded[j])
                src = io["shift"].rearrange("m g b h t -> m (g b) h t")[:, bass.ds(u, 1)]
                eng.dma_start(Q[SHIFT_ROWS:KROWS, j], src.rearrange("m o h t -> m (o h) t")).then_inc(loaded[j], 16)

            @block.sync
            def _(sp):
                load(sp, 0, 0)
                load(sp, 1, 1)
                sp.wait_ge(zero_ok, 2)
                for n in range(EXPERTS):
                    rows = io["slots_in"].rearrange("(n s p) d -> n p s d", n=EXPERTS, p=P)[n]
                    sp.dma_start(rows, zero_rows[:, :].unsqueeze(1).to_broadcast([P, SLOT_TILES // EXPERTS, D])
                                 ).then_inc(cleared, 16)

                def store(u, j, n):
                    for q in range(SLICES):
                        hold(sp, k, result_ok, SLICES * u + q + 1 + 2)
                        to = io["attended"].rearrange("g b (s t p) c -> (g b) s p t c", p=P, t=TB)
                        sp.dma_start(to[bass.ds(u, 1), q].rearrange("o p t c -> p (o t) c"),
                                     result[:, q % 2].rearrange("p t h d -> p t (h d)")).then_inc(stored[q % 2], 16)

                with sp.Fori(0, UNITS // 2 - 1) as n:
                    for j in range(2):
                        u = 2 * n + j
                        store(u, j, n)
                        hold(sp, k, scores_ok, 2 * NT * u + 2 * NT)
                        load(sp, u + 2, j)
                for j in range(2):
                    store(UNITS - 2 + j, j, UNITS // 2 - 1)
                for j in range(2):
                    sp.wait_ge(stored[j], 16 * (SLICES // 2 * UNITS + 1))
                sp.wait_ge(cleared, 16 * EXPERTS)

            @block.gpsimd
            def _(pool):
                pool.memset(K[SHIFT_ROWS:P, :, :, :], 1.0).then_inc(ones_ok, 1)
                with pool.Fori(0, UNITS // 2) as n:
                    for j in range(2):
                        u = 2 * n + j
                        for g in DIAG:
                            off = TILE_LIST[g][2]
                            block_of = probs[:, g % PROB_BUFS, :, off:off + P]
                            hold(pool, k, exp_ok, 2 * NT * u + 2 * g + 2 + 2)
                            pool.affine_select(out=block_of, in_=block_of, compare_op=ALU.is_ge, fill=0.0, base=0,
                                               pattern=[[0, HG], [1, P]], channel_multiplier=-1).then_inc(mask_ok, 1)

            @block.scalar
            def _(act):
                act.sem_inc(exp_ok, 2)
                with act.Fori(0, UNITS // 2) as n:
                    for j in range(2):
                        u = 2 * n + j
                        for g, (q, t, off) in enumerate(TILE_LIST):
                            for p in range(2):
                                s = 2 * g + p
                                if p == 0:
                                    act.wait_ge(pv_ok, NT * u + g + 1)
                                act.wait_ge(scores_ok, 2 * NT * u + s + 1)
                                act.activation(probs[:, g % PROB_BUFS, 2 * p:2 * p + 2, off:BT],
                                               ps_s[:, s % SCORE_BUFS, :, off:BT], ACT.Exp).then_inc(exp_ok, 1)

            @block.vector
            def _(dve):
                dve.memset(ps_o[:, :, :], 0.0).then_inc(zero_ok, 1)
                dve.memset(zero_rows[:, :], 0.0).then_inc(zero_ok, 1)
                dve.sem_inc(result_ok, 2)
                dve.sem_inc(stored[0], 16)
                dve.sem_inc(stored[1], 16)

                def take_v(u, j):
                    dve.tensor_copy(V[:, j], k["V"].rearrange("p g (b t) h d -> p (g b) t h d", b=BATCH)[:, bass.ds(u, 1)]
                                    ).then_inc(v_ok, 1)

                def unit(u, j, n):
                    for q in range(SLICES):
                        dve.wait_ge(pv_ok, NT * u + LAST[q] + 1 + PROB_BUFS)
                        dve.tensor_copy(sums[:, q % 2], ps_o[:, q % 2]).then_inc(sums_ok, 1)
                        dve.wait_ge(turned_ok, SLICES * u + q + 1)
                        turned = ps_o[:, q % 2].rearrange("p (t h c) -> p t h c", t=TB, h=HG)
                        dve.reciprocal(inv[:, q % 2], turned[:, :, :, DH]).then_inc(inv_ok, 1)
                        dve.wait_ge(inv_ok, SLICES * u + q + 1)
                        dve.wait_ge(stored[q % 2], 16 * (SLICES // 2 * u + q // 2 + 1))
                        dve.tensor_tensor(result[:, q % 2], turned[:, :, :, 0:DH],
                                          inv[:, q % 2].unsqueeze(3).to_broadcast([P, TB, HG, DH]),
                                          ALU.mult).then_inc(result_ok, 1)

                take_v(0, 0)
                take_v(1, 1)
                with dve.Fori(0, UNITS // 2 - 1) as n:
                    for j in range(2):
                        unit(2 * n + j, j, n)
                        take_v(2 * n + j + 2, j)
                for j in range(2):
                    unit(UNITS - 2 + j, j, UNITS // 2 - 1)

            @block.tensor
            def _(pe):
                pe.sem_inc(pv_ok, PROB_BUFS)
                pe.wait_ge(ones_ok, 1)
                pe.wait_ge(zero_ok, 1)

                def scores(u, j, g):
                    q, t, off = TILE_LIST[g]
                    for p in range(2):
                        s = 2 * g + p
                        before = s - SCORE_BUFS if s >= SCORE_BUFS else max(
                            x for x in range(2 * NT) if x % SCORE_BUFS == s % SCORE_BUFS) - 2 * NT
                        pe.wait_ge(exp_ok, 2 * NT * u + before + 1 + 2)
                        for h in range(2):
                            last = pe.matmul(ps_s[:, s % SCORE_BUFS, h, off:BT],
                                             K[0:KROWS, j, 2 * p + h, t * P:(t + 1) * P],
                                             Q[0:KROWS, j, 2 * p + h, q * BT + off:(q + 1) * BT],
                                             start=True, stop=True)
                        last.then_inc(scores_ok, 1)

                def weigh(u, j, g):
                    q, t, off = TILE_LIST[g]
                    if t == 0:
                        pe.wait_ge(result_ok, SLICES * u + q + 1)
                    pe.wait_ge(exp_ok, 2 * NT * u + 2 * g + 2 + 2)
                    if g in DIAG:
                        pe.wait_ge(mask_ok, len(DIAG) * u + DIAG.index(g) + 1)
                    for h in range(HG):
                        last = pe.matmul(ps_o[32 * h:32 * h + DH + 1, q % 2, off:BT], V[:, j, t, h, :],
                                         probs[:, g % PROB_BUFS, h, off:BT],
                                         start=(t == 0), stop=(g == LAST[q]))
                    last.then_inc(pv_ok, 1)

                def turn(u, q):
                    pe.wait_ge(sums_ok, SLICES * u + q + 1)
                    for t in range(TB):
                        last = pe.transpose(ps_o[:, q % 2, t * P:(t + 1) * P], sums[:, q % 2, t * P:(t + 1) * P],
                                            k["ident"][:, :])
                    last.then_inc(turned_ok, 1)

                with pe.Fori(0, UNITS // 2) as n:
                    steps = [(j, g) for j in range(2) for g in range(NT)]
                    for at in range(len(steps) + LAG + 2):
                        if at < len(steps):
                            j, g = steps[at]
                            if g == 0:
                                pe.wait_ge(loaded[j], 16 * LOADS * n + 16 * LOADS)
                                pe.wait_ge(v_ok, 2 * n + j + 1)
                            scores(2 * n + j, j, g)
                        if 0 <= at - LAG < len(steps):
                            j, g = steps[at - LAG]
                            weigh(2 * n + j, j, g)
                        if at - LAG - 2 >= 0:
                            j, g = steps[at - LAG - 2]
                            if g in LAST:
                                turn(2 * n + j, LAST.index(g))


def phase_out_projection(k):
    nc, io = k["nc"], k["io"]
    with ExitStack() as mem:
        def sb(name, shape, dt):
            return mem.enter_context(nc.sbuf_tensor(name, shape, dt))

        w_raw = sb("wo_raw", [P, DC, D], F32)
        w_hi, w_lo = sb("wo_hi", [P, DC, D], F32R), sb("wo_lo", [P, DC, D], F32R)
        r_raw = sb("router_raw", [P, DC, EXPERTS], F32)
        r_hi, r_lo = sb("router_hi", [P, DC, EXPERTS], F32R), sb("router_lo", [P, DC, EXPERTS], F32R)
        rows = sb("attended_rows", [P, 2, TB, GROUPS, HG * DH], F32)
        aT_hi, aT_lo = sb("aT_hi", [P, 2, DC, BT], F32R), sb("aT_lo", [P, 2, DC, BT], F32R)
        ps_a = mem.enter_context(nc.psum_tensor("ps_a", [P, DC, BT], F32))
        ps_t = mem.enter_context(nc.psum_tensor("ps_x", [P, DC, BT], F32))
        ps_y = mem.enter_context(nc.psum_tensor("ps_y", [P, TB, D], F32))
        ps_r = mem.enter_context(nc.psum_tensor("ps_r", [P, TB, EXPERTS], F32))
        norm = layer_norm(k, mem, "ln2")
        a_turn, x_turn = turner(k, "a_turn", ps_a), turner(k, "x2_turn", ps_t)
        w_in, w_split, y_ok, added_ok, r_ok, r_used = sems(k, "out_projection", "w_in w_split y_ok added_ok r_ok r_used")
        rows_in = sems(k, "rows_in", "even odd")

        with nc.Block() as block:

            @block.sync
            def _(sp):
                sp.dma_start(w_raw[:, :, :], io["wo"].rearrange("(c p) n -> p c n", p=P)).then_inc(w_in, 16)
                sp.dma_start(r_raw[:, :, :], io["router"].rearrange("(c p) n -> p c n", p=P)).then_inc(w_in, 16)
                for i in range(BLOCKS):
                    if i >= 2:
                        sp.wait_ge(a_turn["ps_ok"], i - 1)
                    b, t0 = i * BT // SEQ, i * BT % SEQ
                    for g in range(GROUPS):
                        sp.dma_start(rows[:, i % 2, :, g, :],
                                     io["attended"][g, b, t0:t0 + BT, :].rearrange("(t p) c -> p t c", p=P)
                                     ).then_inc(rows_in[i % 2], 16)

            @block.scalar
            def _(act):
                def a_high(i, j):
                    wait_past(act, y_ok, at_least(i - 1))
                    high_parts(act, a_turn, i, lambda c: aT_hi[:, j, c])

                def x_high(i):
                    high_parts(act, x_turn, i, lambda c: k["xT_hi"][:, c, bass.ds(i * BT, BT)])

                def body(i, j, n):
                    if not is_last(i, BLOCKS):
                        a_high(i + 1, 1 - j)
                    if not is_first(i):
                        x_high(i - 1)
                    norm_root(act, norm, i, j)

                a_high(0, 0)
                over_blocks(act, BLOCKS, body)
                x_high(BLOCKS - 1)

            @block.vector
            def _(dve):
                dve.wait_ge(w_in, 32)
                split_weights(dve, w_raw[:, :, :], w_hi[:, :, :], w_lo[:, :, :], w_split, 0)
                split_weights(dve, r_raw[:, :, :], r_hi[:, :, :], r_lo[:, :, :], w_split, 2)

                def a_low(i, j):
                    low_parts(dve, a_turn, i, lambda c: aT_lo[:, j, c], lambda c: aT_hi[:, j, c])

                def x_low(i):
                    low_parts(dve, x_turn, i, lambda c: k["xT_lo"][:, c, bass.ds(i * BT, BT)],
                              lambda c: k["xT_hi"][:, c, bass.ds(i * BT, BT)])

                def take_scores(i):
                    dve.wait_ge(r_ok, i + 1)
                    dve.tensor_copy(k["route"][:, bass.ds(TB * i, TB), :], ps_r[:, :, :]).then_inc(r_used, 1)

                def body(i, j, n):
                    if not is_last(i, BLOCKS):
                        a_low(i + 1, 1 - j)
                    dve.wait_ge(y_ok, i + 1)
                    for g in range(2):
                        x = k["X"][:, bass.ds(TB * i + 2 * g, 2), :]
                        last = dve.tensor_tensor(x, x, ps_y[:, 2 * g:2 * g + 2, :], ALU.add)
                    last.then_inc(added_ok, 1)
                    hold(dve, k, added_ok, i + 1)
                    norm_measure(dve, norm, i, j)
                    if not (is_first(i) or is_last(i, 2)):
                        take_scores(i - 2)
                    if not is_first(i):
                        x_low(i - 1)
                    norm_apply(dve, norm, i, j, lambda t: k["xn"][:, bass.ds(TB * i + t, 1), :])

                a_low(0, 0)
                over_blocks(dve, BLOCKS, body)
                take_scores(BLOCKS - 2)
                x_low(BLOCKS - 1)
                take_scores(BLOCKS - 1)

            @block.tensor
            def _(pe):
                pe.wait_ge(w_split, 4)

                def turn_a(i, j, n):
                    pe.wait_ge(rows_in[j], 16 * GROUPS * (n + 1))
                    turn_block(pe, a_turn, i, lambda t, c: rows[:, j, t, 2 * c:2 * c + 2, :].rearrange("p g c -> p (g c)"))

                def project(i, j):
                    pe.wait_ge(a_turn["lo_ok"], DC * i + DC)
                    wait_past(pe, added_ok, i)
                    for t in range(TB):
                        for d in range(DC):
                            o = t * P
                            last = mm3(pe, ps_y[:, t], (aT_hi[:, j, d, o:o + P], aT_lo[:, j, d, o:o + P]),
                                       (w_hi[:, d], w_lo[:, d]), d == 0, d == DC - 1)
                    last.then_inc(y_ok, 1)

                def turn_x(i):
                    pe.wait_ge(norm["xn_ok"], i + 1)
                    turn_block(pe, x_turn, i, lambda t, c: k["xn"][:, TB * i + t, c * P:(c + 1) * P])

                def scores(i):
                    pe.wait_ge(x_turn["lo_ok"], DC * i + DC)
                    wait_past(pe, r_used, i)
                    for t in range(TB):
                        for d in range(DC):
                            at = slice(i * BT + t * P, i * BT + (t + 1) * P)
                            last = mm3(pe, ps_r[:, t], (k["xT_hi"][:, d, at], k["xT_lo"][:, d, at]),
                                       (r_hi[:, d], r_lo[:, d]), d == 0, d == DC - 1)
                    last.then_inc(r_ok, 1)

                turn_a(0, 0, 0)
                for i in range(BLOCKS + 2):
                    if i + 1 < BLOCKS:
                        turn_a(i + 1, (i + 1) % 2, (i + 1) // 2)
                    if i < BLOCKS:
                        project(i, i % 2)
                    if i >= 2:
                        scores(i - 2)
                    if 1 <= i <= BLOCKS:
                        turn_x(i - 1)


def phase_route(k):
    nc, io = k["nc"], k["io"]
    with ExitStack() as mem:
        def sb(name, shape, dt):
            return mem.enter_context(nc.sbuf_tensor(name, shape, dt))

        def ps(name, shape, dt=F32):
            return mem.enter_context(nc.psum_tensor(name, shape, dt))

        lower = sb("lower_index", [P, EXPERTS, EXPERTS], BF16)
        higher = sb("higher_index", [P, EXPERTS, EXPERTS], BF16)
        rank = sb("rank", [P, TILES, EXPERTS], F32)
        is_rank = sb("is_rank", [P, TOP_K, TILES, EXPERTS], F32)
        chosen = sb("chosen", [P, TILES, EXPERTS], BF16)
        before = sb("before", [P, P], BF16)
        ones = sb("ones_square", [P, P], BF16)
        counts = sb("counts", [P, TILES, EXPERTS], F32)
        running = sb("running", [P, TILES, EXPERTS], F32)
        padded = sb("padded_int", [P, EXPERTS], I32)
        room = sb("room", [P, EXPERTS], F32)
        ends = sb("ends", [P, EXPERTS], F32)
        starts = sb("starts", [P, EXPERTS], F32)
        place = sb("place", [P, TILES, EXPERTS], F32)
        picked = sb("picked", [P, TOP_K, TILES, EXPERTS], F32)
        place_of = sb("place_of", [P, TOP_K, TILES], F32)
        score_of = sb("score_of", [P, TOP_K, TILES], F32)
        gate = sb("gate", [P, TOP_K, TILES], F32)
        tile_start = sb("tile_start", [1, SLOT_TILES, EXPERTS], F32)
        passed_end = sb("passed_end", [1, SLOT_TILES, EXPERTS], F32)
        expert = sb("tile_expert_f", [1, SLOT_TILES], F32)
        zeros = sb("zero_rows", [P, TILES, EXPERTS], F32)
        scaled = sb("scaled_rows", [P, 4, D], F32)
        w_raw = sb("shared_raw", [P, DC, FF], F32)
        wi_hi, wi_lo = sb("w_in_hi", [P, DC, FF], F32R), sb("w_in_lo", [P, DC, FF], F32R)
        wg_hi, wg_lo = sb("w_swiglu_hi", [P, DC, FF], F32R), sb("w_swiglu_lo", [P, DC, FF], F32R)
        wo_hi, wo_lo = sb("w_out_hi", [P, FC, D], F32R), sb("w_out_lo", [P, FC, D], F32R)
        silu = sb("silu", [P, 2, BT], F32)
        h = sb("h_shared", [P, 2, BT], F32)
        beats, ties = (a[:, :, :].rearrange("p n t -> p (n t)").bitcast(BF16).rearrange(
            "p (t e r) -> p t e r", e=EXPERTS, r=EXPERTS) for a in (silu, h))
        h_hi, h_lo = sb("h_hi", [P, FC, BT], F32R), sb("h_lo", [P, FC, BT], F32R)
        ps_m, ps_g, ps_y = ps("ps_mid", [P, 2, BT]), ps("ps_gated", [P, 2, BT]), ps("ps_shared", [P, TB, D])
        ps_c = ps("ps_count", [P, TILES * EXPERTS])
        ps_b = ps("ps_before", [P, TILES * EXPERTS])

        made, r_step, counted, gate_ok, scaled_ok = sems(k, "route", "made r_step counted gate_ok scaled_ok")
        scattered = sems(k, "scattered", "0 1 2 3")
        w_in, w_split = sems(k, "shared", "w_in w_split")
        mid_ok, gated_ok, silu_ok, h_ok, hi_ok, lo_ok, y_ok, y_used = sems(k, 
            "shared", "mid_ok gated_ok silu_ok h_ok hi_ok lo_ok y_ok y_used")

        with nc.Block() as block:

            @block.sync
            def _(sp):
                raws = ("w_in_shared", "w_swiglu", "w_out_shared")
                for n, name in enumerate(raws):
                    if n:
                        sp.wait_ge(w_split, 2 * n)
                    src = io[name].rearrange("(c p) n -> p c n", p=P)
                    dst = w_raw[:, :, :] if n < 2 else w_raw[:, :, :].rearrange("p c n -> p (c n)").rearrange(
                        "p (c n) -> p c n", c=FC)
                    sp.dma_start(dst, src).then_inc(w_in, 16)

            @block.gpsimd
            def _(pool):
                pool.memset(lower[:, :, :], 1.0).then_inc(made, 1)
                pool.memset(higher[:, :, :], 1.0).then_inc(made, 1)
                pool.memset(before[:, :], 1.0).then_inc(made, 1)
                pool.memset(ones[:, :], 1.0).then_inc(made, 1)
                pool.memset(zeros[:, :, :], 0.0).then_inc(made, 1)
                pool.iota(k["tile_expert"][:, :, :], pattern=[[P, SLOT_TILES], [0, EXPERTS]], base=0,
                          channel_multiplier=0).then_inc(made, 1)
                pool.wait_ge(made, 6)
                pool.affine_select(out=lower[:, :, :], in_=lower[:, :, :], compare_op=ALU.is_gt, fill=0.0, base=0,
                                   pattern=[[1, EXPERTS], [-1, EXPERTS]], channel_multiplier=0).then_inc(made, 1)
                pool.affine_select(out=higher[:, :, :], in_=higher[:, :, :], compare_op=ALU.is_ge, fill=0.0, base=0,
                                   pattern=[[-1, EXPERTS], [1, EXPERTS]], channel_multiplier=0).then_inc(made, 1)
                pool.affine_select(out=before[:, :], in_=before[:, :], compare_op=ALU.is_gt, fill=0.0, base=0,
                                   pattern=[[1, P]], channel_multiplier=-1).then_inc(made, 1)
                for t in range(TILES):
                    for r in range(TOP_K):
                        s = TOP_K * t + r
                        pool.wait_ge(scaled_ok, s + 1)
                        pool.indirect_dma_start(
                            out=io["slots_in"], out_offset=bass.IndirectOffsetOnAxis(ap=k["slot"][:, r, t:t + 1], axis=0),
                            in_=scaled[:, s % 4, :], in_offset=None).then_inc(scattered[s % 4], 16)
                for n in range(4):
                    pool.wait_ge(scattered[n], 16 * (TOP_K * TILES // 4))

            @block.vector
            def _(dve):
                step = 0

                def link(op):
                    nonlocal step
                    step += 1
                    op.then_inc(r_step, 1)
                    dve.wait_ge(r_step, step)

                for n, (hi, lo) in enumerate(((wi_hi, wi_lo), (wg_hi, wg_lo), (wo_hi, wo_lo))):
                    dve.wait_ge(w_in, 16 * (n + 1))
                    raw = w_raw[:, :, :] if n < 2 else w_raw[:, :, :].rearrange("p c n -> p (c n)").rearrange(
                        "p (c n) -> p c n", c=FC)
                    split_weights(dve, raw, hi[:, :, :], lo[:, :, :], w_split, 2 * n)
                dve.wait_ge(made, 9)
                full = [P, TILES, EXPERTS, EXPERTS]
                own = k["route"][:, :, :].unsqueeze(3).to_broadcast(full)
                rival = k["route"][:, :, :].unsqueeze(2).to_broadcast(full)
                dve.tensor_tensor(beats[:, :, :, :], rival, own, ALU.is_gt)
                link(dve.tensor_tensor(ties[:, :, :, :], rival, own, ALU.is_ge))
                dve.tensor_tensor(beats[:, :, :, :], beats[:, :, :, :],
                                  higher[:, :, :].unsqueeze(1).to_broadcast(full), ALU.mult)
                link(dve.tensor_tensor(ties[:, :, :, :], ties[:, :, :, :],
                                       lower[:, :, :].unsqueeze(1).to_broadcast(full), ALU.mult))
                link(dve.tensor_tensor(beats[:, :, :, :], beats[:, :, :, :], ties[:, :, :, :], ALU.add))
                link(dve.tensor_reduce(rank[:, :, :], beats[:, :, :, :], AX.X, ALU.add))
                link(dve.tensor_scalar(chosen[:, :, :], rank[:, :, :], float(TOP_K), None, ALU.is_lt))
                k["chosen_at"] = step
                for r in range(TOP_K):
                    link(dve.tensor_scalar(is_rank[:, r], rank[:, :, :], float(r), None, ALU.is_equal))
                    link(dve.tensor_tensor(picked[:, r], is_rank[:, r], k["route"][:, :, :], ALU.mult))
                link(dve.tensor_reduce(score_of[:, :, :], picked[:, :, :, :], AX.X, ALU.add))
                k["scores_at"] = step
                dve.wait_ge(counted, 1)
                link(dve.tensor_copy(counts[:, :, :], ps_c[:, :].rearrange("p (t e) -> p t e", e=EXPERTS)))
                for e in range(EXPERTS):
                    op = dve.tensor_tensor_scan(running[:, :, e], counts[:, :, e], zeros[:, :, e], 0.0, ALU.add, ALU.add)
                link(op)
                link(dve.tensor_scalar(padded[:, :], running[:, TILES - 1, :], float(P - 1), None, ALU.add))
                link(dve.tensor_scalar(padded[:, :], padded[:, :], -P, None, ALU.bitwise_and))
                link(dve.tensor_copy(room[:, :], padded[:, :]))
                link(dve.tensor_tensor_scan(ends[:, :], room[:, :], zeros[:, 0, :], 0.0, ALU.add, ALU.add))
                link(dve.tensor_tensor(starts[:, :], ends[:, :], room[:, :], ALU.subtract))
                link(dve.tensor_tensor(place[:, :, :], running[:, :, :], counts[:, :, :], ALU.subtract))
                link(dve.tensor_tensor(place[:, :, :], place[:, :, :],
                                       ps_b[:, :].rearrange("p (t e) -> p t e", e=EXPERTS), ALU.add))
                link(dve.tensor_tensor(place[:, :, :], place[:, :, :],
                                       starts[:, :].unsqueeze(1).to_broadcast([P, TILES, EXPERTS]), ALU.add))
                for r in range(TOP_K):
                    op = dve.tensor_tensor(picked[:, r], is_rank[:, r], place[:, :, :], ALU.mult)
                link(op)
                link(dve.tensor_reduce(place_of[:, :, :], picked[:, :, :, :], AX.X, ALU.add))
                link(dve.tensor_copy(k["slot"][:, :, :], place_of[:, :, :]))
                link(dve.tensor_copy(tile_start[:, :, :], k["tile_expert"][:, :, :]))
                link(dve.tensor_tensor(passed_end[:, :, :], tile_start[:, :, :],
                                       ends[0:1, :].unsqueeze(1).to_broadcast([1, SLOT_TILES, EXPERTS]), ALU.is_ge))
                link(dve.tensor_reduce(expert[:, :], passed_end[:, :, :], AX.X, ALU.add))
                link(dve.tensor_scalar(k["tile_expert"][:, :, 0], expert[:, :], float(EXPERTS - 1), None, ALU.min))
                dve.wait_ge(gate_ok, 1)

                def scale_rows(s):
                    t, r = s // TOP_K, s % TOP_K
                    if s >= 4:
                        dve.wait_ge(scattered[s % 4], 16 * (s // 4))
                    dve.tensor_scalar(scaled[:, s % 4, :], k["xn"][:, t, :], gate[:, r, t:t + 1], None,
                                      ALU.mult).then_inc(scaled_ok, 1)

                per_block = TOP_K * TILES // BLOCKS
                for i in range(BLOCKS):
                    for f in range(FC):
                        n = FC * i + f
                        dve.wait_ge(silu_ok, n + 1)
                        dve.wait_ge(gated_ok, n + 1)
                        if n >= 2:
                            dve.wait_ge(hi_ok, n - 1)
                        dve.tensor_tensor(h[:, f % 2], silu[:, f % 2], ps_g[:, f % 2], ALU.mult).then_inc(h_ok, 1)
                        for s in range(per_block // FC):
                            scale_rows(per_block * i + per_block // FC * f + s)
                        dve.wait_ge(hi_ok, n + 1)
                        dve.tensor_tensor(h_lo[:, f], h[:, f % 2], h_hi[:, f].bitcast(F32), ALU.subtract
                                          ).then_inc(lo_ok, 1)
                    dve.wait_ge(y_ok, i + 1)
                    for g in range(2):
                        x = k["X"][:, TB * i + 2 * g:TB * i + 2 * g + 2, :]
                        last = dve.tensor_tensor(x, x, ps_y[:, 2 * g:2 * g + 2, :], ALU.add)
                    last.then_inc(y_used, 1)

            @block.scalar
            def _(act):
                act.wait_ge(r_step, k["scores_at"])
                act.activation(gate[:, :, :], score_of[:, :, :], ACT.Sigmoid).then_inc(gate_ok, 1)
                for i in range(BLOCKS):
                    for f in range(FC):
                        n = FC * i + f
                        act.wait_ge(mid_ok, n + 1)
                        if n >= 2:
                            act.wait_ge(h_ok, n - 1)
                        act.activation(silu[:, f % 2], ps_m[:, f % 2], ACT.Silu).then_inc(silu_ok, 1)
                        act.wait_ge(h_ok, n + 1)
                        if i and f == 0:
                            act.wait_ge(y_ok, i)
                        act.activation(h_hi[:, f], h[:, f % 2], ACT.Copy).then_inc(hi_ok, 1)

            @block.tensor
            def _(pe):
                pe.wait_ge(r_step, k["chosen_at"])
                flat = chosen[:, :, :].rearrange("p t e -> p (t e)")
                pe.matmul(ps_b[:, :], before[:, :], flat, start=True, stop=True)
                pe.matmul(ps_c[:, :], ones[:, :], flat, start=True, stop=True).then_inc(counted, 1)
                pe.wait_ge(w_split, 6)

                def expand(i, f):
                    n = FC * i + f
                    x = [(k["xT_hi"][:, d, i * BT:(i + 1) * BT], k["xT_lo"][:, d, i * BT:(i + 1) * BT]) for d in range(DC)]
                    if n >= 2:
                        pe.wait_ge(silu_ok, n - 1)
                        pe.wait_ge(h_ok, n - 1)
                    for dst, hi, lo, sem in ((ps_m, wi_hi, wi_lo, mid_ok), (ps_g, wg_hi, wg_lo, gated_ok)):
                        for d in range(DC):
                            last = mm3(pe, dst[:, f % 2], (hi[:, d, f * P:(f + 1) * P], lo[:, d, f * P:(f + 1) * P]),
                                       x[d], d == 0, d == DC - 1)
                        last.then_inc(sem, 1)

                def contract(i):
                    pe.wait_ge(lo_ok, FC * i + FC)
                    if i:
                        pe.wait_ge(y_used, i)
                    for t in range(TB):
                        for f in range(FC):
                            last = mm3(pe, ps_y[:, t], (h_hi[:, f, t * P:(t + 1) * P], h_lo[:, f, t * P:(t + 1) * P]),
                                       (wo_hi[:, f], wo_lo[:, f]), f == 0, f == FC - 1)
                    last.then_inc(y_ok, 1)

                for i in range(BLOCKS):
                    for f in range(FC):
                        expand(i, f)
                    contract(i)


def phase_experts(k):
    nc, io = k["nc"], k["io"]
    with ExitStack() as mem:
        def sb(name, shape, dt):
            return mem.enter_context(nc.sbuf_tensor(name, shape, dt))

        def ps(name, shape, dt=F32):
            return mem.enter_context(nc.psum_tensor(name, shape, dt))

        wi = sb("we_in", [P, EXPERTS, DC, FF], F32)
        wg = sb("we_swiglu", [P, EXPERTS, DC, FF], F32)
        wo = sb("we_out", [P, EXPERTS, FC, D], F32)
        rows = sb("slot_rows", [P, 2, D], F32)
        xT = sb("slot_xT", [P, 2, DC, P], F32)
        silu = sb("slot_silu", [P, 2, FF], F32)
        h = sb("slot_h", [P, 2, FF], F32)
        hT = sb("slot_hT", [P, 2, FC, P], F32)
        y = sb("slot_y", [P, 2, D], F32)
        ps_x, ps_h, ps_y = ps("ps_xT", [P, DC, P]), ps("ps_hT", [P, FC, P]), ps("ps_slot_y", [P, D])
        ps_m, ps_g = ps("ps_slot_mid", [P, 2, FF]), ps("ps_slot_gated", [P, 2, FF])
        w_in = sem(k, "experts_w_in")
        rows_in, y_out = sems(k, "slot_rows_in", "even odd"), sems(k, "slot_y_out", "even odd")
        x_ok, xT_ok, mid_ok, gated_ok, silu_ok, h_ok, hps_ok, hT_ok, yps_ok, y_ok = sems(
            k, "slot", "x_ok xT_ok mid_ok gated_ok silu_ok h_ok hps_ok hT_ok yps_ok y_ok")

        with nc.Block() as block:

            @block.sync
            def _(sp):
                src = io["slots_in"].rearrange("(s p) d -> s p d", p=P)
                sp.dma_start(rows[:, 0, :], src[0]).then_inc(rows_in[0], 16)
                sp.dma_start(rows[:, 1, :], src[1]).then_inc(rows_in[1], 16)
                for name, w in (("w_in_e", wi), ("w_swiglu_e", wg), ("w_out_e", wo)):
                    for e in range(EXPERTS):
                        sp.dma_start(w[:, e], io[name][e].rearrange("(c p) f -> p c f", p=P)).then_inc(w_in, 16)
                with sp.Fori(0, SLOT_TILES // 2 - 1) as n:
                    for j in range(2):
                        hold(sp, k, x_ok, 2 * n + j + 1)
                        sp.dma_start(rows[:, j, :], src[bass.ds(2 * n + j + 2, 1)].rearrange("o p d -> p (o d)")
                                     ).then_inc(rows_in[j], 16)

            @block.gpsimd
            def _(pool):
                dst = io["slots_out"].rearrange("(s p) d -> s p d", p=P)

                def store(i, j, n):
                    hold(pool, k, y_ok, i + 1)
                    pool.dma_start(dst[bass.ds(i, 1)].rearrange("o p d -> p (o d)"), y[:, j, :]).then_inc(y_out[j], 16)

                with pool.Fori(0, SLOT_TILES // 2) as n:
                    for j in range(2):
                        store(2 * n + j, j, n)
                for j in range(2):
                    pool.wait_ge(y_out[j], 16 * (SLOT_TILES // 2))

            @block.scalar
            def _(act):
                def turned(i, j):
                    act.wait_ge(x_ok, i + 1)
                    act.activation(xT[:, j], ps_x[:, :, :], ACT.Copy).then_inc(xT_ok, 1)

                def result(i, j, n):
                    act.wait_ge(yps_ok, i + 1)
                    wait_past(act, y_out[j], 16 * n)
                    act.activation(y[:, j], ps_y[:, :], ACT.Copy).then_inc(y_ok, 1)

                def body(i, j, n):
                    act.wait_ge(mid_ok, i + 1)
                    wait_past(act, h_ok, at_least(i - 1))
                    act.activation(silu[:, j], ps_m[:, j], ACT.Silu).then_inc(silu_ok, 1)
                    if not is_last(i, SLOT_TILES):
                        turned(i + 1, 1 - j)
                    if not is_first(i):
                        result(i - 1, 1 - j, n - (1 - j))

                turned(0, 0)
                over_blocks(act, SLOT_TILES, body)
                result(SLOT_TILES - 1, 1, SLOT_TILES // 2 - 1)

            @block.vector
            def _(dve):
                def turned(i, j):
                    dve.wait_ge(hps_ok, i + 1)
                    wait_past(dve, yps_ok, at_least(i - 1))
                    dve.tensor_copy(hT[:, j], ps_h[:, :, :]).then_inc(hT_ok, 1)

                def body(i, j, n):
                    if not is_first(i):
                        turned(i - 1, 1 - j)
                    dve.wait_ge(silu_ok, i + 1)
                    dve.wait_ge(gated_ok, i + 1)
                    dve.tensor_tensor(h[:, j], silu[:, j], ps_g[:, j], ALU.mult).then_inc(h_ok, 1)

                over_blocks(dve, SLOT_TILES, body)
                turned(SLOT_TILES - 1, 1)

            @block.tensor
            def _(pe):
                def expert_of(i):
                    return pe.value_load(k["tile_expert"][0:1, bass.ds(i, 1), 0:1].rearrange("p s o -> p (s o)"),
                                         min_val=0, max_val=EXPERTS - 1)

                def turn_x(i, j, n):
                    pe.wait_ge(rows_in[j], 16 * n + 16)
                    wait_past(pe, xT_ok, i)
                    for c in range(DC):
                        last = pe.transpose(ps_x[:, c], rows[:, j, c * P:(c + 1) * P], k["ident"][:, :])
                    last.then_inc(x_ok, 1)

                def expand(i, j, e, dst, w, sem):
                    for d in range(DC):
                        last = pe.matmul(dst[:, j], xT[:, j, d], w[:, bass.ds(e, 1), d, :],
                                         start=(d == 0), stop=(d == DC - 1))
                    last.then_inc(sem, 1)

                def turn_h(i, j):
                    pe.wait_ge(h_ok, i + 1)
                    wait_past(pe, hT_ok, i)
                    for f in range(FC):
                        last = pe.transpose(ps_h[:, f], h[:, j, f * P:(f + 1) * P], k["ident"][:, :])
                    last.then_inc(hps_ok, 1)

                def contract(i, j):
                    e = expert_of(i)
                    pe.wait_ge(hT_ok, i + 1)
                    wait_past(pe, y_ok, i)
                    for f in range(FC):
                        last = pe.matmul(ps_y[:, :], hT[:, j, f], wo[:, bass.ds(e, 1), f, :],
                                         start=(f == 0), stop=(f == FC - 1))
                    last.then_inc(yps_ok, 1)

                def body(i, j, n):
                    e = expert_of(i)
                    pe.wait_ge(xT_ok, i + 1)
                    wait_past(pe, h_ok, at_least(i - 1))
                    expand(i, j, e, ps_m, wi, mid_ok)
                    if not is_first(i):
                        turn_h(i - 1, 1 - j)
                    expand(i, j, e, ps_g, wg, gated_ok)
                    if not is_last(i, SLOT_TILES):
                        turn_x(i + 1, 1 - j, n + j)
                    if not is_first(i):
                        contract(i - 1, 1 - j)

                pe.wait_ge(w_in, 16 * 3 * EXPERTS)
                turn_x(0, 0, 0)
                over_blocks(pe, SLOT_TILES, body)
                turn_h(SLOT_TILES - 1, 1)
                contract(SLOT_TILES - 1, 1)


SEQ_TILES = SEQ // P
SEQ_BLOCKS = SEQ // BT


def phase_keys(k, b):
    nc, io = k["nc"], k["io"]
    with ExitStack() as mem:
        def sb(name, shape, dt):
            return mem.enter_context(nc.sbuf_tensor(name + str(b), shape, dt))

        def ps(name, shape, dt=F32):
            return mem.enter_context(nc.psum_tensor(name + str(b), shape, dt))

        w_raw = sb("kv_raw", [P, DC, 2 * D], F32)
        w_hi, w_lo = sb("kv_hi", [P, DC, 2 * D], F32R), sb("kv_lo", [P, DC, 2 * D], F32R)
        back = sb("back", [P, 2, TOP_K, TB, D], F32)
        xn = sb("xn3", [P, 2, TB, D], F32)
        ps_t, ps_k, ps_v = ps("ps_x3", [P, DC, BT]), ps("ps_k3", [P, DC, BT]), ps("ps_v3", [P, TB, D])
        norm = layer_norm(k, mem, f"ln3_{b}")
        x_turn = turner(k, f"x3_turn{b}", ps_t)
        w_in, w_split, sum_ok, k_ok, k_hi, k_lo, v_ok, v_hi, v_lo = sems(k, 
            f"keys{b}", "w_in w_split sum_ok k_ok k_hi k_lo v_ok v_hi v_lo")
        back_in = sems(k, f"back_in{b}", "even odd")
        T0 = b * SEQ_TILES

        with nc.Block() as block:

            @block.sync
            def _(sp):
                sp.dma_start(w_raw[:, :, :], io["w_kv"].rearrange("(c p) n -> p c n", p=P)).then_inc(w_in, 16)

            @block.gpsimd
            def _(pool):
                for i in range(SEQ_BLOCKS):
                    if i >= 2:
                        pool.wait_ge(sum_ok, 2 * i - 2)
                    for r in range(TOP_K):
                        for t in range(TB):
                            T = T0 + TB * i + t
                            pool.indirect_dma_start(
                                out=back[:, i % 2, r, t, :], out_offset=None, in_=io["slots_out"],
                                in_offset=bass.IndirectOffsetOnAxis(ap=k["slot"][:, r, T:T + 1], axis=0)
                            ).then_inc(back_in[i % 2], 16)

            @block.scalar
            def _(act):
                for i in range(SEQ_BLOCKS):
                    norm_root(act, norm, i, i % 2)
                    high_parts(act, x_turn, i, lambda c: k["qT_hi"][:, c, i * BT:(i + 1) * BT])
                    for c in range(DC):
                        act.wait_ge(k_ok, DC * i + c + 1)
                        act.activation(k["kT_hi"][:, c, i * BT:(i + 1) * BT], ps_k[:, c], ACT.Copy).then_inc(k_hi, 1)
                    for g in range(2):
                        act.wait_ge(v_ok, 2 * i + g + 1)
                        t = TB * i + 2 * g
                        act.activation(k["v_hi"][:, t:t + 2, :], ps_v[:, 2 * g:2 * g + 2, :], ACT.Copy).then_inc(v_hi, 1)

            @block.vector
            def _(dve):
                dve.wait_ge(w_in, 16)
                split_weights(dve, w_raw[:, :, :], w_hi[:, :, :], w_lo[:, :, :], w_split, 0)

                for i in range(SEQ_BLOCKS):
                    j = i % 2
                    x = k["X"][:, T0 + TB * i:T0 + TB * i + TB, :]
                    dve.wait_ge(back_in[j], 16 * TOP_K * TB * (i // 2 + 1))
                    for r in range(TOP_K):
                        dve.tensor_tensor(x, x, back[:, j, r], ALU.add).then_inc(sum_ok, 1)
                        dve.wait_ge(sum_ok, 2 * i + r + 1)
                    norm_measure(dve, norm, i, j, T0)
                    norm_apply(dve, norm, i, j, lambda t: xn[:, j, t:t + 1, :], T0)
                    dve.wait_ge(norm["xn_ok"], i + 1)
                    dve.tensor_tensor(x, x, xn[:, j], ALU.add).then_inc(k["residual_ok"], 1)
                    low_parts(dve, x_turn, i, lambda c: k["qT_lo"][:, c, i * BT:(i + 1) * BT],
                               lambda c: k["qT_hi"][:, c, i * BT:(i + 1) * BT])
                    for c in range(DC):
                        dve.wait_ge(k_hi, DC * i + c + 1)
                        at = slice(i * BT, (i + 1) * BT)
                        dve.tensor_tensor(k["kT_lo"][:, c, at], ps_k[:, c], k["kT_hi"][:, c, at].bitcast(F32),
                                          ALU.subtract).then_inc(k_lo, 1)
                    for g in range(2):
                        dve.wait_ge(v_hi, 2 * i + g + 1)
                        t = TB * i + 2 * g
                        dve.tensor_tensor(k["v_lo"][:, t:t + 2, :], ps_v[:, 2 * g:2 * g + 2, :],
                                          k["v_hi"][:, t:t + 2, :].bitcast(F32), ALU.subtract).then_inc(v_lo, 1)

            @block.tensor
            def _(pe):
                pe.wait_ge(w_split, 2)
                for i in range(SEQ_BLOCKS):
                    j = i % 2
                    pe.wait_ge(norm["xn_ok"], i + 1)
                    turn_block(pe, x_turn, i, lambda t, c: xn[:, j, t, c * P:(c + 1) * P])
                    pe.wait_ge(x_turn["lo_ok"], DC * i + DC)
                    for c in range(DC):
                        wait_past(pe, k_lo, DC * (i - 1) + c + 1)
                        for d in range(DC):
                            at = slice(i * BT, (i + 1) * BT)
                            last = mm3(pe, ps_k[:, c], (w_hi[:, d, c * P:(c + 1) * P], w_lo[:, d, c * P:(c + 1) * P]),
                                       (k["qT_hi"][:, d, at], k["qT_lo"][:, d, at]), d == 0, d == DC - 1)
                        last.then_inc(k_ok, 1)
                    for g in range(2):
                        wait_past(pe, v_lo, 2 * (i - 1) + g + 1)
                        for t in (2 * g, 2 * g + 1):
                            for d in range(DC):
                                at = slice(i * BT + t * P, i * BT + (t + 1) * P)
                                last = mm3(pe, ps_v[:, t], (k["qT_hi"][:, d, at], k["qT_lo"][:, d, at]),
                                           (w_hi[:, d, D:2 * D], w_lo[:, d, D:2 * D]), d == 0, d == DC - 1)
                        last.then_inc(v_ok, 1)


def phase_attend(k, b):
    nc, io = k["nc"], k["io"]
    with ExitStack() as mem:
        def sb(name, shape, dt):
            return mem.enter_context(nc.sbuf_tensor(name + str(b), shape, dt))

        def ps(name, shape, dt=F32):
            return mem.enter_context(nc.psum_tensor(name + str(b), shape, dt))

        chunk_top = sb("chunk_max", [P, SEQ_TILES, SEQ_BLOCKS], F32)
        chunk_total = sb("chunk_sum", [P, SEQ_TILES, SEQ_BLOCKS], F32)
        top = sb("row_max", [P, SEQ_TILES], F32)
        neg_top = sb("neg_row_max", [P, SEQ_TILES], F32)
        total = sb("row_sum", [P, SEQ_TILES], F32)
        inv = sb("inv_row_sum", [P, SEQ_TILES], F32)
        probs = sb("probs3", [P, 2, SEQ], F32)
        pT_hi, pT_lo = sb("pT_hi", [P, 2, TB, P], F32R), sb("pT_lo", [P, 2, TB, P], F32R)
        ps_s, ps_t, ps_o = ps("ps_s3", [P, SEQ]), ps("ps_p3", [P, 2, TB, P]), ps("ps_o3", [P, 2, BT])
        s_ok, masked_ok, chunk_ok, top_ok, neg_ok, exp_ok = sems(
            k, f"attend{b}", "s_ok masked_ok chunk_ok top_ok neg_ok exp_ok")
        t_ok, hi_ok, lo_ok, pv_ok, total_ok, inv_ok, used_ok = sems(
            k, f"attend{b}", "t_ok hi_ok lo_ok pv_ok total_ok inv_ok used_ok")
        T0 = b * SEQ_TILES
        PARTS = [(q, g, min(TB, q + 1 - g)) for q in range(SEQ_TILES) for g in range(0, q + 1, TB)]
        OF = [[n for n, part in enumerate(PARTS) if part[0] == q] for q in range(SEQ_TILES)]

        with nc.Block() as block:

            @block.vector
            def _(dve):
                def soften(q):
                    for n in OF[q]:
                        _, g, m = PARTS[n]
                        dve.wait_ge(s_ok, n + 1)
                        if n == OF[q][-1]:
                            diag = ps_s[:, q * P:(q + 1) * P]
                            dve.tensor_tensor(diag, diag, k["causal"][:, :], ALU.add).then_inc(masked_ok, 1)
                            dve.wait_ge(masked_ok, q + 1)
                        dve.tensor_reduce(chunk_top[:, q, g // TB:g // TB + 1], ps_s[:, g * P:(g + m) * P], AX.X,
                                          ALU.max).then_inc(chunk_ok, 1)
                    dve.wait_ge(chunk_ok, OF[q][-1] + 1)
                    dve.tensor_reduce(top[:, q:q + 1], chunk_top[:, q, 0:len(OF[q])], AX.X, ALU.max).then_inc(top_ok, 1)
                    dve.wait_ge(top_ok, q + 1)
                    dve.tensor_scalar(neg_top[:, q:q + 1], top[:, q:q + 1], -1.0, None, ALU.mult).then_inc(neg_ok, 1)

                def lows(n):
                    dve.wait_ge(hi_ok, n + 1)
                    m = PARTS[n][2]
                    dve.tensor_tensor(pT_lo[:, n % 2, 0:m], ps_t[:, n % 2, 0:m], pT_hi[:, n % 2, 0:m].bitcast(F32),
                                      ALU.subtract).then_inc(lo_ok, 1)

                soften(0)
                for q in range(SEQ_TILES):
                    for n in OF[q][:2]:
                        lows(n)
                    if q + 1 < SEQ_TILES:
                        soften(q + 1)
                    for n in OF[q][2:]:
                        lows(n)
                    dve.wait_ge(exp_ok, OF[q][-1] + 1)
                    dve.tensor_reduce(total[:, q:q + 1], chunk_total[:, q, 0:len(OF[q])], AX.X, ALU.add
                                      ).then_inc(total_ok, 1)
                    dve.wait_ge(total_ok, q + 1)
                    dve.reciprocal(inv[:, q:q + 1], total[:, q:q + 1]).then_inc(inv_ok, 1)
                    dve.wait_ge(pv_ok, OF[q][-1] + 1)
                    dve.wait_ge(inv_ok, q + 1)
                    x = k["X"][:, T0 + q, :]
                    dve.scalar_tensor_tensor(out=x, in0=ps_o[:, q % 2, 0:D], scalar=inv[:, q:q + 1], in1=x,
                                             op0=ALU.mult, op1=ALU.add).then_inc(used_ok, 1)

            @block.scalar
            def _(act):
                def weigh(n):
                    q, g, m = PARTS[n]
                    if n == OF[q][0]:
                        act.wait_ge(neg_ok, q + 1)
                        if q >= 2:
                            act.wait_ge(t_ok, OF[q - 2][-1] + 1)
                    act.activation(probs[:, q % 2, g * P:(g + m) * P], ps_s[:, g * P:(g + m) * P], ACT.Exp,
                                   bias=neg_top[:, q:q + 1], accum_out=chunk_total[:, q, g // TB:g // TB + 1]
                                   ).then_inc(exp_ok, 1)

                def high(n):
                    m = PARTS[n][2]
                    act.wait_ge(t_ok, n + 1)
                    if n >= 2:
                        act.wait_ge(pv_ok, n - 1)
                    act.activation(pT_hi[:, n % 2, 0:m], ps_t[:, n % 2, 0:m], ACT.Copy).then_inc(hi_ok, 1)

                weigh(0)
                for q in range(SEQ_TILES):
                    following = list(OF[q + 1]) if q + 1 < SEQ_TILES else []
                    for n in OF[q][:2]:
                        high(n)
                    for at in range(max(len(following), len(OF[q]) - 2)):
                        if at < len(following):
                            weigh(following[at])
                        if at + 2 < len(OF[q]):
                            high(OF[q][at + 2])

            @block.tensor
            def _(pe):
                def score(q):
                    for n in OF[q]:
                        _, g, m = PARTS[n]
                        if q and n - OF[q][0] < len(OF[q - 1]):
                            pe.wait_ge(exp_ok, OF[q - 1][n - OF[q][0]] + 1)
                        for d in range(DC):
                            at = slice(q * P, (q + 1) * P)
                            to = slice(g * P, (g + m) * P)
                            last = mm3(pe, ps_s[:, to], (k["qT_hi"][:, d, at], k["qT_lo"][:, d, at]),
                                       (k["kT_hi"][:, d, to], k["kT_lo"][:, d, to]), d == 0, d == DC - 1)
                        last.then_inc(s_ok, 1)

                def turn(n):
                    q, g, m = PARTS[n]
                    pe.wait_ge(exp_ok, n + 1)
                    if n >= 2:
                        pe.wait_ge(lo_ok, n - 1)
                    for t in range(m):
                        last = pe.transpose(ps_t[:, n % 2, t], probs[:, q % 2, (g + t) * P:(g + t + 1) * P],
                                            k["ident"][:, :])
                    last.then_inc(t_ok, 1)

                def weigh(n):
                    q, g, m = PARTS[n]
                    pe.wait_ge(lo_ok, n + 1)
                    if g == 0 and q >= 2:
                        pe.wait_ge(used_ok, q - 1)
                    for t in range(m):
                        last = mm3(pe, ps_o[:, q % 2, 0:D], (pT_hi[:, n % 2, t], pT_lo[:, n % 2, t]),
                                   (k["v_hi"][:, g + t], k["v_lo"][:, g + t]), g + t == 0, g + t == q)
                    last.then_inc(pv_ok, 1)

                score(0)
                for q in range(SEQ_TILES):
                    for n in OF[q][:2]:
                        turn(n)
                    if q + 1 < SEQ_TILES:
                        score(q + 1)
                    for n in OF[q]:
                        weigh(n)
                        if n + 2 in OF[q]:
                            turn(n + 2)


def phase_mlp(k):
    nc, io = k["nc"], k["io"]
    F4 = 4 * D
    FC4 = F4 // P
    with ExitStack() as mem:
        def sb(name, shape, dt):
            return mem.enter_context(nc.sbuf_tensor(name, shape, dt))

        def ps(name, shape, dt=F32):
            return mem.enter_context(nc.psum_tensor(name, shape, dt))

        raw = [sb("w1_raw", [P, DC, F4], F32), sb("w2_raw", [P, FC4, D], F32)]
        w1, w2 = sb("w1_ternary", [P, DC, F4], F32R), sb("w2_ternary", [P, FC4, D], F32R)
        below = sb("below", [P, 2 * F4], F32)
        size = sb("abs_sum", [P, 2], F32)
        gamma, half = sb("gamma", [P, 2], F32), sb("half_gamma", [P, 2, 2], F32)
        ones = sb("ones_f32", [P, P], F32)
        b1 = sb("b1_columns", [P, FC4], F32)
        b2 = sb("b2_rows", [P, D], F32)
        xn = sb("xn4", [P, 2, TB, D], F32)
        xT_hi, xT_lo = sb("x4T_hi", [P, 2, DC, BT], F32R), sb("x4T_lo", [P, 2, DC, BT], F32R)
        h = sb("h4", [P, 2, BT], F32)
        h_hi, h_lo = sb("h4_hi", [P, 2, FC4, BT], F32R), sb("h4_lo", [P, 2, FC4, BT], F32R)
        y = sb("y4", [P, 2, TB, D], F32)
        ps_t, ps_h, ps_y = ps("ps_x4", [P, DC, BT]), ps("ps_h4", [P, 3, BT]), ps("ps_y4", [P, TB, D])
        ps_g = ps("ps_gamma", [P, 2])
        norm = layer_norm(k, mem, "ln4")
        x_turn = turner(k, "x4_turn", ps_t)
        w_in, b_in, made, q_step, summed, res_ok = sems(k, "mlp", "w_in b_in made q_step summed res_ok")
        hps_ok, hi_ok, h_ok, lo_ok, yps_ok, y_ok = sems(k, "mlp", "hps_ok hi_ok h_ok lo_ok yps_ok y_ok")
        y_out = sems(k, "y_out", "even odd")

        with nc.Block() as block:

            @block.sync
            def _(sp):
                sp.dma_start(raw[0][:, :, :], io["w1"].rearrange("(c p) n -> p c n", p=P)).then_inc(w_in, 16)
                sp.dma_start(raw[1][:, :, :], io["w2"].rearrange("(c p) n -> p c n", p=P)).then_inc(w_in, 16)
                sp.dma_start(b1[:, :], io["b1"]).then_inc(b_in, 16)
                sp.dma_start(b2[:, :], io["b2"].to_broadcast([P, D])).then_inc(b_in, 16)
                out = io["out"].rearrange("(n p) d -> p n d", p=P)
                for i in range(BLOCKS):
                    sp.wait_ge(y_ok, 2 * i + 2)
                    sp.dma_start(out[:, TB * i:TB * i + TB, :], y[:, i % 2]).then_inc(y_out[i % 2], 16)
                for j in range(2):
                    sp.wait_ge(y_out[j], 16 * (BLOCKS // 2))

            @block.gpsimd
            def _(pool):
                pool.memset(ones[:, :], 1.0).then_inc(made, 1)

                def body(i, j, n):
                    for f in range(FC4):
                        at = FC4 * i + f
                        pool.wait_ge(h_ok, at + 1)
                        pool.tensor_tensor(h_lo[:, j, f], h[:, f % 2], h_hi[:, j, f].bitcast(F32), ALU.subtract
                                           ).then_inc(lo_ok, 1)

                over_blocks(pool, BLOCKS, body)

            @block.scalar
            def _(act):
                act.wait_ge(b_in, 32)
                norm_root(act, norm, 0, 0)
                high_parts(act, x_turn, 0, lambda c: xT_hi[:, 0, c])

                def body(i, j, n):
                    if not is_last(i, BLOCKS):
                        norm_root(act, norm, i + 1, 1 - j)
                    wait_past(act, yps_ok, at_least(2 * (i - 1)))
                    for f in range(FC4):
                        act.wait_ge(hps_ok, FC4 * i + f + 1)
                        act.activation(h_hi[:, j, f], ps_h[:, f % 3], ACT.Relu, bias=b1[:, f:f + 1]).then_inc(hi_ok, 1)
                        if f == 6 and not is_last(i, BLOCKS):
                            high_parts(act, x_turn, i + 1, lambda c: xT_hi[:, 1 - j, c])

                over_blocks(act, BLOCKS, body)

            @block.vector
            def _(dve):
                step = 0

                def link(op):
                    nonlocal step
                    step += 1
                    op.then_inc(q_step, 1)
                    dve.wait_ge(q_step, step)

                norm_measure(dve, norm, 0, 0)
                dve.wait_ge(w_in, 32)
                for m in range(2):
                    op = dve.tensor_reduce(size[:, m:m + 1], raw[m][:, :, :], AX.XY, ALU.add, apply_absolute_value=True)
                link(op)
                k["size_at"] = step
                norm_apply(dve, norm, 0, 0, lambda t: xn[:, 0, t:t + 1, :])
                dve.wait_ge(summed, 1)
                link(dve.tensor_scalar(gamma[:, :], ps_g[:, :], 1.0 / (D * F4), EPS, ALU.mult, ALU.add))
                link(dve.tensor_scalar(half[:, 0, :], gamma[:, :], 0.5, None, ALU.mult))
                link(dve.tensor_scalar(half[:, 1, :], gamma[:, :], -0.5, None, ALU.mult))
                for m, w in enumerate((w1, w2)):
                    flat = raw[m][:, :, :].rearrange("p c n -> p (c n)")
                    link(dve.tensor_scalar(below[:, :], flat, half[:, 1, m:m + 1], None, ALU.is_lt))
                    link(dve.scalar_tensor_tensor(out=w[:, :, :].rearrange("p c n -> p (c n)"), in0=flat,
                                                  scalar=half[:, 0, m:m + 1], in1=below[:, :],
                                                  op0=ALU.is_gt, op1=ALU.subtract))
                k["ternary_at"] = step

                def x_low(i, j):
                    low_parts(dve, x_turn, i, lambda c: xT_lo[:, j, c], lambda c: xT_hi[:, j, c])

                def result(i, j, n, g):
                    if g == 0:
                        wait_past(dve, y_out[j], 16 * n)
                    dve.wait_ge(res_ok, i + 1)
                    dve.wait_ge(yps_ok, 2 * i + g + 1)
                    dve.tensor_tensor(y[:, j, 2 * g:2 * g + 2], ps_y[:, 2 * g:2 * g + 2],
                                      k["X"][:, bass.ds(TB * i + 2 * g, 2), :], ALU.add).then_inc(y_ok, 1)

                def body(i, j, n):
                    if not is_last(i, BLOCKS):
                        norm_measure(dve, norm, i + 1, 1 - j)
                    for f in range(FC4):
                        at = FC4 * i + f
                        dve.wait_ge(hi_ok, at + 1)
                        wait_past(dve, lo_ok, at - 1)
                        dve.tensor_scalar(h[:, f % 2], ps_h[:, f % 3], b1[:, f:f + 1], 0.0, ALU.add, ALU.max
                                          ).then_inc(h_ok, 1)
                        if f == 1:
                            x = k["X"][:, bass.ds(TB * i, TB), :]
                            dve.tensor_tensor(x, x, b2[:, :].unsqueeze(1).to_broadcast([P, TB, D]), ALU.add
                                              ).then_inc(res_ok, 1)
                        if f == 3 and not is_last(i, BLOCKS):
                            norm_apply(dve, norm, i + 1, 1 - j, lambda t: xn[:, 1 - j, t:t + 1, :])
                        if f == 5 and not is_first(i):
                            result(i - 1, 1 - j, n - (1 - j), 0)
                        if f == 6 and not is_last(i, BLOCKS):
                            x_low(i + 1, 1 - j)
                    if not is_first(i):
                        result(i - 1, 1 - j, n - (1 - j), 1)

                x_low(0, 0)
                over_blocks(dve, BLOCKS, body)
                for g in range(2):
                    result(BLOCKS - 1, 1, BLOCKS // 2 - 1, g)

            @block.tensor
            def _(pe):
                pe.wait_ge(made, 1)
                pe.wait_ge(q_step, k["size_at"])
                pe.matmul(ps_g[:, :], ones[:, :], size[:, :], start=True, stop=True).then_inc(summed, 1)

                def turn(i, j):
                    pe.wait_ge(norm["xn_ok"], i + 1)
                    turn_block(pe, x_turn, i, lambda t, c: xn[:, j, t, c * P:(c + 1) * P])

                def contract(i, j, part):
                    t, half = part // 2, part % 2
                    if t % 2 == 0 and half == 0:
                        wait_past(pe, y_ok, at_least(2 * (i - 1) + t // 2 + 1))
                    for f in range(half * FC4 // 2, (half + 1) * FC4 // 2):
                        if part == 0 or t == 0:
                            pe.wait_ge(lo_ok, FC4 * i + f + 1)
                        pe.matmul(ps_y[:, t], h_hi[:, j, f, t * P:(t + 1) * P], w2[:, f], start=(f == 0), stop=False)
                        last = pe.matmul(ps_y[:, t], h_lo[:, j, f, t * P:(t + 1) * P], w2[:, f], start=False,
                                         stop=(f == FC4 - 1))
                    if t % 2 and half:
                        last.then_inc(yps_ok, 1)

                def body(i, j, n):
                    pe.wait_ge(x_turn["lo_ok"], DC * i + DC)
                    for f in range(FC4):
                        wait_past(pe, h_ok, FC4 * i + f - (1 if f < 2 else 2))
                        for d in range(DC):
                            w = w1[:, d, f * P:(f + 1) * P]
                            pe.matmul(ps_h[:, f % 3], w, xT_hi[:, j, d], start=(d == 0), stop=False)
                            last = pe.matmul(ps_h[:, f % 3], w, xT_lo[:, j, d], start=False, stop=(d == DC - 1))
                        last.then_inc(hps_ok, 1)
                        if not is_first(i):
                            contract(i - 1, 1 - j, f)
                        if f == 5 and not is_last(i, BLOCKS):
                            turn(i + 1, 1 - j)

                turn(0, 0)
                pe.wait_ge(q_step, k["ternary_at"])
                over_blocks(pe, BLOCKS, body)
                for part in range(2 * TB):
                    contract(BLOCKS - 1, 1, part)


def program(nc, io):
    io = dict(io)

    def scratch(name, shape, dt):
        return nc.dram_tensor(name, shape, dt, kind="Internal").ap()

    io["qk"] = scratch("qk_parts", (2, 3, GROUPS, BATCH, HG * DH, SEQ), BF16)
    io["shift"] = scratch("shift_parts", (3, GROUPS, BATCH, HG, SEQ), BF16)
    io["attended"] = scratch("attended", (GROUPS, BATCH, SEQ, HG * DH), F32)
    io["slots_in"] = scratch("slots_in", (SLOTS, D), F32)
    io["slots_out"] = scratch("slots_out", (SLOTS, D), F32)
    with ExitStack() as ctx:
        k = {"nc": nc, "io": io}
        k["passed"], k["residual_ok"] = (ctx.enter_context(nc.semaphore(name)) for name in ("passed", "residual_ok"))
        k["X"] = ctx.enter_context(nc.sbuf_tensor("X", [P, TILES, D], F32))
        k["ident"] = ctx.enter_context(nc.sbuf_tensor("ident", [P, P], F32))
        k["causal"] = ctx.enter_context(nc.sbuf_tensor("causal", [P, P], F32))
        k["head_sel"] = ctx.enter_context(nc.sbuf_tensor("head_sel", [P, P // DH], BF16))
        k["eps"] = ctx.enter_context(nc.sbuf_tensor("eps", [P, 1], F32))
        k["unsafe"] = ctx.enter_context(nc.sbuf_tensor("unsafe", [1, 1], I32))
        k["route"] = ctx.enter_context(nc.sbuf_tensor("route_scores", [P, TILES, EXPERTS], F32))
        k["slot"] = ctx.enter_context(nc.sbuf_tensor("slot", [P, TOP_K, TILES], I32))
        k["tile_expert"] = ctx.enter_context(nc.sbuf_tensor("tile_expert", [1, SLOT_TILES, EXPERTS], I32))
        with ExitStack() as mem, semaphores(k):
            k["V"] = mem.enter_context(nc.sbuf_tensor("V", [P, GROUPS, TILES, HG, DH + 1], F32))
            phase_constants(k)
            phase_qkv(k)
            phase_shift(k)
            phase_attention(k)
        with ExitStack() as mem, semaphores(k):
            k["xn"] = mem.enter_context(nc.sbuf_tensor("xn2", [P, TILES, D], F32))
            k["xT_hi"] = mem.enter_context(nc.sbuf_tensor("xn2T_hi", [P, DC, TOK], F32R))
            k["xT_lo"] = mem.enter_context(nc.sbuf_tensor("xn2T_lo", [P, DC, TOK], F32R))
            phase_out_projection(k)
            phase_route(k)
        with semaphores(k):
            phase_experts(k)
        for b in range(BATCH):
            with ExitStack() as mem, semaphores(k):
                def sb(name, shape):
                    return mem.enter_context(nc.sbuf_tensor(name + str(b), shape, F32R))

                k["qT_hi"], k["qT_lo"] = sb("q3T_hi", [P, DC, SEQ]), sb("q3T_lo", [P, DC, SEQ])
                k["kT_hi"], k["kT_lo"] = sb("k3T_hi", [P, DC, SEQ]), sb("k3T_lo", [P, DC, SEQ])
                k["v_hi"], k["v_lo"] = sb("v3_hi", [P, SEQ_TILES, D]), sb("v3_lo", [P, SEQ_TILES, D])
                phase_keys(k, b)
                phase_attend(k, b)
        with semaphores(k):
            phase_mlp(k)


def kernel(**inputs):
    import numpy as np
    import concourse.bacc as bacc
    from concourse.bass_utils import run_bass_kernel_spmd

    given = {name: np.asarray(a) for name, a in inputs.items()}
    arrays = {
        "x": given["L0_attn_in_features"].reshape(TOK, D),
        "wq": given["L0_attn_q_proj_weight"].T, "wk": given["L0_attn_k_proj_weight"].T,
        "wv": given["L0_attn_v_proj_weight"].T, "wo": given["L0_attn_o_proj_weight"].T,
        "router": given["L0_ffn_router_DE"],
        "w_in_shared": given["L0_ffn_w_in_shared_FD"].T, "w_swiglu": given["L0_ffn_w_swiglu_FD"].T,
        "w_out_shared": given["L0_ffn_w_out_shared_DF"].T,
        "w_in_e": given["L0_ffn_w_in_eDF"], "w_swiglu_e": given["L0_ffn_w_swiglu_eDF"],
        "w_out_e": given["L0_ffn_w_out_eFD"],
        "w_kv": given["L1_attn_W"].T,
        "w1": given["L1_ffn_W1"].T, "b1": given["L1_ffn_b1"].reshape(-1, P).T,
        "w2": given["L1_ffn_W2"].T, "b2": given["L1_ffn_b2"].reshape(1, D),
    }
    arrays = {name: np.ascontiguousarray(a) for name, a in arrays.items()}
    nc = bacc.Bacc("TRN2", target_bir_lowering=False, num_devices=1)
    io = {name: nc.dram_tensor(name, a.shape, mybir.dt.from_np(a.dtype), kind="ExternalInput").ap()
          for name, a in arrays.items()}
    io["out"] = nc.dram_tensor("out", (TOK, D), F32, kind="ExternalOutput").ap()
    program(nc, io)
    result = run_bass_kernel_spmd(nc, [arrays], core_ids=[0])
    return result.results[0]["out"].reshape(BATCH, SEQ, D)
```

```python
from contextlib import ExitStack, contextmanager

import concourse.bass as bass
from concourse import mybir

F32 = mybir.dt.float32
F32R = mybir.dt.float32r
BF16 = mybir.dt.bfloat16
I32 = mybir.dt.int32
ALU = mybir.AluOpType
ACT = mybir.ActivationFunctionType
AX = mybir.AxisListType

P = 128
BATCH, SEQ, D = 2, 2048, 256
TOK = BATCH * SEQ
DC = D // P
TILES = TOK // P
TB = 4
BT = TB * P
BLOCKS = TOK // BT
HEADS, DH = 16, D // 16
HG = 4
GROUPS = HEADS // HG
EPS = 1e-5
SHIFT_ROWS = 6 * DH
KROWS = SHIFT_ROWS + 3
UNITS = GROUPS * BATCH
Q_SLOTS, K_SLOTS = (0, 0, 1, 1, 0, 2), (0, 1, 0, 1, 2, 0)
SAFE_SQUARE = 48.0 ** 2


EXPERTS, TOP_K, FF = 8, 2, 512
FC = FF // P
SLOT_TILES = TOP_K * TOK // P + EXPERTS
REGION = TOK + P
SLOTS = EXPERTS * REGION + EXPERTS * P
OUT_SLOTS = SLOT_TILES * P


def sem(k, name):
    handle = k["sem_ctx"].enter_context(k["nc"].semaphore(name))
    k["used"].append(handle)
    return handle


def sems(k, stem, names):
    return [sem(k, f"{stem}_{n}") for n in names.split()]


@contextmanager
def semaphores(k):
    with ExitStack() as k["sem_ctx"]:
        k["used"] = []
        yield
        with k["nc"].Block() as block:

            @block.gpsimd
            def _(pool):
                for handle in k["used"]:
                    pool.sem_clear(handle)


def wait_past(eng, sem, value):
    if not isinstance(value, int) or value > 0:
        eng.wait_ge(sem, value)


def hold(eng, k, sem, value):
    eng.wait_ge(sem, value)
    eng.sem_inc(k["passed"], 1)


def is_first(i):
    return isinstance(i, int) and i == 0


def is_last(i, count):
    return isinstance(i, int) and i == count - 1


def at_least(value):
    return max(value, 0) if isinstance(value, int) else value


def over_blocks(eng, count, body):
    for j in range(2):
        body(j, j, 0)
    if count > 4:
        with eng.Fori(1, count // 2 - 1) as n:
            for j in range(2):
                body(2 * n + j, j, n)
    for j in range(2):
        body(count - 2 + j, j, count // 2 - 1)


def mm3(pe, out, lhs, rhs, start, stop):
    (lh, ll), (rh, rl) = lhs, rhs
    pe.matmul(out, lh, rh, start=start, stop=False)
    pe.matmul(out, lh, rl, start=False, stop=False)
    return pe.matmul(out, ll, rh, start=False, stop=stop)


def turner(k, stem, ps):
    ps_ok, hi_ok, lo_ok = sems(k, stem, "ps_ok hi_ok lo_ok")
    return {"ps": ps, "ident": k["ident"], "ps_ok": ps_ok, "hi_ok": hi_ok, "lo_ok": lo_ok}


def turn_block(pe, w, i, rows):
    wait_past(pe, w["lo_ok"], DC * i)
    for t in range(TB):
        for c in range(DC):
            last = pe.transpose(w["ps"][:, c, t * P:(t + 1) * P], rows(t, c), w["ident"][:, :])
    last.then_inc(w["ps_ok"], 1)


def high_parts(act, w, i, out):
    act.wait_ge(w["ps_ok"], i + 1)
    for c in range(DC):
        act.activation(out(c), w["ps"][:, c], ACT.Copy).then_inc(w["hi_ok"], 1)


def low_parts(dve, w, i, out, high):
    for c in range(DC):
        dve.wait_ge(w["hi_ok"], DC * i + c + 1)
        dve.tensor_tensor(out(c), w["ps"][:, c], high(c).bitcast(F32), ALU.subtract).then_inc(w["lo_ok"], 1)


def split_weights(dve, raw, hi, lo, sem, at):
    dve.tensor_copy(hi, raw).then_inc(sem, 1)
    dve.wait_ge(sem, at + 1)
    dve.tensor_tensor(lo, raw, hi.bitcast(F32), ALU.subtract).then_inc(sem, 1)


def phase_constants(k):
    nc = k["nc"]
    made, picked = sems(k, "constants", "made picked")
    with nc.Block() as block:

        @block.gpsimd
        def _(pool):
            pool.memset(k["ident"][:, :], 0.0).then_inc(made, 1)
            pool.memset(k["head_sel"][:, :], 1.0).then_inc(made, 1)
            pool.memset(k["eps"][:, :], EPS).then_inc(made, 1)
            pool.memset(k["causal"][:, :], 0.0).then_inc(made, 1)
            pool.memset(k["V"][:, :, :, :, DH:DH + 1], 1.0).then_inc(made, 1)
            pool.wait_ge(made, 5)
            pool.affine_select(out=k["causal"][:, :], in_=k["causal"][:, :], compare_op=ALU.is_ge, fill=-3.0e38,
                               base=0, pattern=[[-1, P]], channel_multiplier=1).then_inc(picked, 1)
            pool.affine_select(out=k["ident"][:, :], in_=k["ident"][:, :], compare_op=ALU.not_equal, fill=1.0,
                               base=0, pattern=[[-1, P]], channel_multiplier=1).then_inc(picked, 1)
            pool.affine_select(out=k["head_sel"][:, :], in_=k["head_sel"][:, :], compare_op=ALU.is_ge, fill=0.0,
                               base=0, pattern=[[-DH, P // DH]], channel_multiplier=1).then_inc(picked, 1)
            pool.wait_ge(picked, 3)
            pool.affine_select(out=k["head_sel"][:, :], in_=k["head_sel"][:, :], compare_op=ALU.is_ge, fill=0.0,
                               base=DH - 1, pattern=[[DH, P // DH]], channel_multiplier=-1).then_inc(picked, 1)


def layer_norm(k, mem, stem):
    nc = k["nc"]
    norm = {"X": k["X"], "eps": k["eps"], "k": k}
    for name, shape in (("stats", [P, 2, TB, 6]), ("moments", [P, 2, TB, 2]), ("std", [P, 2, TB]), ("rstd", [P, 2, TB])):
        norm[name] = mem.enter_context(nc.sbuf_tensor(f"{stem}_{name}", shape, F32))
    for name in ("stats_ok", "moments_ok", "std_ok", "rstd_ok", "xn_ok"):
        norm[name] = sem(k, f"{stem}_{name}")
    return norm


def norm_measure(dve, w, b, j, first=0):
    for t in range(TB):
        dve.bn_stats(w["stats"][:, j, t, :], w["X"][:, bass.ds(first + TB * b + t, 1), :]).then_inc(w["stats_ok"], 1)
    hold(dve, w["k"], w["stats_ok"], TB * b + TB)
    for t in range(TB):
        dve.bn_aggr(w["moments"][:, j, t, :], w["stats"][:, j, t, :]).then_inc(w["moments_ok"], 1)


def norm_root(act, w, b, j):
    act.wait_ge(w["moments_ok"], TB * b + TB)
    act.activation(w["std"][:, j], w["moments"][:, j, :, 1], ACT.Sqrt, bias=w["eps"][:, 0:1]).then_inc(w["std_ok"], 1)


def norm_apply(dve, w, b, j, out, first=0):
    dve.wait_ge(w["std_ok"], b + 1)
    dve.reciprocal(w["rstd"][:, j], w["std"][:, j]).then_inc(w["rstd_ok"], 1)
    dve.wait_ge(w["rstd_ok"], b + 1)
    for t in range(TB):
        last = dve.tensor_scalar(out(t), w["X"][:, bass.ds(first + TB * b + t, 1), :], w["moments"][:, j, t, 0:1],
                                 w["rstd"][:, j, t:t + 1], ALU.subtract, ALU.mult)
    last.then_inc(w["xn_ok"], 1)


def phase_qkv(k):
    nc, io = k["nc"], k["io"]
    with ExitStack() as mem:
        def sb(name, shape, dt):
            return mem.enter_context(nc.sbuf_tensor(name, shape, dt))

        def ps(name, shape, dt=F32):
            return mem.enter_context(nc.psum_tensor(name, shape, dt))

        w_raw = sb("w_raw", [P, 3, DC, D], F32)
        w_hi = sb("w_hi", [P, 3, DC, D], F32R)
        w_lo = sb("w_lo", [P, 3, DC, D], F32R)
        xn = sb("xn1", [P, 2, TB, D], F32)
        xnT_hi = sb("xn1T_hi", [P, 2, DC, BT], F32R)
        xnT_lo = sb("xn1T_lo", [P, 2, DC, BT], F32R)
        part1 = sb("part1", [P, 2, 4, BT], BF16)
        part2 = sb("part2", [P, 2, 4, BT], BF16)
        part3 = sb("part3", [P, 2, 4, BT], BF16)
        rest = sb("rest", [P, 2, 4, BT], F32)
        square = sb("square", [P, 2, 4, BT], BF16)
        norm_max = sb("norm_max", [P, BLOCKS], F32)
        norm_top = sb("norm_top", [P, 1], F32)
        norm_row = sb("norm_row", [1, P], F32)
        over = sb("over", [1, 2, 8], F32)
        zeros = sb("shift_zeros", [P, HEADS * TOK * 3 // P], BF16)
        ps_t = ps("ps_t", [P, DC, BT])
        ps_qk = ps("ps_qk", [P, 4, BT])
        ps_v = ps("ps_v", [P, 2, D])
        ps_n = ps("ps_n", [P, BT])
        norm = layer_norm(k, mem, "ln1")

        w_in, w_split, zero_ok, zero_out = sems(k, "qkv", "w_in w_split zero_ok zero_out")
        x_in = sems(k, "x_in", "even odd")
        parts_out = sems(k, "parts_out", "even odd")
        t_ok, t_hi_ok, t_lo_ok = sems(k, "qkv", "t_ok t_hi_ok t_lo_ok")
        qk_ok, part1_ok, rest_ok, part2_ok, part3_ok = sems(k, "qkv", "qk_ok part1_ok rest_ok part2_ok part3_ok")
        v_ok, v_used, n_ok, n_used, top_ok, topT_ok, row_ok = sems(k, 
            "qkv", "v_ok v_used n_ok n_used top_ok topT_ok row_ok")

        x_view = io["x"].rearrange("(n p) d -> p n d", p=P)
        with nc.Block() as block:

            @block.sync
            def _(sp):
                sp.dma_start(k["X"][:, 0:TB, :], x_view[:, 0:TB, :]).then_inc(x_in[0], 16)
                for n, name in enumerate("qkv"):
                    sp.dma_start(w_raw[:, n], io["w" + name].rearrange("(c p) n -> p c n", p=P)).then_inc(w_in, 16)
                for b in range(1, BLOCKS):
                    wait_past(sp, x_in[b % 2], 16 * (b // 2))
                    sp.dma_start(k["X"][:, b * TB:(b + 1) * TB, :],
                                 x_view[:, b * TB:(b + 1) * TB, :]).then_inc(x_in[b % 2], 16)
                sp.wait_ge(zero_ok, 1)
                sp.dma_start(io["shift"].rearrange("m g b h t -> (m g b h t)").rearrange("(p n) -> p n", p=P),
                             zeros[:, :]).then_inc(zero_out, 16)
                for b in range(BLOCKS):
                    j = b % 2
                    sp.wait_ge(part3_ok, b + 1)
                    t0 = b * BT % SEQ
                    for n, part in enumerate((part1, part2, part3)):
                        for m in range(2):
                            to = io["qk"][m, n, :, b * BT // SEQ, :, t0:t0 + BT].rearrange(
                                "(c g) r t -> g r c t", c=DC)
                            for g in range(2):
                                sp.dma_start(to[g], part[64 * g:64 * g + 64, j, DC * m:DC * m + DC]).then_inc(
                                    parts_out[j], 16)
                for j in range(2):
                    sp.wait_ge(parts_out[j], 192 * (BLOCKS // 2))
                sp.wait_ge(zero_out, 16)

            @block.gpsimd
            def _(pool):
                pool.memset(zeros[:, :].bitcast(I32), 0).then_inc(zero_ok, 1)

                def body(i, j, n):
                    pool.wait_ge(part2_ok, i + 1)
                    wait_past(pool, parts_out[j], 192 * n)
                    pool.tensor_tensor(part3[:, j], rest[:, j], part2[:, j], ALU.subtract).then_inc(part3_ok, 1)

                over_blocks(pool, BLOCKS, body)

            @block.scalar
            def _(act):
                def highs(i, j):
                    act.wait_ge(t_ok, i + 1)
                    for c in range(DC):
                        act.activation(xnT_hi[:, j, c], ps_t[:, c], ACT.Copy).then_inc(t_hi_ok, 1)

                def body(i, j, n):
                    wait_past(act, parts_out[j], 192 * n)
                    wait_past(act, n_ok, i - 1 if not isinstance(i, int) or i else 0)
                    for c in range(4):
                        act.wait_ge(qk_ok, 4 * i + c + 1)
                        scale = DH ** -0.5 if c < DC else 1.0
                        act.activation(part1[:, j, c], ps_qk[:, c], ACT.Copy, scale=scale)
                        act.activation(square[:, j, c], ps_qk[:, c], ACT.Square, scale=scale).then_inc(part1_ok, 1)
                        if c == 0 and not is_last(i, BLOCKS):
                            norm_root(act, norm, i + 1, 1 - j)
                        if c == 2 and not is_last(i, BLOCKS):
                            highs(i + 1, 1 - j)
                        if c % 2:
                            g = c // 2
                            act.wait_ge(v_ok, 2 * i + g + 1)
                            for t in range(2):
                                last = act.activation(
                                    k["V"][:, :, bass.ds(TB * i + 2 * g + t, 1), :, 0:DH],
                                    ps_v[:, t].rearrange("p (g h d) -> p g h d", h=HG, d=DH), ACT.Copy)
                            last.then_inc(v_used, 1)

                norm_root(act, norm, 0, 0)
                highs(0, 0)
                over_blocks(act, BLOCKS, body)

            @block.vector
            def _(dve):
                dve.memset(ps_n[:, :], 0.0).then_inc(n_used, 1)
                dve.wait_ge(x_in[0], 16)
                norm_measure(dve, norm, 0, 0)
                dve.wait_ge(w_in, 48)
                dve.tensor_copy(w_hi[:, :], w_raw[:, :]).then_inc(w_split, 1)
                dve.wait_ge(w_split, 1)
                dve.tensor_tensor(w_lo[:, :], w_raw[:, :], w_hi[:, :].bitcast(F32), ALU.subtract).then_inc(w_split, 1)
                norm_apply(dve, norm, 0, 0, lambda t: xn[:, 0, t:t + 1, :])

                def rests(i, j, c):
                    dve.wait_ge(part1_ok, 4 * i + c + 1)
                    if c < DC:
                        op = dve.scalar_tensor_tensor(out=rest[:, j, c], in0=ps_qk[:, c], scalar=DH ** -0.5,
                                                      in1=part1[:, j, c], op0=ALU.mult, op1=ALU.subtract)
                    else:
                        op = dve.tensor_tensor(rest[:, j, c], ps_qk[:, c], part1[:, j, c], ALU.subtract)
                    op.then_inc(rest_ok, 1)

                def lows(i, j):
                    for c in range(DC):
                        dve.wait_ge(t_hi_ok, DC * i + c + 1)
                        dve.tensor_tensor(xnT_lo[:, j, c], ps_t[:, c], xnT_hi[:, j, c].bitcast(F32),
                                          ALU.subtract).then_inc(t_lo_ok, 1)

                def greatest_norms(i):
                    dve.wait_ge(n_ok, i + 1)
                    dve.tensor_reduce(norm_max[:, bass.ds(i, 1)], ps_n[:, :], AX.X, ALU.max).then_inc(n_used, 1)

                def body(i, j, n):
                    last = is_last(i, BLOCKS)
                    if not last:
                        hold(dve, k, x_in[1 - j], 16 * (n + j) + 16)
                        norm_measure(dve, norm, i + 1, 1 - j)
                    wait_past(dve, part3_ok, i - 1 if not isinstance(i, int) or i else 0)
                    rests(i, j, 0)
                    rests(i, j, 1)
                    if not is_first(i):
                        greatest_norms(i - 1)
                    if not last:
                        norm_apply(dve, norm, i + 1, 1 - j, lambda t: xn[:, 1 - j, t:t + 1, :])
                    rests(i, j, 2)
                    if not last:
                        lows(i + 1, 1 - j)
                    rests(i, j, 3)
                    dve.wait_ge(rest_ok, 4 * i + 4)
                    wait_past(dve, parts_out[j], 192 * n)
                    dve.tensor_copy(part2[:, j], rest[:, j]).then_inc(part2_ok, 1)

                lows(0, 0)
                over_blocks(dve, BLOCKS, body)
                greatest_norms(BLOCKS - 1)
                dve.wait_ge(n_used, BLOCKS + 1)
                dve.tensor_reduce(norm_top[:, :], norm_max[:, :], AX.X, ALU.max).then_inc(top_ok, 1)
                dve.wait_ge(topT_ok, 1)
                dve.tensor_copy(norm_row[:, :], ps_n[0:1, 0:P]).then_inc(row_ok, 1)
                dve.wait_ge(row_ok, 1)
                row = norm_row[:, :].rearrange("p (m c r) -> p m c r", m=2, c=2)
                dve.tensor_tensor(over[:, :, :], row[:, 0, :, 0:8], row[:, 1, :, 0:8], ALU.mult).then_inc(row_ok, 1)
                dve.wait_ge(row_ok, 2)
                dve.tensor_scalar(over[:, :, :], over[:, :, :], SAFE_SQUARE, None, ALU.is_gt).then_inc(row_ok, 1)
                dve.wait_ge(row_ok, 3)
                dve.tensor_reduce(k["unsafe"][:, :], over[:, :, :], AX.XY, ALU.max).then_inc(row_ok, 1)

            @block.tensor
            def _(pe):
                def turn(i, j):
                    pe.wait_ge(norm["xn_ok"], i + 1)
                    wait_past(pe, t_lo_ok, DC * i)
                    for t in range(TB):
                        for c in range(DC):
                            last = pe.transpose(ps_t[:, c, t * P:(t + 1) * P],
                                                xn[:, j, t, c * P:(c + 1) * P], k["ident"][:, :])
                    last.then_inc(t_ok, 1)

                def norms(i, j):
                    pe.wait_ge(part1_ok, 4 * i + 4)
                    pe.wait_ge(n_used, i + 1)
                    for c in range(4):
                        last = pe.matmul(ps_n[32 * c:32 * c + 8, :], k["head_sel"][:, :], square[:, j, c],
                                         start=True, stop=True)
                    last.then_inc(n_ok, 1)

                def body(i, j, n):
                    pe.wait_ge(t_lo_ok, DC * i + DC)
                    for c in range(4):
                        wait_past(pe, rest_ok, 4 * i + c - 3)
                        w, o = c // DC, (c % DC) * P
                        for d in range(DC):
                            last = mm3(pe, ps_qk[:, c], (w_hi[:, w, d, o:o + P], w_lo[:, w, d, o:o + P]),
                                       (xnT_hi[:, j, d], xnT_lo[:, j, d]), d == 0, d == DC - 1)
                        last.then_inc(qk_ok, 1)
                        if c % 2:
                            g = c // 2
                            wait_past(pe, v_used, 2 * i + g)
                            for t in range(2):
                                o = (2 * g + t) * P
                                for d in range(DC):
                                    last = mm3(pe, ps_v[:, t], (xnT_hi[:, j, d, o:o + P], xnT_lo[:, j, d, o:o + P]),
                                               (w_hi[:, 2, d], w_lo[:, 2, d]), d == 0, d == DC - 1)
                            last.then_inc(v_ok, 1)
                        if c == 0 and not is_first(i):
                            norms(i - 1, 1 - j)
                        if c == 2 and not is_last(i, BLOCKS):
                            turn(i + 1, 1 - j)

                pe.wait_ge(w_split, 2)
                turn(0, 0)
                over_blocks(pe, BLOCKS, body)
                norms(BLOCKS - 1, 1)
                pe.wait_ge(top_ok, 1)
                pe.transpose(ps_n[0:1, 0:P], norm_top[:, :], k["ident"][:, :]).then_inc(topT_ok, 1)


def load_stacks(eng, io, u, Q, K, sem):
    for slots, dst, m in ((Q_SLOTS, Q, 0), (K_SLOTS, K, 1)):
        for n, part in enumerate(slots):
            src = io["qk"].rearrange("m n g b r t -> m n (g b) r t")[m, part, bass.ds(u, 1)]
            eng.dma_start(dst[DH * n:DH * n + DH], src.rearrange("o (h d) t -> d (o h) t", d=DH)).then_inc(sem, 16)


def phase_shift(k):
    nc, io = k["nc"], k["io"]
    QT = SEQ // P
    with ExitStack() as mem:
        def sb(name, shape, dt):
            return mem.enter_context(nc.sbuf_tensor(name, shape, dt))

        Q, K = sb("Q_max", [P, HG, SEQ], BF16), sb("K_max", [P, HG, SEQ], BF16)
        mask = sb("wide_mask", [P, 2 * SEQ - P], BF16)
        masked = sb("masked_scores", [P, SEQ], F32)
        top = sb("top", [P, HG * QT], F32)
        neg = sb("neg_top", [HG * QT, P], F32)
        left = sb("left", [HG * QT, 2, P], F32)
        parts = sb("shift_part", [HG * QT, 3, P], BF16)
        ps_s = mem.enter_context(nc.psum_tensor("ps_max", [P, SEQ], F32))
        ps_t = mem.enter_context(nc.psum_tensor("ps_top", [HG * QT, P], F32))
        loaded, scores_ok, mask_ok, masked_ok, top_ok, turned_ok, neg_ok, split_ok, stored, parts_free = sems(k, 
            "shift", "loaded scores_ok mask_ok masked_ok top_ok turned_ok neg_ok split_ok stored parts_free")
        EACH = HG * QT

        with nc.Block() as block:

            def where_unsafe(eng):
                return eng.If(eng.value_load(k["unsafe"][0:1, 0:1], min_val=0, max_val=1) > 0)

            @block.sync
            def _(sp):
                with where_unsafe(sp):
                    load_stacks(sp, io, 0, Q[:, :, :], K[:, :, :], loaded)
                    with sp.Fori(1, UNITS) as u:
                        hold(sp, k, scores_ok, EACH * u)
                        load_stacks(sp, io, u, Q[:, :, :], K[:, :, :], loaded)
                    sp.wait_ge(loaded, 16 * 12 * UNITS)

            @block.gpsimd
            def _(pool):
                with where_unsafe(pool):
                    pool.memset(mask[:, :], 0.0).then_inc(mask_ok, 1)
                    pool.wait_ge(mask_ok, 1)
                    pool.affine_select(out=mask[:, :], in_=mask[:, :], compare_op=ALU.is_ge, fill=-3.0e38,
                                       base=SEQ - P, pattern=[[-1, 2 * SEQ - P]], channel_multiplier=1
                                       ).then_inc(mask_ok, 1)
                    with pool.Fori(0, UNITS) as u:
                        hold(pool, k, split_ok, 3 * u + 3)
                        for n in range(3):
                            pool.dma_start(
                                io["shift"].rearrange("m g b h (t p) -> m (g b) (h t) p", p=P)[n, bass.ds(u, 1)]
                                .rearrange("o r p -> (o r) p"), parts[:, n, :]).then_inc(stored, 16)
                        pool.wait_ge(stored, 48 * u + 48)
                        pool.sem_inc(parts_free, 1)

            @block.vector
            def _(dve):
                with where_unsafe(dve):
                    dve.sem_inc(masked_ok, 1)
                    dve.sem_inc(parts_free, 1)
                    dve.sem_inc(top_ok, 1)
                    dve.wait_ge(mask_ok, 2)
                    with dve.Fori(0, UNITS) as u:
                        for h in range(HG):
                            with dve.Fori(0, QT) as t:
                                at = EACH * u + QT * h + t
                                dve.wait_ge(scores_ok, at + 1)
                                dve.wait_ge(top_ok, at + 1)
                                dve.tensor_tensor(masked[:, :], ps_s[:, :], mask[:, bass.ds(SEQ - P - P * t, SEQ)],
                                                  ALU.add).then_inc(masked_ok, 1)
                                dve.wait_ge(masked_ok, at + 2)
                                dve.tensor_reduce(top[:, bass.ds(QT * h + t, 1)], masked[:, :], AX.X, ALU.max
                                                  ).then_inc(top_ok, 1)
                        dve.wait_ge(turned_ok, u + 1)
                        dve.tensor_scalar(neg[:, :], ps_t[:, :], -1.0, None, ALU.mult).then_inc(neg_ok, 1)
                        dve.wait_ge(neg_ok, 3 * u + 1)
                        dve.wait_ge(parts_free, u + 1)
                        rest = neg[:, :]
                        for n in range(3):
                            dve.tensor_copy(parts[:, n], rest).then_inc(split_ok, 1)
                            if n < 2:
                                dve.wait_ge(split_ok, 3 * u + n + 1)
                                dve.tensor_tensor(left[:, n], rest, parts[:, n], ALU.subtract).then_inc(neg_ok, 1)
                                dve.wait_ge(neg_ok, 3 * u + n + 2)
                                rest = left[:, n]

            @block.tensor
            def _(pe):
                with where_unsafe(pe):
                    with pe.Fori(0, UNITS) as u:
                        hold(pe, k, loaded, 192 * u + 192)
                        for h in range(HG):
                            with pe.Fori(0, QT) as t:
                                at = EACH * u + QT * h + t
                                pe.wait_ge(masked_ok, at + 1)
                                for c in range(0, SEQ, BT):
                                    last = pe.matmul(ps_s[:, c:c + BT], Q[0:SHIFT_ROWS, h, bass.ds(P * t, P)],
                                                     K[0:SHIFT_ROWS, h, c:c + BT], start=True, stop=True)
                                last.then_inc(scores_ok, 1)
                        hold(pe, k, top_ok, EACH * u + EACH + 1)
                        pe.transpose(ps_t[:, :], top[:, :], k["ident"][:, :]).then_inc(turned_ok, 1)


def phase_attention(k):
    nc, io = k["nc"], k["io"]
    SLICES = SEQ // BT
    TILE_LIST = [(q, t, max(0, (t - TB * q) * P)) for q in range(SLICES) for t in range(TB * (q + 1))]
    NT = len(TILE_LIST)
    LAST = [max(g for g, (q, _, _) in enumerate(TILE_LIST) if q == s) for s in range(SLICES)]
    DIAG = [g for g, (q, t, _) in enumerate(TILE_LIST) if t >= TB * q]
    SCORE_BUFS, PROB_BUFS = 3, 4
    LAG = 2
    LOADS = 13

    with ExitStack() as mem:
        def sb(name, shape, dt):
            return mem.enter_context(nc.sbuf_tensor(name, shape, dt))

        Q = sb("Q_stack", [P, 2, HG, SEQ], BF16)
        K = sb("K_stack", [P, 2, HG, SEQ], BF16)
        V = sb("V_unit", [P, 2, SEQ // P, HG, DH + 1], F32)
        probs = sb("probs", [P, PROB_BUFS, HG, BT], F32)
        sums = sb("weighted", [P, 2, BT], F32)
        inv = sb("inv_denominator", [P, 2, TB, HG], F32)
        result = sb("attention_rows", [P, 2, TB, HG, DH], F32)
        ps_s = mem.enter_context(nc.psum_tensor("ps_s", [P, SCORE_BUFS, 2, BT], F32))
        ps_o = mem.enter_context(nc.psum_tensor("ps_o", [P, 2, BT], F32))

        loaded = sems(k, "unit_loaded", "even odd")
        stored = sems(k, "rows_stored", "even odd")
        ones_ok, zero_ok, v_ok, scores_ok, exp_ok, mask_ok, pv_ok, sums_ok, turned_ok, inv_ok, result_ok = sems(k, 
            "attention", "ones_ok zero_ok v_ok scores_ok exp_ok mask_ok pv_ok sums_ok turned_ok inv_ok result_ok")

        with nc.Block() as block:

            def load(eng, u, j):
                load_stacks(eng, io, u, Q[:, j], K[:, j], loaded[j])
                src = io["shift"].rearrange("m g b h t -> m (g b) h t")[:, bass.ds(u, 1)]
                eng.dma_start(Q[SHIFT_ROWS:KROWS, j], src.rearrange("m o h t -> m (o h) t")).then_inc(loaded[j], 16)

            @block.sync
            def _(sp):
                load(sp, 0, 0)
                load(sp, 1, 1)

                def store(u, j, n):
                    for q in range(SLICES):
                        hold(sp, k, result_ok, SLICES * u + q + 1 + 2)
                        to = io["attended"].rearrange("g b (s t p) c -> (g b) s p t c", p=P, t=TB)
                        sp.dma_start(to[bass.ds(u, 1), q].rearrange("o p t c -> p (o t) c"),
                                     result[:, q % 2].rearrange("p t h d -> p t (h d)")).then_inc(stored[q % 2], 16)

                with sp.Fori(0, UNITS // 2 - 1) as n:
                    for j in range(2):
                        u = 2 * n + j
                        store(u, j, n)
                        hold(sp, k, scores_ok, 2 * NT * u + 2 * NT)
                        load(sp, u + 2, j)
                for j in range(2):
                    store(UNITS - 2 + j, j, UNITS // 2 - 1)
                for j in range(2):
                    sp.wait_ge(stored[j], 16 * (SLICES // 2 * UNITS + 1))

            @block.gpsimd
            def _(pool):
                pool.memset(K[SHIFT_ROWS:P, :, :, :], 1.0).then_inc(ones_ok, 1)
                with pool.Fori(0, UNITS // 2) as n:
                    for j in range(2):
                        u = 2 * n + j
                        for g in DIAG:
                            off = TILE_LIST[g][2]
                            block_of = probs[:, g % PROB_BUFS, :, off:off + P]
                            hold(pool, k, exp_ok, 2 * NT * u + 2 * g + 2 + 2)
                            pool.affine_select(out=block_of, in_=block_of, compare_op=ALU.is_ge, fill=0.0, base=0,
                                               pattern=[[0, HG], [1, P]], channel_multiplier=-1).then_inc(mask_ok, 1)

            @block.scalar
            def _(act):
                act.sem_inc(exp_ok, 2)
                with act.Fori(0, UNITS // 2) as n:
                    for j in range(2):
                        u = 2 * n + j
                        for g, (q, t, off) in enumerate(TILE_LIST):
                            for p in range(2):
                                s = 2 * g + p
                                if p == 0:
                                    act.wait_ge(pv_ok, NT * u + g + 1)
                                act.wait_ge(scores_ok, 2 * NT * u + s + 1)
                                act.activation(probs[:, g % PROB_BUFS, 2 * p:2 * p + 2, off:BT],
                                               ps_s[:, s % SCORE_BUFS, :, off:BT], ACT.Exp).then_inc(exp_ok, 1)

            @block.vector
            def _(dve):
                dve.memset(ps_o[:, :, :], 0.0).then_inc(zero_ok, 1)
                dve.sem_inc(result_ok, 2)
                dve.sem_inc(stored[0], 16)
                dve.sem_inc(stored[1], 16)

                def take_v(u, j):
                    dve.tensor_copy(V[:, j], k["V"].rearrange("p g (b t) h d -> p (g b) t h d", b=BATCH)[:, bass.ds(u, 1)]
                                    ).then_inc(v_ok, 1)

                def unit(u, j, n):
                    for q in range(SLICES):
                        dve.wait_ge(pv_ok, NT * u + LAST[q] + 1 + PROB_BUFS)
                        dve.tensor_copy(sums[:, q % 2], ps_o[:, q % 2]).then_inc(sums_ok, 1)
                        dve.wait_ge(turned_ok, SLICES * u + q + 1)
                        turned = ps_o[:, q % 2].rearrange("p (t h c) -> p t h c", t=TB, h=HG)
                        dve.reciprocal(inv[:, q % 2], turned[:, :, :, DH]).then_inc(inv_ok, 1)
                        dve.wait_ge(inv_ok, SLICES * u + q + 1)
                        dve.wait_ge(stored[q % 2], 16 * (SLICES // 2 * u + q // 2 + 1))
                        dve.tensor_tensor(result[:, q % 2], turned[:, :, :, 0:DH],
                                          inv[:, q % 2].unsqueeze(3).to_broadcast([P, TB, HG, DH]),
                                          ALU.mult).then_inc(result_ok, 1)

                take_v(0, 0)
                take_v(1, 1)
                with dve.Fori(0, UNITS // 2 - 1) as n:
                    for j in range(2):
                        unit(2 * n + j, j, n)
                        take_v(2 * n + j + 2, j)
                for j in range(2):
                    unit(UNITS - 2 + j, j, UNITS // 2 - 1)

            @block.tensor
            def _(pe):
                pe.sem_inc(pv_ok, PROB_BUFS)
                pe.wait_ge(ones_ok, 1)
                pe.wait_ge(zero_ok, 1)

                def scores(u, j, g):
                    q, t, off = TILE_LIST[g]
                    for p in range(2):
                        s = 2 * g + p
                        before = s - SCORE_BUFS if s >= SCORE_BUFS else max(
                            x for x in range(2 * NT) if x % SCORE_BUFS == s % SCORE_BUFS) - 2 * NT
                        pe.wait_ge(exp_ok, 2 * NT * u + before + 1 + 2)
                        for h in range(2):
                            last = pe.matmul(ps_s[:, s % SCORE_BUFS, h, off:BT],
                                             K[0:KROWS, j, 2 * p + h, t * P:(t + 1) * P],
                                             Q[0:KROWS, j, 2 * p + h, q * BT + off:(q + 1) * BT],
                                             start=True, stop=True)
                        last.then_inc(scores_ok, 1)

                def weigh(u, j, g):
                    q, t, off = TILE_LIST[g]
                    if t == 0:
                        pe.wait_ge(result_ok, SLICES * u + q + 1)
                    pe.wait_ge(exp_ok, 2 * NT * u + 2 * g + 2 + 2)
                    if g in DIAG:
                        pe.wait_ge(mask_ok, len(DIAG) * u + DIAG.index(g) + 1)
                    for h in range(HG):
                        last = pe.matmul(ps_o[32 * h:32 * h + DH + 1, q % 2, off:BT], V[:, j, t, h, :],
                                         probs[:, g % PROB_BUFS, h, off:BT],
                                         start=(t == 0), stop=(g == LAST[q]))
                    last.then_inc(pv_ok, 1)

                def turn(u, q):
                    pe.wait_ge(sums_ok, SLICES * u + q + 1)
                    for t in range(TB):
                        last = pe.transpose(ps_o[:, q % 2, t * P:(t + 1) * P], sums[:, q % 2, t * P:(t + 1) * P],
                                            k["ident"][:, :])
                    last.then_inc(turned_ok, 1)

                with pe.Fori(0, UNITS // 2) as n:
                    steps = [(j, g) for j in range(2) for g in range(NT)]
                    for at in range(len(steps) + LAG + 2):
                        if at < len(steps):
                            j, g = steps[at]
                            if g == 0:
                                pe.wait_ge(loaded[j], 16 * LOADS * n + 16 * LOADS)
                                pe.wait_ge(v_ok, 2 * n + j + 1)
                            scores(2 * n + j, j, g)
                        if 0 <= at - LAG < len(steps):
                            j, g = steps[at - LAG]
                            weigh(2 * n + j, j, g)
                        if at - LAG - 2 >= 0:
                            j, g = steps[at - LAG - 2]
                            if g in LAST:
                                turn(2 * n + j, LAST.index(g))


def live(i):
    return not isinstance(i, int) or 0 <= i < BLOCKS


def over_steps(eng, step):
    for i in range(2):
        step(i, i % 2, i // 2)
    with eng.Fori(1, BLOCKS // 2 - 1) as n:
        for j in range(2):
            step(2 * n + j, j, n)
    for i in range(BLOCKS - 2, BLOCKS + 2):
        step(i, i % 2, i // 2)


def phase_tokens(k):
    nc, io = k["nc"], k["io"]
    FULL = [P, TB, EXPERTS, EXPERTS]
    RANKS, PLACES = 11, 6
    with ExitStack() as mem:
        def sb(name, shape, dt):
            return mem.enter_context(nc.sbuf_tensor(name, shape, dt))

        def ps(name, shape, dt=F32):
            return mem.enter_context(nc.psum_tensor(name, shape, dt))

        w_hi, w_lo = sb("wo_hi", [P, DC, D], F32R), sb("wo_lo", [P, DC, D], F32R)
        r_raw = sb("router_raw", [P, DC, EXPERTS], F32)
        r_hi, r_lo = sb("router_hi", [P, DC, EXPERTS], F32R), sb("router_lo", [P, DC, EXPERTS], F32R)
        rows = sb("attended_rows", [P, 2, TB, GROUPS, HG * DH], F32)
        aT_hi, aT_lo = sb("aT_hi", [P, DC, BT], F32R), sb("aT_lo", [P, DC, BT], F32R)
        xn = sb("xn2", [P, 2, TB, D], F32)
        xT_hi, xT_lo = sb("xn2T_hi", [P, 2, DC, BT], F32R), sb("xn2T_lo", [P, 2, DC, BT], F32R)
        lower = sb("lower_index", [P, EXPERTS, EXPERTS], BF16)
        higher = sb("higher_index", [P, EXPERTS, EXPERTS], BF16)
        score = sb("router_scores", [P, TB, EXPERTS], F32)
        beats, ties = sb("beats", FULL, BF16), sb("ties", FULL, BF16)
        rank = sb("rank", [P, TB, EXPERTS], F32)
        is_rank = sb("is_rank", [P, TOP_K, TB, EXPERTS], F32)
        chosen = sb("chosen", [P, TB, EXPERTS], BF16)
        before = sb("before", [P, P], BF16)
        ones = sb("ones_square", [P, P], BF16)
        region_int = sb("region_int", [P, EXPERTS], I32)
        region = sb("region", [P, EXPERTS], F32)
        base = sb("next_row", [P, EXPERTS], F32)
        place = sb("place", [P, TB, EXPERTS], F32)
        picked = sb("picked", [P, TOP_K, TB, EXPERTS], F32)
        place_of = sb("place_of", [P, TOP_K, TB], F32)
        score_of = sb("score_of", [P, TOP_K, TB], F32)
        gate = sb("gate", [P, TOP_K, TB], F32)
        scaled = sb("scaled_rows", [P, TOP_K * TB, D], F32)
        count = sb("count", [P, EXPERTS], F32)
        padded = sb("padded_int", [P, EXPERTS], I32)
        room = sb("room", [P, EXPERTS], F32)
        ends = sb("ends", [P, EXPERTS], F32)
        unused = sb("unused_rows", [P, EXPERTS], F32)
        zeros = sb("zero_row", [P, D], F32)
        start_int = sb("tile_start_int", [1, SLOT_TILES], I32)
        tile_start = sb("tile_start", [1, SLOT_TILES], F32)
        expert = sb("tile_expert_f", [1, SLOT_TILES], F32)
        tile_row = sb("tile_row_f", [1, SLOT_TILES], F32)
        end_row = sb("end_row", [1, EXPERTS], I32)
        wi_hi, wi_lo = sb("w_in_hi", [P, DC, FF], F32R), sb("w_in_lo", [P, DC, FF], F32R)
        wg_hi, wg_lo = sb("w_swiglu_hi", [P, DC, FF], F32R), sb("w_swiglu_lo", [P, DC, FF], F32R)
        wo_hi, wo_lo = sb("w_out_hi", [P, FC, D], F32R), sb("w_out_lo", [P, FC, D], F32R)
        silu = sb("silu", [P, 2, BT], F32)
        h = sb("h_shared", [P, 2, BT], F32)
        w_raw = silu[:, 0, :].rearrange("p (c n) -> p c n", c=DC)
        s_raws = (h[:, :, :], scaled[:, 0:4, :].rearrange("p s d -> p (s d)").rearrange("p (c n) -> p c n", c=DC),
                  scaled[:, 4:8, :])
        moved, out_row, moved_sum = (silu[:, :, :].rearrange("p n t -> p (n t)")[:, at:at + size] for at, size in (
            (0, TOP_K * TILES * (EXPERTS - 1)), (512, TOP_K * TILES), (512 + TOP_K * TILES, TOP_K * TILES)))
        moved = moved.rearrange("p (s e) -> p s e", e=EXPERTS - 1)
        passed_end, skipped = (a[0:1, :, :].rearrange("p n t -> p (n t)")[:, 0:SLOT_TILES * EXPERTS].rearrange(
            "p (s e) -> p s e", e=EXPERTS) for a in (silu, h))
        h_hi, h_lo = sb("h_hi", [P, FC, BT], F32R), sb("h_lo", [P, FC, BT], F32R)

        ps_t, ps_y = ps("ps_turned", [P, DC, BT]), ps("ps_rows", [P, TB, D])
        ps_m, ps_g = ps("ps_mid", [P, BT]), ps("ps_gated", [P, BT])
        ps_r = ps("ps_router", [P, TB, EXPERTS])
        ps_b = ps("ps_places", [P, TB + 1, EXPERTS])

        norm = layer_norm(k, mem, "ln2")
        a_turn, x_turn = turner(k, "a_turn", ps_t), turner(k, "x2_turn", ps_t)
        w_in, w_split, y_ok, added_ok, r_ok, r_used = sems(k, "out_projection", "w_in w_split y_ok added_ok r_ok r_used")
        rows_in = sems(k, "rows_in", "even odd")
        made, rank_step, chosen_ok, counted, place_step, gate_ok, scaled_ok = sems(
            k, "route", "made rank_step chosen_ok counted place_step gate_ok scaled_ok")
        table_step, spare_ok, pad_ok, pads_out = sems(k, "table", "table_step spare_ok pad_ok pads_out")
        scattered = sem(k, "scattered")
        s_in, s_high, s_split = sems(k, "shared", "w_in w_high w_split")
        mid_ok, gated_ok, silu_ok, h_ok, hi_ok, lo_ok, s_ok, s_used = sems(
            k, "shared", "mid_ok gated_ok silu_ok h_ok hi_ok lo_ok s_ok s_used")

        with nc.Block() as block:

            @block.sync
            def _(sp):
                def load(i):
                    b, t0 = i * BT // SEQ, i * BT % SEQ
                    for g in range(GROUPS):
                        sp.dma_start(rows[:, i % 2, :, g, :],
                                     io["attended"][g, b, t0:t0 + BT, :].rearrange("(t p) c -> p t c", p=P)
                                     ).then_inc(rows_in[i % 2], 16)

                sp.dma_start(w_raw[:, :, :], io["wo"].rearrange("(c p) n -> p c n", p=P)).then_inc(w_in, 16)
                load(0)
                sp.dma_start(r_raw[:, :, :], io["router"].rearrange("(c p) n -> p c n", p=P)).then_inc(w_in, 16)
                load(1)
                for name, raw in zip(("w_in_shared", "w_swiglu", "w_out_shared"), s_raws):
                    sp.dma_start(raw, io[name].rearrange("(c p) n -> p c n", p=P)).then_inc(s_in, 16)
                sp.wait_ge(made, 1)
                sp.dma_start(io["slots_in"][EXPERTS * REGION:SLOTS, :].rearrange("(n p) d -> p n d", p=P),
                             zeros[:, :].unsqueeze(1).to_broadcast([P, EXPERTS, D])).then_inc(spare_ok, 16)
                for i in range(2, BLOCKS):
                    sp.wait_ge(a_turn["ps_ok"], i - 1)
                    load(i)
                    if i == 3:
                        for name, w in (("w_in_e", k["we_in"]), ("w_swiglu_e", k["we_swiglu"])):
                            for e in range(EXPERTS):
                                sp.dma_start(w[:, e], io[name][e].rearrange("(c p) f -> p c f", p=P)
                                             ).then_inc(k["experts_in"], 16)
                sp.wait_ge(pad_ok, 1)
                for e in range(EXPERTS):
                    at = sp.value_load(end_row[0:1, e:e + 1], min_val=e * REGION, max_val=e * REGION + TOK)
                    sp.dma_start(io["slots_in"][bass.ds(at, P), :], zeros[:, :]).then_inc(pads_out, 16)
                sp.wait_ge(spare_ok, 16)
                sp.wait_ge(pads_out, 16 * EXPERTS)

            @block.gpsimd
            def _(pool):
                pool.memset(zeros[:, :], 0.0).then_inc(made, 1)
                pool.memset(lower[:, :, :], 1.0).then_inc(made, 1)
                pool.memset(higher[:, :, :], 1.0).then_inc(made, 1)
                pool.memset(before[:, :], 1.0).then_inc(made, 1)
                pool.memset(ones[:, :], 1.0).then_inc(made, 1)
                pool.iota(region_int[:, :], pattern=[[REGION, EXPERTS]], base=0, channel_multiplier=0).then_inc(made, 1)
                pool.iota(start_int[:, :], pattern=[[P, SLOT_TILES]], base=0,
                          channel_multiplier=0).then_inc(made, 1)
                pool.wait_ge(made, 7)
                pool.affine_select(out=lower[:, :, :], in_=lower[:, :, :], compare_op=ALU.is_gt, fill=0.0, base=0,
                                   pattern=[[1, EXPERTS], [-1, EXPERTS]], channel_multiplier=0).then_inc(made, 1)
                pool.affine_select(out=higher[:, :, :], in_=higher[:, :, :], compare_op=ALU.is_ge, fill=0.0, base=0,
                                   pattern=[[-1, EXPERTS], [1, EXPERTS]], channel_multiplier=0).then_inc(made, 1)
                pool.affine_select(out=before[:, :], in_=before[:, :], compare_op=ALU.is_gt, fill=0.0, base=0,
                                   pattern=[[1, P]], channel_multiplier=-1).then_inc(made, 1)

                def low(b, f):
                    pool.wait_ge(hi_ok, FC * b + f + 1)
                    pool.tensor_tensor(h_lo[:, f], h[:, f % 2], h_hi[:, f].bitcast(F32), ALU.subtract
                                       ).then_inc(lo_ok, 1)

                def scatter(b, s):
                    r, t = s % TOP_K, s // TOP_K
                    pool.wait_ge(scaled_ok, TOP_K * TB * b + s + 1)
                    pool.indirect_dma_start(
                        out=io["slots_in"],
                        out_offset=bass.IndirectOffsetOnAxis(ap=k["slot"][:, r, TB * b + t:TB * b + t + 1], axis=0),
                        in_=scaled[:, s, :], in_offset=None).then_inc(scattered, 16)

                EACH = TOP_K * TB // FC
                for b in range(BLOCKS + 1):
                    if b:
                        pool.wait_ge(place_step, PLACES * b)
                    for f in range(FC):
                        if b < BLOCKS:
                            low(b, f)
                        if b:
                            for s in range(EACH * f, EACH * f + EACH):
                                scatter(b - 1, s)
                pool.wait_ge(scattered, 16 * TOP_K * TILES)

            @block.scalar
            def _(act):
                def step(i, j, n):
                    if live(i - 1):
                        high_parts(act, x_turn, i - 1, lambda c: xT_hi[:, 1 - j, c])
                    if live(i + 1):
                        act.wait_ge(y_ok, 2 * i + 2)
                        high_parts(act, a_turn, i + 1, lambda c: aT_hi[:, c])
                    if live(i):
                        norm_root(act, norm, i, j)
                    if live(i - 1):
                        for f in range(FC):
                            at = FC * (i - 1) + f
                            act.wait_ge(mid_ok, at + 1)
                            wait_past(act, h_ok, at_least(at - 1))
                            act.activation(silu[:, f % 2], ps_m[:, :], ACT.Silu).then_inc(silu_ok, 1)
                            act.wait_ge(h_ok, at + 1)
                            act.activation(h_hi[:, f], h[:, f % 2], ACT.Copy).then_inc(hi_ok, 1)
                        act.wait_ge(rank_step, RANKS * i)
                        wait_past(act, scaled_ok, at_least(TOP_K * TB * (i - 1)))
                        act.activation(gate[:, :, :], score_of[:, :, :], ACT.Sigmoid).then_inc(gate_ok, 1)

                high_parts(act, a_turn, 0, lambda c: aT_hi[:, c])
                act.wait_ge(s_in, 48)
                for raw, hi in zip(s_raws, (wi_hi, wg_hi, wo_hi)):
                    act.activation(hi[:, :, :], raw, ACT.Copy).then_inc(s_high, 1)
                over_steps(act, step)

            @block.vector
            def _(dve):
                def a_low(i):
                    low_parts(dve, a_turn, i, lambda c: aT_lo[:, c], lambda c: aT_hi[:, c])

                def add_rows(i, sem, at, used):
                    for g in range(2):
                        dve.wait_ge(sem, at + g + 1)
                        x = k["X"][:, bass.ds(TB * i + 2 * g, 2), :]
                        dve.tensor_tensor(x, x, ps_y[:, 2 * g:2 * g + 2, :], ALU.add).then_inc(used, 1)

                def rank_block(b):
                    local = 0

                    def link(op):
                        nonlocal local
                        local += 1
                        op.then_inc(rank_step, 1)
                        dve.wait_ge(rank_step, RANKS * b + local)

                    dve.wait_ge(r_ok, b + 1)
                    link(dve.tensor_copy(score[:, :, :], ps_r[:, :, :]))
                    own = score[:, :, :].unsqueeze(3).to_broadcast(FULL)
                    rival = score[:, :, :].unsqueeze(2).to_broadcast(FULL)
                    dve.tensor_tensor(beats[:, :, :, :], rival, own, ALU.is_gt)
                    link(dve.tensor_tensor(ties[:, :, :, :], rival, own, ALU.is_ge))
                    dve.tensor_tensor(beats[:, :, :, :], beats[:, :, :, :],
                                      higher[:, :, :].unsqueeze(1).to_broadcast(FULL), ALU.mult)
                    link(dve.tensor_tensor(ties[:, :, :, :], ties[:, :, :, :],
                                           lower[:, :, :].unsqueeze(1).to_broadcast(FULL), ALU.mult))
                    link(dve.tensor_tensor(beats[:, :, :, :], beats[:, :, :, :], ties[:, :, :, :], ALU.add))
                    link(dve.tensor_reduce(rank[:, :, :], beats[:, :, :, :], AX.X, ALU.add))
                    wait_past(dve, counted, b)
                    link(dve.tensor_scalar(chosen[:, :, :], rank[:, :, :], float(TOP_K), None, ALU.is_lt))
                    for r in range(TOP_K):
                        link(dve.tensor_scalar(is_rank[:, r], rank[:, :, :], float(r), None, ALU.is_equal))
                    for r in range(TOP_K):
                        link(dve.tensor_tensor(picked[:, r], is_rank[:, r], score[:, :, :], ALU.mult))
                    wait_past(dve, gate_ok, b)
                    link(dve.tensor_reduce(score_of[:, :, :], picked[:, :, :, :], AX.X, ALU.add))
                    assert local == RANKS

                def place_block(b):
                    local = 0

                    def link(op):
                        nonlocal local
                        local += 1
                        op.then_inc(place_step, 1)
                        dve.wait_ge(place_step, PLACES * b + local)

                    dve.wait_ge(counted, b + 1)
                    link(dve.tensor_tensor(place[:, :, :], ps_b[:, 0:TB, :],
                                           base[:, :].unsqueeze(1).to_broadcast([P, TB, EXPERTS]), ALU.add))
                    link(dve.tensor_tensor(base[:, :], base[:, :], ps_b[:, TB, :], ALU.add))
                    for r in range(TOP_K):
                        link(dve.tensor_tensor(picked[:, r], is_rank[:, r], place[:, :, :], ALU.mult))
                    link(dve.tensor_reduce(place_of[:, :, :], picked[:, :, :, :], AX.X, ALU.add))
                    link(dve.tensor_copy(k["slot"][:, :, bass.ds(TB * b, TB)], place_of[:, :, :]))
                    assert local == PLACES

                def scale_rows(b, j):
                    dve.wait_ge(gate_ok, b + 1)
                    wait_past(dve, scattered, 16 * TOP_K * TB * b)
                    for s in range(TOP_K * TB):
                        r, t = s % TOP_K, s // TOP_K
                        dve.tensor_scalar(scaled[:, s, :], xn[:, j, t, :], gate[:, r, t:t + 1], None,
                                          ALU.mult).then_inc(scaled_ok, 1)

                table = 0

                def link(op):
                    nonlocal table
                    table += 1
                    op.then_inc(table_step, 1)
                    dve.wait_ge(table_step, table)

                def make_tables():
                    dve.tensor_copy(end_row[:, :], base[0:1, :]).then_inc(pad_ok, 1)
                    link(dve.tensor_tensor(count[:, :], base[:, :], region[:, :], ALU.subtract))
                    link(dve.tensor_scalar(padded[:, :], count[:, :], float(P - 1), None, ALU.add))
                    link(dve.tensor_scalar(padded[:, :], padded[:, :], -P, None, ALU.bitwise_and))
                    link(dve.tensor_copy(room[:, :], padded[:, :]))
                    link(dve.tensor_scalar(unused[:, :], room[:, :], -1.0, float(REGION), ALU.mult, ALU.add))
                    slots = k["slot"][:, :, :].rearrange("p r t -> p (r t)")
                    slot_shape = [P, TOP_K * TILES, EXPERTS - 1]
                    link(dve.tensor_copy(out_row[:, :], slots))
                    link(dve.tensor_tensor(moved[:, :, :], out_row[:, :].unsqueeze(2).to_broadcast(slot_shape),
                                           region[:, 1:EXPERTS].unsqueeze(1).to_broadcast(slot_shape), ALU.is_ge))
                    link(dve.tensor_tensor(moved[:, :, :], moved[:, :, :],
                                           unused[:, 0:EXPERTS - 1].unsqueeze(1).to_broadcast(slot_shape), ALU.mult))
                    link(dve.tensor_reduce(moved_sum[:, :], moved[:, :, :], AX.X, ALU.add))
                    link(dve.tensor_tensor(out_row[:, :], out_row[:, :], moved_sum[:, :], ALU.subtract))
                    link(dve.tensor_copy(k["out_slot"][:, :, :].rearrange("p r t -> p (r t)"), out_row[:, :]))
                    link(dve.tensor_tensor_scan(ends[:, :], room[:, :], zeros[:, 0:EXPERTS], 0.0, ALU.add, ALU.add))
                    dve.wait_ge(lo_ok, FC * BLOCKS)
                    table_shape = [1, SLOT_TILES, EXPERTS]
                    link(dve.tensor_tensor(passed_end[:, :, :], tile_start[:, :].unsqueeze(2).to_broadcast(table_shape),
                                           ends[0:1, :].unsqueeze(1).to_broadcast(table_shape), ALU.is_ge))
                    link(dve.tensor_reduce(expert[:, :], passed_end[:, :, :], AX.X, ALU.add))
                    link(dve.tensor_scalar(k["tile_expert"][:, :], expert[:, :], float(EXPERTS - 1), None, ALU.min))
                    link(dve.tensor_tensor(skipped[:, :, :], passed_end[:, :, :],
                                           unused[0:1, :].unsqueeze(1).to_broadcast(table_shape), ALU.mult))
                    link(dve.tensor_reduce(tile_row[:, :], skipped[:, :, :], AX.X, ALU.add))
                    link(dve.tensor_tensor(tile_row[:, :], tile_row[:, :], tile_start[:, :], ALU.add))
                    link(dve.tensor_scalar(k["tile_place"][:, :], tile_row[:, :], 1.0 / P, None, ALU.mult))

                def step(i, j, n):
                    if live(i - 1):
                        low_parts(dve, x_turn, i - 1, lambda c: xT_lo[:, 1 - j, c], lambda c: xT_hi[:, 1 - j, c])
                    if live(i):
                        add_rows(i, y_ok, 2 * i, added_ok)
                    if live(i + 1):
                        a_low(i + 1)
                    if live(i):
                        hold(dve, k, added_ok, 2 * i + 2)
                        norm_measure(dve, norm, i, j)
                    if live(i - 1):
                        rank_block(i - 1)
                    if live(i - 2):
                        scale_rows(i - 2, j)
                    if isinstance(i, int) and i == BLOCKS + 1:
                        make_tables()
                    if live(i - 2):
                        add_rows(i - 2, s_ok, 2 * (i - 2), s_used)
                    if live(i):
                        norm_apply(dve, norm, i, j, lambda t: xn[:, j, t:t + 1, :])
                    if live(i - 1):
                        for f in range(FC):
                            at = FC * (i - 1) + f
                            dve.wait_ge(silu_ok, at + 1)
                            dve.wait_ge(gated_ok, at + 1)
                            wait_past(dve, lo_ok, at_least(at - 1))
                            dve.tensor_tensor(h[:, f % 2], silu[:, f % 2], ps_g[:, :], ALU.mult).then_inc(h_ok, 1)
                            if f == 2:
                                place_block(i - 1)
                    if isinstance(i, int) and i == 0:
                        for n, (raw, hi, lo) in enumerate(zip(s_raws, (wi_hi, wg_hi, wo_hi), (wi_lo, wg_lo, wo_lo))):
                            dve.wait_ge(s_high, n + 1)
                            dve.tensor_tensor(lo[:, :, :], raw, hi[:, :, :].bitcast(F32), ALU.subtract
                                              ).then_inc(s_split, 1)

                dve.sem_inc(s_used, 2)
                dve.wait_ge(w_in, 32)
                split_weights(dve, w_raw[:, :, :], w_hi[:, :, :], w_lo[:, :, :], w_split, 0)
                split_weights(dve, r_raw[:, :, :], r_hi[:, :, :], r_lo[:, :, :], w_split, 2)
                a_low(0)
                dve.wait_ge(made, 10)
                dve.tensor_copy(region[:, :], region_int[:, :])
                dve.tensor_copy(base[:, :], region_int[:, :])
                link(dve.tensor_copy(tile_start[:, :], start_int[:, :]))
                over_steps(dve, step)

            @block.tensor
            def _(pe):
                def turn_a(i, j, n):
                    pe.wait_ge(rows_in[j], 16 * GROUPS * (n + 1))
                    wait_past(pe, x_turn["lo_ok"], at_least(DC * (i - 1)))
                    turn_block(pe, a_turn, i, lambda t, c: rows[:, j, t, 2 * c:2 * c + 2, :].rearrange("p g c -> p (g c)"))

                def project(i, j):
                    pe.wait_ge(a_turn["lo_ok"], DC * i + DC)
                    for g in range(2):
                        wait_past(pe, s_used, at_least(2 * (i - 3) + g + 1 + 2))
                        wait_past(pe, added_ok, at_least(2 * (i - 1) + g + 1))
                        for t in (2 * g, 2 * g + 1):
                            for d in range(DC):
                                o = t * P
                                last = mm3(pe, ps_y[:, t], (aT_hi[:, d, o:o + P], aT_lo[:, d, o:o + P]),
                                           (w_hi[:, d], w_lo[:, d]), d == 0, d == DC - 1)
                        last.then_inc(y_ok, 1)

                def turn_x(i, j):
                    pe.wait_ge(norm["xn_ok"], i + 1)
                    if live(i + 1):
                        pe.wait_ge(a_turn["lo_ok"], DC * (i + 1) + DC)
                    turn_block(pe, x_turn, i, lambda t, c: xn[:, j, t, c * P:(c + 1) * P])

                def scores(i, j):
                    pe.wait_ge(x_turn["lo_ok"], DC * i + DC)
                    wait_past(pe, rank_step, at_least(RANKS * (i - 1) + 1))
                    for t in range(TB):
                        for d in range(DC):
                            at = slice(t * P, (t + 1) * P)
                            last = mm3(pe, ps_r[:, t], (xT_hi[:, j, d, at], xT_lo[:, j, d, at]),
                                       (r_hi[:, d], r_lo[:, d]), d == 0, d == DC - 1)
                    last.then_inc(r_ok, 1)

                def count_rows(b):
                    pe.wait_ge(rank_step, RANKS * b + 6)
                    wait_past(pe, place_step, at_least(PLACES * (b - 1) + 2))
                    for t in range(TB + 1):
                        for u in range(min(t, TB - 1) + 1 if t < TB else TB):
                            last = pe.matmul(ps_b[:, t], before[:, :] if u == t else ones[:, :], chosen[:, u],
                                             start=(u == 0), stop=(u == min(t, TB - 1)))
                    last.then_inc(counted, 1)

                def expand(i, j, f):
                    at = FC * i + f
                    x = [(xT_hi[:, j, d], xT_lo[:, j, d]) for d in range(DC)]
                    for dst, hi, lo, used, sem in ((ps_m, wi_hi, wi_lo, silu_ok, mid_ok),
                                                   (ps_g, wg_hi, wg_lo, h_ok, gated_ok)):
                        wait_past(pe, used, at)
                        for d in range(DC):
                            last = mm3(pe, dst[:, :], (hi[:, d, f * P:(f + 1) * P], lo[:, d, f * P:(f + 1) * P]),
                                       x[d], d == 0, d == DC - 1)
                        last.then_inc(sem, 1)

                def contract(i):
                    pe.wait_ge(lo_ok, FC * i + FC)
                    for g in range(2):
                        if live(i + 2):
                            pe.wait_ge(added_ok, 2 * (i + 2) + g + 1)
                        else:
                            pe.wait_ge(s_used, 2 * (i - 1) + g + 1 + 2)
                        for t in (2 * g, 2 * g + 1):
                            for f in range(FC):
                                last = mm3(pe, ps_y[:, t], (h_hi[:, f, t * P:(t + 1) * P], h_lo[:, f, t * P:(t + 1) * P]),
                                           (wo_hi[:, f], wo_lo[:, f]), f == 0, f == FC - 1)
                        last.then_inc(s_ok, 1)

                def step(i, j, n):
                    if live(i - 1):
                        turn_x(i - 1, 1 - j)
                    if live(i):
                        project(i, j)
                    if live(i + 1):
                        turn_a(i + 1, 1 - j, n + j)
                    if live(i - 1):
                        scores(i - 1, 1 - j)
                    if live(i - 2):
                        contract(i - 2)
                    if live(i - 1):
                        if isinstance(i, int) and i == 1:
                            pe.wait_ge(s_split, 3)
                        for f in range(FC):
                            expand(i - 1, 1 - j, f)
                            if f == 2:
                                count_rows(i - 1)

                pe.wait_ge(w_split, 4)
                turn_a(0, 0, 0)
                over_steps(pe, step)


def phase_experts(k):
    nc, io = k["nc"], k["io"]
    with ExitStack() as mem:
        def sb(name, shape, dt):
            return mem.enter_context(nc.sbuf_tensor(name, shape, dt))

        def ps(name, shape, dt=F32):
            return mem.enter_context(nc.psum_tensor(name, shape, dt))

        wi, wg = k["we_in"], k["we_swiglu"]
        wo = sb("we_out", [P, EXPERTS, FC, D], F32)
        rows = sb("slot_rows", [P, 2, D], F32)
        xT = sb("slot_xT", [P, 2, DC, P], F32)
        silu = sb("slot_silu", [P, 2, FF], F32)
        h = sb("slot_h", [P, 2, FF], F32)
        hT = sb("slot_hT", [P, 2, FC, P], F32)
        y = sb("slot_y", [P, 2, D], F32)
        ps_x, ps_h, ps_y = ps("ps_xT", [P, DC, P]), ps("ps_hT", [P, FC, P]), ps("ps_slot_y", [P, D])
        ps_m, ps_g = ps("ps_slot_mid", [P, 2, FF]), ps("ps_slot_gated", [P, 2, FF])
        w_in = sem(k, "experts_w_in")
        rows_in, y_out = sems(k, "slot_rows_in", "even odd"), sems(k, "slot_y_out", "even odd")
        x_ok, xT_ok, mid_ok, gated_ok, silu_ok, h_ok, hps_ok, hT_ok, yps_ok, y_ok = sems(
            k, "slot", "x_ok xT_ok mid_ok gated_ok silu_ok h_ok hps_ok hT_ok yps_ok y_ok")

        with nc.Block() as block:

            @block.sync
            def _(sp):
                src = io["slots_in"].rearrange("(s p) d -> s p d", p=P)

                def load(i, j):
                    at = sp.value_load(k["tile_place"][0:1, bass.ds(i, 1)], min_val=0, max_val=SLOTS // P - 1)
                    sp.dma_start(rows[:, j, :], src[bass.ds(at, 1)].rearrange("o p d -> p (o d)")
                                 ).then_inc(rows_in[j], 16)

                load(0, 0)
                load(1, 1)
                for e in range(EXPERTS):
                    sp.dma_start(wo[:, e], io["w_out_e"][e].rearrange("(c p) f -> p c f", p=P)).then_inc(w_in, 16)
                with sp.Fori(0, SLOT_TILES // 2 - 1) as n:
                    for j in range(2):
                        hold(sp, k, x_ok, 2 * n + j + 1)
                        load(2 * n + j + 2, j)

            @block.gpsimd
            def _(pool):
                dst = io["slots_out"].rearrange("(s p) d -> s p d", p=P)

                def store(i, j, n):
                    hold(pool, k, y_ok, i + 1)
                    pool.dma_start(dst[bass.ds(i, 1)].rearrange("o p d -> p (o d)"), y[:, j, :]).then_inc(y_out[j], 16)

                with pool.Fori(0, SLOT_TILES // 2) as n:
                    for j in range(2):
                        store(2 * n + j, j, n)
                for j in range(2):
                    pool.wait_ge(y_out[j], 16 * (SLOT_TILES // 2))

            @block.scalar
            def _(act):
                def turned(i, j):
                    act.wait_ge(x_ok, i + 1)
                    act.activation(xT[:, j], ps_x[:, :, :], ACT.Copy).then_inc(xT_ok, 1)

                def result(i, j, n):
                    act.wait_ge(yps_ok, i + 1)
                    wait_past(act, y_out[j], 16 * n)
                    act.activation(y[:, j], ps_y[:, :], ACT.Copy).then_inc(y_ok, 1)

                def body(i, j, n):
                    act.wait_ge(mid_ok, i + 1)
                    wait_past(act, h_ok, at_least(i - 1))
                    act.activation(silu[:, j], ps_m[:, j], ACT.Silu).then_inc(silu_ok, 1)
                    if not is_last(i, SLOT_TILES):
                        turned(i + 1, 1 - j)
                    if not is_first(i):
                        result(i - 1, 1 - j, n - (1 - j))

                turned(0, 0)
                over_blocks(act, SLOT_TILES, body)
                result(SLOT_TILES - 1, 1, SLOT_TILES // 2 - 1)

            @block.vector
            def _(dve):
                def turned(i, j):
                    dve.wait_ge(hps_ok, i + 1)
                    wait_past(dve, yps_ok, at_least(i - 1))
                    dve.tensor_copy(hT[:, j], ps_h[:, :, :]).then_inc(hT_ok, 1)

                def body(i, j, n):
                    if not is_first(i):
                        turned(i - 1, 1 - j)
                    dve.wait_ge(silu_ok, i + 1)
                    dve.wait_ge(gated_ok, i + 1)
                    dve.tensor_tensor(h[:, j], silu[:, j], ps_g[:, j], ALU.mult).then_inc(h_ok, 1)

                over_blocks(dve, SLOT_TILES, body)
                turned(SLOT_TILES - 1, 1)

            @block.tensor
            def _(pe):
                def expert_of(i):
                    return pe.value_load(k["tile_expert"][0:1, bass.ds(i, 1)],
                                         min_val=0, max_val=EXPERTS - 1)

                def turn_x(i, j, n):
                    pe.wait_ge(rows_in[j], 16 * n + 16)
                    wait_past(pe, xT_ok, i)
                    for c in range(DC):
                        last = pe.transpose(ps_x[:, c], rows[:, j, c * P:(c + 1) * P], k["ident"][:, :])
                    last.then_inc(x_ok, 1)

                def expand(i, j, e, dst, w, sem):
                    for d in range(DC):
                        last = pe.matmul(dst[:, j], xT[:, j, d], w[:, bass.ds(e, 1), d, :],
                                         start=(d == 0), stop=(d == DC - 1))
                    last.then_inc(sem, 1)

                def turn_h(i, j):
                    pe.wait_ge(h_ok, i + 1)
                    wait_past(pe, hT_ok, i)
                    for f in range(FC):
                        last = pe.transpose(ps_h[:, f], h[:, j, f * P:(f + 1) * P], k["ident"][:, :])
                    last.then_inc(hps_ok, 1)

                def contract(i, j):
                    e = expert_of(i)
                    if is_first(i):
                        pe.wait_ge(w_in, 16 * EXPERTS)
                    pe.wait_ge(hT_ok, i + 1)
                    wait_past(pe, y_ok, i)
                    for f in range(FC):
                        last = pe.matmul(ps_y[:, :], hT[:, j, f], wo[:, bass.ds(e, 1), f, :],
                                         start=(f == 0), stop=(f == FC - 1))
                    last.then_inc(yps_ok, 1)

                def body(i, j, n):
                    e = expert_of(i)
                    pe.wait_ge(xT_ok, i + 1)
                    wait_past(pe, h_ok, at_least(i - 1))
                    expand(i, j, e, ps_m, wi, mid_ok)
                    if not is_first(i):
                        turn_h(i - 1, 1 - j)
                    expand(i, j, e, ps_g, wg, gated_ok)
                    if not is_last(i, SLOT_TILES):
                        turn_x(i + 1, 1 - j, n + j)
                    if not is_first(i):
                        contract(i - 1, 1 - j)

                pe.wait_ge(k["experts_in"], 16 * 2 * EXPERTS)
                turn_x(0, 0, 0)
                over_blocks(pe, SLOT_TILES, body)
                turn_h(SLOT_TILES - 1, 1)
                contract(SLOT_TILES - 1, 1)


SEQ_TILES = SEQ // P
SEQ_BLOCKS = SEQ // BT


def phase_keys(k, b):
    nc, io = k["nc"], k["io"]
    with ExitStack() as mem:
        def sb(name, shape, dt):
            return mem.enter_context(nc.sbuf_tensor(name + str(b), shape, dt))

        def ps(name, shape, dt=F32):
            return mem.enter_context(nc.psum_tensor(name + str(b), shape, dt))

        w_raw = sb("kv_raw", [P, DC, 2 * D], F32)
        w_hi, w_lo = sb("kv_hi", [P, DC, 2 * D], F32R), sb("kv_lo", [P, DC, 2 * D], F32R)
        back = None if b else sb("back", [P, 2, TOP_K, TB, D], F32)
        xn = sb("xn3", [P, 2, TB, D], F32)
        ps_t, ps_k, ps_v = ps("ps_x3", [P, DC, BT]), ps("ps_k3", [P, DC, BT]), ps("ps_v3", [P, TB, D])
        norm = layer_norm(k, mem, f"ln3_{b}")
        x_turn = turner(k, f"x3_turn{b}", ps_t)
        w_in, w_split, sum_ok, k_ok, k_hi, k_lo, v_ok, v_hi, v_lo = sems(k, 
            f"keys{b}", "w_in w_split sum_ok k_ok k_hi k_lo v_ok v_hi v_lo")
        back_in = sems(k, f"back_in{b}", "even odd")
        T0 = b * SEQ_TILES

        with nc.Block() as block:

            @block.sync
            def _(sp):
                sp.dma_start(w_raw[:, :, :], io["w_kv"].rearrange("(c p) n -> p c n", p=P)).then_inc(w_in, 16)

            @block.gpsimd
            def _(pool):
                def residual(i):
                    x = k["X"][:, T0 + TB * i:T0 + TB * i + TB, :]
                    pool.wait_ge(norm["xn_ok"], i + 1)
                    pool.tensor_tensor(x, x, xn[:, i % 2], ALU.add).then_inc(k["residual_ok"], 1)

                for i in range(SEQ_BLOCKS):
                    if b:
                        residual(i)
                        continue
                    if i >= 2:
                        pool.wait_ge(sum_ok, 2 * i - 2)
                    for r in range(TOP_K):
                        for t in range(TB):
                            T = T0 + TB * i + t
                            pool.indirect_dma_start(
                                out=back[:, i % 2, r, t, :], out_offset=None, in_=io["slots_out"],
                                in_offset=bass.IndirectOffsetOnAxis(ap=k["out_slot"][:, r, T:T + 1], axis=0)
                            ).then_inc(back_in[i % 2], 16)
                    if i:
                        residual(i - 1)
                if not b:
                    residual(SEQ_BLOCKS - 1)

            @block.scalar
            def _(act):
                norm_root(act, norm, 0, 0)
                for i in range(SEQ_BLOCKS):
                    high_parts(act, x_turn, i, lambda c: k["qT_hi"][:, c, i * BT:(i + 1) * BT])
                    if i + 1 < SEQ_BLOCKS:
                        norm_root(act, norm, i + 1, (i + 1) % 2)
                    for c in range(DC):
                        act.wait_ge(k_ok, DC * i + c + 1)
                        act.activation(k["kT_hi"][:, c, i * BT:(i + 1) * BT], ps_k[:, c], ACT.Copy).then_inc(k_hi, 1)
                    for g in range(2):
                        act.wait_ge(v_ok, 2 * i + g + 1)
                        t = TB * i + 2 * g
                        act.activation(k["v_hi"][:, t:t + 2, :], ps_v[:, 2 * g:2 * g + 2, :], ACT.Copy).then_inc(v_hi, 1)

            @block.vector
            def _(dve):
                def normed(i):
                    j = i % 2
                    x = k["X"][:, T0 + TB * i:T0 + TB * i + TB, :]
                    if not b:
                        dve.wait_ge(back_in[j], 16 * TOP_K * TB * (i // 2 + 1))
                        for r in range(TOP_K):
                            dve.tensor_tensor(x, x, back[:, j, r], ALU.add).then_inc(sum_ok, 1)
                            dve.wait_ge(sum_ok, 2 * i + r + 1)
                    if i >= 2:
                        dve.wait_ge(k["residual_ok"], SEQ_BLOCKS * b + i - 1)
                    norm_measure(dve, norm, i, j, T0)
                    norm_apply(dve, norm, i, j, lambda t: xn[:, j, t:t + 1, :], T0)

                def split():
                    dve.wait_ge(w_in, 16)
                    split_weights(dve, w_raw[:, :, :], w_hi[:, :, :], w_lo[:, :, :], w_split, 0)

                if not b:
                    split()
                normed(0)
                if b:
                    split()
                for i in range(SEQ_BLOCKS):
                    low_parts(dve, x_turn, i, lambda c: k["qT_lo"][:, c, i * BT:(i + 1) * BT],
                               lambda c: k["qT_hi"][:, c, i * BT:(i + 1) * BT])
                    if i + 1 < SEQ_BLOCKS:
                        normed(i + 1)
                    for c in range(DC):
                        dve.wait_ge(k_hi, DC * i + c + 1)
                        at = slice(i * BT, (i + 1) * BT)
                        dve.tensor_tensor(k["kT_lo"][:, c, at], ps_k[:, c], k["kT_hi"][:, c, at].bitcast(F32),
                                          ALU.subtract).then_inc(k_lo, 1)
                    for g in range(2):
                        dve.wait_ge(v_hi, 2 * i + g + 1)
                        t = TB * i + 2 * g
                        dve.tensor_tensor(k["v_lo"][:, t:t + 2, :], ps_v[:, 2 * g:2 * g + 2, :],
                                          k["v_hi"][:, t:t + 2, :].bitcast(F32), ALU.subtract).then_inc(v_lo, 1)

            @block.tensor
            def _(pe):
                pe.wait_ge(w_split, 2)
                for i in range(SEQ_BLOCKS):
                    j = i % 2
                    pe.wait_ge(norm["xn_ok"], i + 1)
                    turn_block(pe, x_turn, i, lambda t, c: xn[:, j, t, c * P:(c + 1) * P])
                    pe.wait_ge(x_turn["lo_ok"], DC * i + DC)
                    for c in range(DC):
                        wait_past(pe, k_lo, DC * (i - 1) + c + 1)
                        for d in range(DC):
                            at = slice(i * BT, (i + 1) * BT)
                            last = mm3(pe, ps_k[:, c], (w_hi[:, d, c * P:(c + 1) * P], w_lo[:, d, c * P:(c + 1) * P]),
                                       (k["qT_hi"][:, d, at], k["qT_lo"][:, d, at]), d == 0, d == DC - 1)
                        last.then_inc(k_ok, 1)
                    for g in range(2):
                        wait_past(pe, v_lo, 2 * (i - 1) + g + 1)
                        for t in (2 * g, 2 * g + 1):
                            for d in range(DC):
                                at = slice(i * BT + t * P, i * BT + (t + 1) * P)
                                last = mm3(pe, ps_v[:, t], (k["qT_hi"][:, d, at], k["qT_lo"][:, d, at]),
                                           (w_hi[:, d, D:2 * D], w_lo[:, d, D:2 * D]), d == 0, d == DC - 1)
                        last.then_inc(v_ok, 1)


def phase_attend(k, b):
    nc, io = k["nc"], k["io"]
    with ExitStack() as mem:
        def sb(name, shape, dt):
            return mem.enter_context(nc.sbuf_tensor(name + str(b), shape, dt))

        def ps(name, shape, dt=F32):
            return mem.enter_context(nc.psum_tensor(name + str(b), shape, dt))

        chunk_top = sb("chunk_max", [P, SEQ_TILES, SEQ_BLOCKS], F32)
        chunk_total = sb("chunk_sum", [P, SEQ_TILES, SEQ_BLOCKS], F32)
        top = sb("row_max", [P, SEQ_TILES], F32)
        neg_top = sb("neg_row_max", [P, SEQ_TILES], F32)
        total = sb("row_sum", [P, SEQ_TILES], F32)
        inv = sb("inv_row_sum", [P, SEQ_TILES], F32)
        probs = sb("probs3", [P, 2, SEQ], F32)
        pT_hi, pT_lo = sb("pT_hi", [P, 2, TB, P], F32R), sb("pT_lo", [P, 2, TB, P], F32R)
        back = None if b else sb("next_back", [P, TOP_K, SEQ_TILES, D], F32)
        ps_s, ps_t, ps_o = ps("ps_s3", [P, SEQ]), ps("ps_p3", [P, 2, TB, P]), ps("ps_o3", [P, 2, BT])
        s_ok, masked_ok, chunk_ok, top_ok, neg_ok, exp_ok = sems(
            k, f"attend{b}", "s_ok masked_ok chunk_ok top_ok neg_ok exp_ok")
        t_ok, hi_ok, lo_ok, pv_ok, total_ok, inv_ok, used_ok = sems(
            k, f"attend{b}", "t_ok hi_ok lo_ok pv_ok total_ok inv_ok used_ok")
        back_in, summed = sems(k, f"next_rows{b}", "back_in summed")
        T0 = b * SEQ_TILES
        PARTS = [(q, g, min(TB, q + 1 - g)) for q in range(SEQ_TILES) for g in range(0, q + 1, TB)]
        OF = [[n for n, part in enumerate(PARTS) if part[0] == q] for q in range(SEQ_TILES)]

        with nc.Block() as block:

            if not b:
                @block.gpsimd
                def _(pool):
                    for r in range(TOP_K):
                        for t in range(SEQ_TILES):
                            T = T0 + SEQ_TILES + t
                            pool.indirect_dma_start(
                                out=back[:, r, t, :], out_offset=None, in_=io["slots_out"],
                                in_offset=bass.IndirectOffsetOnAxis(ap=k["out_slot"][:, r, T:T + 1], axis=0)
                            ).then_inc(back_in, 16)
                    pool.wait_ge(back_in, 16 * TOP_K * SEQ_TILES)
                    for i in range(SEQ_BLOCKS):
                        x = k["X"][:, T0 + SEQ_TILES + TB * i:T0 + SEQ_TILES + TB * i + TB, :]
                        for r in range(TOP_K):
                            pool.tensor_tensor(x, x, back[:, r, TB * i:TB * i + TB, :], ALU.add).then_inc(summed, 1)
                            pool.wait_ge(summed, TOP_K * i + r + 1)

            @block.vector
            def _(dve):
                def soften(q):
                    for n in OF[q]:
                        _, g, m = PARTS[n]
                        dve.wait_ge(s_ok, n + 1)
                        if n == OF[q][-1]:
                            diag = ps_s[:, q * P:(q + 1) * P]
                            dve.tensor_tensor(diag, diag, k["causal"][:, :], ALU.add).then_inc(masked_ok, 1)
                            dve.wait_ge(masked_ok, q + 1)
                        dve.tensor_reduce(chunk_top[:, q, g // TB:g // TB + 1], ps_s[:, g * P:(g + m) * P], AX.X,
                                          ALU.max).then_inc(chunk_ok, 1)
                    dve.wait_ge(chunk_ok, OF[q][-1] + 1)
                    dve.tensor_reduce(top[:, q:q + 1], chunk_top[:, q, 0:len(OF[q])], AX.X, ALU.max).then_inc(top_ok, 1)
                    dve.wait_ge(top_ok, q + 1)
                    dve.tensor_scalar(neg_top[:, q:q + 1], top[:, q:q + 1], -1.0, None, ALU.mult).then_inc(neg_ok, 1)

                def lows(n):
                    dve.wait_ge(hi_ok, n + 1)
                    m = PARTS[n][2]
                    dve.tensor_tensor(pT_lo[:, n % 2, 0:m], ps_t[:, n % 2, 0:m], pT_hi[:, n % 2, 0:m].bitcast(F32),
                                      ALU.subtract).then_inc(lo_ok, 1)

                soften(0)
                for q in range(SEQ_TILES):
                    for n in OF[q][:2]:
                        lows(n)
                    if q + 1 < SEQ_TILES:
                        soften(q + 1)
                    for n in OF[q][2:]:
                        lows(n)
                    dve.wait_ge(exp_ok, OF[q][-1] + 1)
                    dve.tensor_reduce(total[:, q:q + 1], chunk_total[:, q, 0:len(OF[q])], AX.X, ALU.add
                                      ).then_inc(total_ok, 1)
                    dve.wait_ge(total_ok, q + 1)
                    dve.reciprocal(inv[:, q:q + 1], total[:, q:q + 1]).then_inc(inv_ok, 1)
                    dve.wait_ge(pv_ok, OF[q][-1] + 1)
                    dve.wait_ge(inv_ok, q + 1)
                    x = k["X"][:, T0 + q, :]
                    dve.scalar_tensor_tensor(out=x, in0=ps_o[:, q % 2, 0:D], scalar=inv[:, q:q + 1], in1=x,
                                             op0=ALU.mult, op1=ALU.add).then_inc(used_ok, 1)

            @block.scalar
            def _(act):
                def weigh(n):
                    q, g, m = PARTS[n]
                    if n == OF[q][0]:
                        act.wait_ge(neg_ok, q + 1)
                        if q >= 2:
                            act.wait_ge(t_ok, OF[q - 2][-1] + 1)
                    act.activation(probs[:, q % 2, g * P:(g + m) * P], ps_s[:, g * P:(g + m) * P], ACT.Exp,
                                   bias=neg_top[:, q:q + 1], accum_out=chunk_total[:, q, g // TB:g // TB + 1]
                                   ).then_inc(exp_ok, 1)

                def high(n):
                    m = PARTS[n][2]
                    act.wait_ge(t_ok, n + 1)
                    if n >= 2:
                        act.wait_ge(pv_ok, n - 1)
                    act.activation(pT_hi[:, n % 2, 0:m], ps_t[:, n % 2, 0:m], ACT.Copy).then_inc(hi_ok, 1)

                weigh(0)
                for q in range(SEQ_TILES):
                    following = list(OF[q + 1]) if q + 1 < SEQ_TILES else []
                    for n in OF[q][:2]:
                        high(n)
                    for at in range(max(len(following), len(OF[q]) - 2)):
                        if at < len(following):
                            weigh(following[at])
                        if at + 2 < len(OF[q]):
                            high(OF[q][at + 2])

            @block.tensor
            def _(pe):
                def score(q):
                    for n in OF[q]:
                        _, g, m = PARTS[n]
                        if q and n - OF[q][0] < len(OF[q - 1]):
                            pe.wait_ge(exp_ok, OF[q - 1][n - OF[q][0]] + 1)
                        for d in range(DC):
                            at = slice(q * P, (q + 1) * P)
                            to = slice(g * P, (g + m) * P)
                            last = mm3(pe, ps_s[:, to], (k["qT_hi"][:, d, at], k["qT_lo"][:, d, at]),
                                       (k["kT_hi"][:, d, to], k["kT_lo"][:, d, to]), d == 0, d == DC - 1)
                        last.then_inc(s_ok, 1)

                def turn(n):
                    q, g, m = PARTS[n]
                    pe.wait_ge(exp_ok, n + 1)
                    if n >= 2:
                        pe.wait_ge(lo_ok, n - 1)
                    for t in range(m):
                        last = pe.transpose(ps_t[:, n % 2, t], probs[:, q % 2, (g + t) * P:(g + t + 1) * P],
                                            k["ident"][:, :])
                    last.then_inc(t_ok, 1)

                def weigh(n):
                    q, g, m = PARTS[n]
                    pe.wait_ge(lo_ok, n + 1)
                    if g == 0 and q >= 2:
                        pe.wait_ge(used_ok, q - 1)
                    for t in range(m):
                        last = mm3(pe, ps_o[:, q % 2, 0:D], (pT_hi[:, n % 2, t], pT_lo[:, n % 2, t]),
                                   (k["v_hi"][:, g + t], k["v_lo"][:, g + t]), g + t == 0, g + t == q)
                    last.then_inc(pv_ok, 1)

                score(0)
                for q in range(SEQ_TILES):
                    for n in OF[q][:2]:
                        turn(n)
                    if q + 1 < SEQ_TILES:
                        score(q + 1)
                    for n in OF[q]:
                        weigh(n)
                        if n + 2 in OF[q]:
                            turn(n + 2)


def phase_mlp(k):
    nc, io = k["nc"], k["io"]
    F4 = 4 * D
    FC4 = F4 // P
    with ExitStack() as mem:
        def sb(name, shape, dt):
            return mem.enter_context(nc.sbuf_tensor(name, shape, dt))

        def ps(name, shape, dt=F32):
            return mem.enter_context(nc.psum_tensor(name, shape, dt))

        raw = [sb("w1_raw", [P, DC, F4], F32), sb("w2_raw", [P, FC4, D], F32)]
        w1, w2 = sb("w1_ternary", [P, DC, F4], F32R), sb("w2_ternary", [P, FC4, D], F32R)
        below = sb("below", [P, 2 * F4], F32)
        size = sb("abs_sum", [P, 2], F32)
        gamma, half = sb("gamma", [P, 2], F32), sb("half_gamma", [P, 2, 2], F32)
        ones = sb("ones_f32", [P, P], F32)
        b1 = sb("b1_columns", [P, FC4], F32)
        b2 = sb("b2_rows", [P, D], F32)
        xn = sb("xn4", [P, 2, TB, D], F32)
        xT_hi, xT_lo = sb("x4T_hi", [P, 2, DC, BT], F32R), sb("x4T_lo", [P, 2, DC, BT], F32R)
        h = sb("h4", [P, 2, BT], F32)
        h_hi, h_lo = sb("h4_hi", [P, 2, FC4, BT], F32R), sb("h4_lo", [P, 2, FC4, BT], F32R)
        y = sb("y4", [P, 2, TB, D], F32)
        ps_t, ps_h, ps_y = ps("ps_x4", [P, DC, BT]), ps("ps_h4", [P, 3, BT]), ps("ps_y4", [P, TB, D])
        ps_g = ps("ps_gamma", [P, 2])
        norm = layer_norm(k, mem, "ln4")
        x_turn = turner(k, "x4_turn", ps_t)
        w_in, b_in, made, q_step, summed, res_ok = sems(k, "mlp", "w_in b_in made q_step summed res_ok")
        hps_ok, hi_ok, h_ok, lo_ok, yps_ok, y_ok = sems(k, "mlp", "hps_ok hi_ok h_ok lo_ok yps_ok y_ok")
        y_out = sems(k, "y_out", "even odd")

        with nc.Block() as block:

            @block.sync
            def _(sp):
                sp.dma_start(raw[0][:, :, :], io["w1"].rearrange("(c p) n -> p c n", p=P)).then_inc(w_in, 16)
                sp.dma_start(raw[1][:, :, :], io["w2"].rearrange("(c p) n -> p c n", p=P)).then_inc(w_in, 16)
                sp.dma_start(b1[:, :], io["b1"]).then_inc(b_in, 16)
                sp.dma_start(b2[:, :], io["b2"].to_broadcast([P, D])).then_inc(b_in, 16)
                out = io["out"].rearrange("(n p) d -> p n d", p=P)
                for i in range(BLOCKS):
                    sp.wait_ge(y_ok, 2 * i + 2)
                    sp.dma_start(out[:, TB * i:TB * i + TB, :], y[:, i % 2]).then_inc(y_out[i % 2], 16)
                for j in range(2):
                    sp.wait_ge(y_out[j], 16 * (BLOCKS // 2))

            @block.gpsimd
            def _(pool):
                pool.memset(ones[:, :], 1.0).then_inc(made, 1)

                def body(i, j, n):
                    for f in range(FC4):
                        at = FC4 * i + f
                        pool.wait_ge(h_ok, at + 1)
                        pool.tensor_tensor(h_lo[:, j, f], h[:, f % 2], h_hi[:, j, f].bitcast(F32), ALU.subtract
                                           ).then_inc(lo_ok, 1)

                over_blocks(pool, BLOCKS, body)

            @block.scalar
            def _(act):
                act.wait_ge(b_in, 32)
                norm_root(act, norm, 0, 0)
                high_parts(act, x_turn, 0, lambda c: xT_hi[:, 0, c])

                def body(i, j, n):
                    if not is_last(i, BLOCKS):
                        norm_root(act, norm, i + 1, 1 - j)
                    wait_past(act, yps_ok, at_least(2 * (i - 1)))
                    for f in range(FC4):
                        act.wait_ge(hps_ok, FC4 * i + f + 1)
                        act.activation(h_hi[:, j, f], ps_h[:, f % 3], ACT.Relu, bias=b1[:, f:f + 1]).then_inc(hi_ok, 1)
                        if f == 6 and not is_last(i, BLOCKS):
                            high_parts(act, x_turn, i + 1, lambda c: xT_hi[:, 1 - j, c])

                over_blocks(act, BLOCKS, body)

            @block.vector
            def _(dve):
                step = 0

                def link(op):
                    nonlocal step
                    step += 1
                    op.then_inc(q_step, 1)
                    dve.wait_ge(q_step, step)

                norm_measure(dve, norm, 0, 0)
                dve.wait_ge(w_in, 32)
                for m in range(2):
                    op = dve.tensor_reduce(size[:, m:m + 1], raw[m][:, :, :], AX.XY, ALU.add, apply_absolute_value=True)
                link(op)
                k["size_at"] = step
                norm_apply(dve, norm, 0, 0, lambda t: xn[:, 0, t:t + 1, :])
                dve.wait_ge(summed, 1)
                link(dve.tensor_scalar(gamma[:, :], ps_g[:, :], 1.0 / (D * F4), EPS, ALU.mult, ALU.add))
                link(dve.tensor_scalar(half[:, 0, :], gamma[:, :], 0.5, None, ALU.mult))
                link(dve.tensor_scalar(half[:, 1, :], gamma[:, :], -0.5, None, ALU.mult))
                for m, w in enumerate((w1, w2)):
                    flat = raw[m][:, :, :].rearrange("p c n -> p (c n)")
                    link(dve.tensor_scalar(below[:, :], flat, half[:, 1, m:m + 1], None, ALU.is_lt))
                    link(dve.scalar_tensor_tensor(out=w[:, :, :].rearrange("p c n -> p (c n)"), in0=flat,
                                                  scalar=half[:, 0, m:m + 1], in1=below[:, :],
                                                  op0=ALU.is_gt, op1=ALU.subtract))
                k["ternary_at"] = step

                def x_low(i, j):
                    low_parts(dve, x_turn, i, lambda c: xT_lo[:, j, c], lambda c: xT_hi[:, j, c])

                def result(i, j, n, g):
                    if g == 0:
                        wait_past(dve, y_out[j], 16 * n)
                    dve.wait_ge(res_ok, i + 1)
                    dve.wait_ge(yps_ok, 2 * i + g + 1)
                    dve.tensor_tensor(y[:, j, 2 * g:2 * g + 2], ps_y[:, 2 * g:2 * g + 2],
                                      k["X"][:, bass.ds(TB * i + 2 * g, 2), :], ALU.add).then_inc(y_ok, 1)

                def body(i, j, n):
                    if not is_last(i, BLOCKS):
                        norm_measure(dve, norm, i + 1, 1 - j)
                    for f in range(FC4):
                        at = FC4 * i + f
                        dve.wait_ge(hi_ok, at + 1)
                        wait_past(dve, lo_ok, at - 1)
                        dve.tensor_scalar(h[:, f % 2], ps_h[:, f % 3], b1[:, f:f + 1], 0.0, ALU.add, ALU.max
                                          ).then_inc(h_ok, 1)
                        if f == 1:
                            x = k["X"][:, bass.ds(TB * i, TB), :]
                            dve.tensor_tensor(x, x, b2[:, :].unsqueeze(1).to_broadcast([P, TB, D]), ALU.add
                                              ).then_inc(res_ok, 1)
                        if f == 3 and not is_last(i, BLOCKS):
                            norm_apply(dve, norm, i + 1, 1 - j, lambda t: xn[:, 1 - j, t:t + 1, :])
                        if f == 5 and not is_first(i):
                            result(i - 1, 1 - j, n - (1 - j), 0)
                        if f == 6 and not is_last(i, BLOCKS):
                            x_low(i + 1, 1 - j)
                    if not is_first(i):
                        result(i - 1, 1 - j, n - (1 - j), 1)

                x_low(0, 0)
                over_blocks(dve, BLOCKS, body)
                for g in range(2):
                    result(BLOCKS - 1, 1, BLOCKS // 2 - 1, g)

            @block.tensor
            def _(pe):
                pe.wait_ge(made, 1)
                pe.wait_ge(q_step, k["size_at"])
                pe.matmul(ps_g[:, :], ones[:, :], size[:, :], start=True, stop=True).then_inc(summed, 1)

                def turn(i, j):
                    pe.wait_ge(norm["xn_ok"], i + 1)
                    turn_block(pe, x_turn, i, lambda t, c: xn[:, j, t, c * P:(c + 1) * P])

                def contract(i, j, part):
                    t, half = part // 2, part % 2
                    if t % 2 == 0 and half == 0:
                        wait_past(pe, y_ok, at_least(2 * (i - 1) + t // 2 + 1))
                    for f in range(half * FC4 // 2, (half + 1) * FC4 // 2):
                        if part == 0 or t == 0:
                            pe.wait_ge(lo_ok, FC4 * i + f + 1)
                        pe.matmul(ps_y[:, t], h_hi[:, j, f, t * P:(t + 1) * P], w2[:, f], start=(f == 0), stop=False)
                        last = pe.matmul(ps_y[:, t], h_lo[:, j, f, t * P:(t + 1) * P], w2[:, f], start=False,
                                         stop=(f == FC4 - 1))
                    if t % 2 and half:
                        last.then_inc(yps_ok, 1)

                def body(i, j, n):
                    pe.wait_ge(x_turn["lo_ok"], DC * i + DC)
                    for f in range(FC4):
                        wait_past(pe, h_ok, FC4 * i + f - (1 if f < 2 else 2))
                        for d in range(DC):
                            w = w1[:, d, f * P:(f + 1) * P]
                            pe.matmul(ps_h[:, f % 3], w, xT_hi[:, j, d], start=(d == 0), stop=False)
                            last = pe.matmul(ps_h[:, f % 3], w, xT_lo[:, j, d], start=False, stop=(d == DC - 1))
                        last.then_inc(hps_ok, 1)
                        if not is_first(i):
                            contract(i - 1, 1 - j, f)
                        if f == 5 and not is_last(i, BLOCKS):
                            turn(i + 1, 1 - j)

                turn(0, 0)
                pe.wait_ge(q_step, k["ternary_at"])
                over_blocks(pe, BLOCKS, body)
                for part in range(2 * TB):
                    contract(BLOCKS - 1, 1, part)


def program(nc, io):
    io = dict(io)

    def scratch(name, shape, dt):
        return nc.dram_tensor(name, shape, dt, kind="Internal").ap()

    io["qk"] = scratch("qk_parts", (2, 3, GROUPS, BATCH, HG * DH, SEQ), BF16)
    io["shift"] = scratch("shift_parts", (3, GROUPS, BATCH, HG, SEQ), BF16)
    io["attended"] = scratch("attended", (GROUPS, BATCH, SEQ, HG * DH), F32)
    io["slots_in"] = scratch("slots_in", (SLOTS, D), F32)
    io["slots_out"] = scratch("slots_out", (OUT_SLOTS, D), F32)
    with ExitStack() as ctx:
        k = {"nc": nc, "io": io}
        k["passed"], k["residual_ok"] = (ctx.enter_context(nc.semaphore(name)) for name in ("passed", "residual_ok"))
        k["X"] = ctx.enter_context(nc.sbuf_tensor("X", [P, TILES, D], F32))
        k["ident"] = ctx.enter_context(nc.sbuf_tensor("ident", [P, P], F32))
        k["causal"] = ctx.enter_context(nc.sbuf_tensor("causal", [P, P], F32))
        k["head_sel"] = ctx.enter_context(nc.sbuf_tensor("head_sel", [P, P // DH], BF16))
        k["eps"] = ctx.enter_context(nc.sbuf_tensor("eps", [P, 1], F32))
        k["unsafe"] = ctx.enter_context(nc.sbuf_tensor("unsafe", [1, 1], I32))
        k["slot"] = ctx.enter_context(nc.sbuf_tensor("slot", [P, TOP_K, TILES], I32))
        k["out_slot"] = ctx.enter_context(nc.sbuf_tensor("out_slot", [P, TOP_K, TILES], I32))
        k["tile_expert"] = ctx.enter_context(nc.sbuf_tensor("tile_expert", [1, SLOT_TILES], I32))
        k["tile_place"] = ctx.enter_context(nc.sbuf_tensor("tile_place", [1, SLOT_TILES], I32))
        with ExitStack() as mem, semaphores(k):
            k["V"] = mem.enter_context(nc.sbuf_tensor("V", [P, GROUPS, TILES, HG, DH + 1], F32))
            phase_constants(k)
            phase_qkv(k)
            phase_shift(k)
            phase_attention(k)
        with ExitStack() as mem, semaphores(k):
            k["we_in"] = mem.enter_context(nc.sbuf_tensor("we_in", [P, EXPERTS, DC, FF], F32))
            k["we_swiglu"] = mem.enter_context(nc.sbuf_tensor("we_swiglu", [P, EXPERTS, DC, FF], F32))
            k["experts_in"] = sem(k, "experts_in")
            phase_tokens(k)
            phase_experts(k)
        for b in range(BATCH):
            with ExitStack() as mem, semaphores(k):
                def sb(name, shape):
                    return mem.enter_context(nc.sbuf_tensor(name + str(b), shape, F32R))

                k["qT_hi"], k["qT_lo"] = sb("q3T_hi", [P, DC, SEQ]), sb("q3T_lo", [P, DC, SEQ])
                k["kT_hi"], k["kT_lo"] = sb("k3T_hi", [P, DC, SEQ]), sb("k3T_lo", [P, DC, SEQ])
                k["v_hi"], k["v_lo"] = sb("v3_hi", [P, SEQ_TILES, D]), sb("v3_lo", [P, SEQ_TILES, D])
                phase_keys(k, b)
                phase_attend(k, b)
        with semaphores(k):
            phase_mlp(k)


def kernel(**inputs):
    import numpy as np
    import concourse.bacc as bacc
    from concourse.bass_utils import run_bass_kernel_spmd

    given = {name: np.asarray(a) for name, a in inputs.items()}
    arrays = {
        "x": given["L0_attn_in_features"].reshape(TOK, D),
        "wq": given["L0_attn_q_proj_weight"].T, "wk": given["L0_attn_k_proj_weight"].T,
        "wv": given["L0_attn_v_proj_weight"].T, "wo": given["L0_attn_o_proj_weight"].T,
        "router": given["L0_ffn_router_DE"],
        "w_in_shared": given["L0_ffn_w_in_shared_FD"].T, "w_swiglu": given["L0_ffn_w_swiglu_FD"].T,
        "w_out_shared": given["L0_ffn_w_out_shared_DF"].T,
        "w_in_e": given["L0_ffn_w_in_eDF"], "w_swiglu_e": given["L0_ffn_w_swiglu_eDF"],
        "w_out_e": given["L0_ffn_w_out_eFD"],
        "w_kv": given["L1_attn_W"].T,
        "w1": given["L1_ffn_W1"].T, "b1": given["L1_ffn_b1"].reshape(-1, P).T,
        "w2": given["L1_ffn_W2"].T, "b2": given["L1_ffn_b2"].reshape(1, D),
    }
    arrays = {name: np.ascontiguousarray(a) for name, a in arrays.items()}
    nc = bacc.Bacc("TRN2", target_bir_lowering=False, num_devices=1)
    io = {name: nc.dram_tensor(name, a.shape, mybir.dt.from_np(a.dtype), kind="ExternalInput").ap()
          for name, a in arrays.items()}
    io["out"] = nc.dram_tensor("out", (TOK, D), F32, kind="ExternalOutput").ap()
    program(nc, io)
    result = run_bass_kernel_spmd(nc, [arrays], core_ids=[0])
    return result.results[0]["out"].reshape(BATCH, SEQ, D)
```

```python
from contextlib import ExitStack, contextmanager

import concourse.bass as bass
from concourse import mybir

F32 = mybir.dt.float32
F32R = mybir.dt.float32r
BF16 = mybir.dt.bfloat16
I32 = mybir.dt.int32
ALU = mybir.AluOpType
ACT = mybir.ActivationFunctionType
AX = mybir.AxisListType

P = 128
BATCH, SEQ, D = 2, 2048, 256
TOK = BATCH * SEQ
DC = D // P
TILES = TOK // P
TB = 4
BT = TB * P
BLOCKS = TOK // BT
HEADS, DH = 16, D // 16
HG = 4
GROUPS = HEADS // HG
EPS = 1e-5
SHIFT_ROWS = 6 * DH
KROWS = SHIFT_ROWS + 3
UNITS = GROUPS * BATCH
Q_SLOTS, K_SLOTS = (0, 0, 1, 1, 0, 2), (0, 1, 0, 1, 2, 0)
SAFE_SQUARE = 48.0 ** 2


EXPERTS, TOP_K, FF = 8, 2, 512
FC = FF // P
D_FF = 4 * D
SLOT_TILES = TOP_K * TOK // P + EXPERTS
REGION = TOK + P
SLOTS = EXPERTS * REGION + EXPERTS * P
OUT_SLOTS = SLOT_TILES * P


def sem(k, name):
    handle = k["sem_ctx"].enter_context(k["nc"].semaphore(name))
    k["used"].append(handle)
    return handle


def sems(k, stem, names):
    return [sem(k, f"{stem}_{n}") for n in names.split()]


@contextmanager
def semaphores(k):
    with ExitStack() as k["sem_ctx"]:
        k["used"] = []
        yield
        with k["nc"].Block() as block:

            @block.gpsimd
            def _(pool):
                for handle in k["used"]:
                    pool.sem_clear(handle)


def wait_past(eng, sem, value):
    if not isinstance(value, int) or value > 0:
        eng.wait_ge(sem, value)


def hold(eng, k, sem, value):
    eng.wait_ge(sem, value)
    eng.sem_inc(k["passed"], 1)


def is_first(i):
    return isinstance(i, int) and i == 0


def is_last(i, count):
    return isinstance(i, int) and i == count - 1


def at_least(value):
    return max(value, 0) if isinstance(value, int) else value


def over_blocks(eng, count, body):
    for j in range(2):
        body(j, j, 0)
    if count > 4:
        with eng.Fori(1, count // 2 - 1) as n:
            for j in range(2):
                body(2 * n + j, j, n)
    for j in range(2):
        body(count - 2 + j, j, count // 2 - 1)


def mm3(pe, out, lhs, rhs, start, stop):
    (lh, ll), (rh, rl) = lhs, rhs
    pe.matmul(out, lh, rh, start=start, stop=False)
    pe.matmul(out, lh, rl, start=False, stop=False)
    return pe.matmul(out, ll, rh, start=False, stop=stop)


def turner(k, stem, ps):
    ps_ok, hi_ok, lo_ok = sems(k, stem, "ps_ok hi_ok lo_ok")
    return {"ps": ps, "ident": k["ident"], "ps_ok": ps_ok, "hi_ok": hi_ok, "lo_ok": lo_ok}


def turn_block(pe, w, i, rows):
    wait_past(pe, w["lo_ok"], DC * i)
    for t in range(TB):
        for c in range(DC):
            last = pe.transpose(w["ps"][:, c, t * P:(t + 1) * P], rows(t, c), w["ident"][:, :])
    last.then_inc(w["ps_ok"], 1)


def high_parts(act, w, i, out):
    act.wait_ge(w["ps_ok"], i + 1)
    for c in range(DC):
        act.activation(out(c), w["ps"][:, c], ACT.Copy).then_inc(w["hi_ok"], 1)


def low_parts(dve, w, i, out, high):
    for c in range(DC):
        dve.wait_ge(w["hi_ok"], DC * i + c + 1)
        dve.tensor_tensor(out(c), w["ps"][:, c], high(c).bitcast(F32), ALU.subtract).then_inc(w["lo_ok"], 1)


def split_weights(dve, raw, hi, lo, sem, at):
    dve.tensor_copy(hi, raw).then_inc(sem, 1)
    dve.wait_ge(sem, at + 1)
    dve.tensor_tensor(lo, raw, hi.bitcast(F32), ALU.subtract).then_inc(sem, 1)


def phase_constants(k):
    nc = k["nc"]
    made, picked = sems(k, "constants", "made picked")
    with nc.Block() as block:

        @block.gpsimd
        def _(pool):
            pool.memset(k["ident"][:, :], 0.0).then_inc(made, 1)
            pool.memset(k["head_sel"][:, :], 1.0).then_inc(made, 1)
            pool.memset(k["eps"][:, :], EPS).then_inc(made, 1)
            pool.memset(k["causal"][:, :], 0.0).then_inc(made, 1)
            pool.memset(k["V"][:, :, :, :, DH:DH + 1], 1.0).then_inc(made, 1)
            pool.wait_ge(made, 5)
            pool.affine_select(out=k["causal"][:, :], in_=k["causal"][:, :], compare_op=ALU.is_ge, fill=-3.0e38,
                               base=0, pattern=[[-1, P]], channel_multiplier=1).then_inc(picked, 1)
            pool.affine_select(out=k["ident"][:, :], in_=k["ident"][:, :], compare_op=ALU.not_equal, fill=1.0,
                               base=0, pattern=[[-1, P]], channel_multiplier=1).then_inc(picked, 1)
            pool.affine_select(out=k["head_sel"][:, :], in_=k["head_sel"][:, :], compare_op=ALU.is_ge, fill=0.0,
                               base=0, pattern=[[-DH, P // DH]], channel_multiplier=1).then_inc(picked, 1)
            pool.wait_ge(picked, 3)
            pool.affine_select(out=k["head_sel"][:, :], in_=k["head_sel"][:, :], compare_op=ALU.is_ge, fill=0.0,
                               base=DH - 1, pattern=[[DH, P // DH]], channel_multiplier=-1).then_inc(picked, 1)


def layer_norm(k, mem, stem):
    nc = k["nc"]
    norm = {"X": k["X"], "eps": k["eps"], "k": k}
    for name, shape in (("stats", [P, 2, TB, 6]), ("moments", [P, 2, TB, 2]), ("std", [P, 2, TB]), ("rstd", [P, 2, TB])):
        norm[name] = mem.enter_context(nc.sbuf_tensor(f"{stem}_{name}", shape, F32))
    for name in ("stats_ok", "moments_ok", "std_ok", "rstd_ok", "xn_ok"):
        norm[name] = sem(k, f"{stem}_{name}")
    return norm


def norm_measure(dve, w, b, j, first=0):
    for t in range(TB):
        dve.bn_stats(w["stats"][:, j, t, :], w["X"][:, bass.ds(first + TB * b + t, 1), :]).then_inc(w["stats_ok"], 1)
    hold(dve, w["k"], w["stats_ok"], TB * b + TB)
    for t in range(TB):
        dve.bn_aggr(w["moments"][:, j, t, :], w["stats"][:, j, t, :]).then_inc(w["moments_ok"], 1)


def norm_root(act, w, b, j):
    act.wait_ge(w["moments_ok"], TB * b + TB)
    act.activation(w["std"][:, j], w["moments"][:, j, :, 1], ACT.Sqrt, bias=w["eps"][:, 0:1]).then_inc(w["std_ok"], 1)


def norm_apply(dve, w, b, j, out, first=0):
    dve.wait_ge(w["std_ok"], b + 1)
    dve.reciprocal(w["rstd"][:, j], w["std"][:, j]).then_inc(w["rstd_ok"], 1)
    dve.wait_ge(w["rstd_ok"], b + 1)
    for t in range(TB):
        last = dve.tensor_scalar(out(t), w["X"][:, bass.ds(first + TB * b + t, 1), :], w["moments"][:, j, t, 0:1],
                                 w["rstd"][:, j, t:t + 1], ALU.subtract, ALU.mult)
    last.then_inc(w["xn_ok"], 1)


def phase_qkv(k):
    nc, io = k["nc"], k["io"]
    with ExitStack() as mem:
        def sb(name, shape, dt):
            return mem.enter_context(nc.sbuf_tensor(name, shape, dt))

        def ps(name, shape, dt=F32):
            return mem.enter_context(nc.psum_tensor(name, shape, dt))

        w_raw = sb("w_raw", [P, 3, DC, D], F32)
        w_hi = sb("w_hi", [P, 3, DC, D], F32R)
        w_lo = sb("w_lo", [P, 3, DC, D], F32R)
        xn = sb("xn1", [P, 2, TB, D], F32)
        xnT_hi = sb("xn1T_hi", [P, 2, DC, BT], F32R)
        xnT_lo = sb("xn1T_lo", [P, 2, DC, BT], F32R)
        part1 = sb("part1", [P, 2, 4, BT], BF16)
        part2 = sb("part2", [P, 2, 4, BT], BF16)
        part3 = sb("part3", [P, 2, 4, BT], BF16)
        rest = sb("rest", [P, 2, 4, BT], F32)
        square = sb("square", [P, 2, 4, BT], BF16)
        norm_max = sb("norm_max", [P, BLOCKS], F32)
        norm_top = sb("norm_top", [P, 1], F32)
        norm_row = sb("norm_row", [1, P], F32)
        over = sb("over", [1, 2, 8], F32)
        zeros = sb("shift_zeros", [P, HEADS * TOK * 3 // P], BF16)
        ps_t = ps("ps_t", [P, DC, BT])
        ps_qk = ps("ps_qk", [P, 4, BT])
        ps_v = ps("ps_v", [P, 2, D])
        ps_n = ps("ps_n", [P, BT])
        norm = layer_norm(k, mem, "ln1")

        w_in, w_split, zero_ok, zero_out = sems(k, "qkv", "w_in w_split zero_ok zero_out")
        x_in = sems(k, "x_in", "even odd")
        parts_out = sems(k, "parts_out", "even odd")
        t_ok, t_hi_ok, t_lo_ok = sems(k, "qkv", "t_ok t_hi_ok t_lo_ok")
        qk_ok, part1_ok, rest_ok, part2_ok, part3_ok = sems(k, "qkv", "qk_ok part1_ok rest_ok part2_ok part3_ok")
        v_ok, v_used, n_ok, n_used, top_ok, topT_ok, row_ok = sems(
            k, "qkv", "v_ok v_used n_ok n_used top_ok topT_ok row_ok")

        x_view = io["x"].rearrange("(n p) d -> p n d", p=P)
        with nc.Block() as block:

            @block.sync
            def _(sp):
                sp.dma_start(k["X"][:, 0:TB, :], x_view[:, 0:TB, :]).then_inc(x_in[0], 16)
                for n, name in enumerate("qkv"):
                    sp.dma_start(w_raw[:, n], io["w" + name].rearrange("(c p) n -> p c n", p=P)).then_inc(w_in, 16)
                for b in range(1, BLOCKS):
                    wait_past(sp, x_in[b % 2], 16 * (b // 2))
                    sp.dma_start(k["X"][:, b * TB:(b + 1) * TB, :],
                                 x_view[:, b * TB:(b + 1) * TB, :]).then_inc(x_in[b % 2], 16)
                sp.wait_ge(zero_ok, 1)
                sp.dma_start(io["shift"].rearrange("m g b h t -> (m g b h t)").rearrange("(p n) -> p n", p=P),
                             zeros[:, :]).then_inc(zero_out, 16)
                for b in range(BLOCKS):
                    j = b % 2
                    t0 = b * BT % SEQ
                    if b == SEQ // BT + 2:
                        for parity in range(2):
                            sp.wait_ge(parts_out[parity], 48 * (SEQ // BT // 2))
                        load_stacks(sp, io, 0, 0, k["first_stacks"][0], k["first_stacks"][1], k["loaded"][0])
                    for n, (part, done) in enumerate(((part1, part1_ok), (part2, part2_ok), (part3, part3_ok))):
                        sp.wait_ge(done, 4 * b + 4 if n == 0 else b + 1)
                        to = io["qk"][n, b * BT // SEQ, :, :, :, t0:t0 + BT].rearrange("m (c g) r t -> (g r) (m c) t", c=DC)
                        sp.dma_start(to, part[:, j]).then_inc(parts_out[j], 16)
                for j in range(2):
                    sp.wait_ge(parts_out[j], 48 * (BLOCKS // 2))
                sp.wait_ge(k["loaded"][0], 16 * (len(Q_SLOTS) + len(K_SLOTS)))
                sp.wait_ge(zero_out, 16)

            @block.gpsimd
            def _(pool):
                pool.memset(zeros[:, :].bitcast(I32), 0).then_inc(zero_ok, 1)
                pool.wait_ge(zero_ok, 1)
                pool.memset(k["first_stacks"][1][SHIFT_ROWS:P], 1.0).then_inc(zero_ok, 1)

                pool.wait_ge(zero_ok, 2)

                def body(i, j, n):
                    pool.wait_ge(part2_ok, i + 1)
                    wait_past(pool, parts_out[j], 48 * n)
                    pool.tensor_tensor(part3[:, j], rest[:, j], part2[:, j], ALU.subtract).then_inc(part3_ok, 1)

                over_blocks(pool, BLOCKS, body)

            @block.scalar
            def _(act):
                def highs(i, j):
                    act.wait_ge(t_ok, i + 1)
                    for c in range(DC):
                        act.activation(xnT_hi[:, j, c], ps_t[:, c], ACT.Copy).then_inc(t_hi_ok, 1)

                def body(i, j, n):
                    wait_past(act, parts_out[j], 48 * n)
                    wait_past(act, n_ok, i - 1 if not isinstance(i, int) or i else 0)
                    for c in range(4):
                        act.wait_ge(qk_ok, 4 * i + c + 1)
                        scale = DH ** -0.5 if c < DC else 1.0
                        act.activation(part1[:, j, c], ps_qk[:, c], ACT.Copy, scale=scale)
                        act.activation(square[:, j, c], ps_qk[:, c], ACT.Square, scale=scale).then_inc(part1_ok, 1)
                        if c == 0 and not is_last(i, BLOCKS):
                            norm_root(act, norm, i + 1, 1 - j)
                        if c == 2 and not is_last(i, BLOCKS):
                            highs(i + 1, 1 - j)
                        if c % 2:
                            g = c // 2
                            act.wait_ge(v_ok, 2 * i + g + 1)
                            for t in range(2):
                                last = act.activation(
                                    k["V"][:, :, bass.ds(TB * i + 2 * g + t, 1), :, 0:DH],
                                    ps_v[:, t].rearrange("p (g h d) -> p g h d", h=HG, d=DH), ACT.Copy)
                            last.then_inc(v_used, 1)

                norm_root(act, norm, 0, 0)
                act.wait_ge(w_in, 48)
                act.activation(w_hi[:, :], w_raw[:, :], ACT.Copy).then_inc(w_split, 1)
                highs(0, 0)
                over_blocks(act, BLOCKS, body)

            @block.vector
            def _(dve):
                dve.memset(ps_n[:, :], 0.0).then_inc(n_used, 1)
                dve.wait_ge(x_in[0], 16)
                norm_measure(dve, norm, 0, 0)
                norm_apply(dve, norm, 0, 0, lambda t: xn[:, 0, t:t + 1, :])
                dve.wait_ge(w_split, 1)
                dve.tensor_tensor(w_lo[:, :], w_raw[:, :], w_hi[:, :].bitcast(F32), ALU.subtract).then_inc(w_split, 1)

                def rests(i, j, c):
                    dve.wait_ge(part1_ok, 4 * i + c + 1)
                    if c < DC:
                        op = dve.scalar_tensor_tensor(out=rest[:, j, c], in0=ps_qk[:, c], scalar=DH ** -0.5,
                                                      in1=part1[:, j, c], op0=ALU.mult, op1=ALU.subtract)
                    else:
                        op = dve.tensor_tensor(rest[:, j, c], ps_qk[:, c], part1[:, j, c], ALU.subtract)
                    op.then_inc(rest_ok, 1)

                def lows(i, j):
                    for c in range(DC):
                        dve.wait_ge(t_hi_ok, DC * i + c + 1)
                        dve.tensor_tensor(xnT_lo[:, j, c], ps_t[:, c], xnT_hi[:, j, c].bitcast(F32),
                                          ALU.subtract).then_inc(t_lo_ok, 1)

                def greatest_norms(i):
                    dve.wait_ge(n_ok, i + 1)
                    dve.tensor_reduce(norm_max[:, bass.ds(i, 1)], ps_n[:, :], AX.X, ALU.max).then_inc(n_used, 1)

                def body(i, j, n):
                    last = is_last(i, BLOCKS)
                    if not last:
                        hold(dve, k, x_in[1 - j], 16 * (n + j) + 16)
                        norm_measure(dve, norm, i + 1, 1 - j)
                    wait_past(dve, part3_ok, i - 1 if not isinstance(i, int) or i else 0)
                    rests(i, j, 0)
                    if not last:
                        norm_apply(dve, norm, i + 1, 1 - j, lambda t: xn[:, 1 - j, t:t + 1, :])
                    rests(i, j, 1)
                    if not is_first(i):
                        greatest_norms(i - 1)
                    rests(i, j, 2)
                    if not last:
                        lows(i + 1, 1 - j)
                    rests(i, j, 3)
                    dve.wait_ge(rest_ok, 4 * i + 4)
                    wait_past(dve, parts_out[j], 48 * n)
                    dve.tensor_copy(part2[:, j], rest[:, j]).then_inc(part2_ok, 1)

                lows(0, 0)
                over_blocks(dve, BLOCKS, body)
                greatest_norms(BLOCKS - 1)
                dve.wait_ge(n_used, BLOCKS + 1)
                dve.tensor_reduce(norm_top[:, :], norm_max[:, :], AX.X, ALU.max).then_inc(top_ok, 1)
                dve.wait_ge(topT_ok, 1)
                dve.tensor_copy(norm_row[:, :], ps_n[0:1, 0:P]).then_inc(row_ok, 1)
                dve.wait_ge(row_ok, 1)
                row = norm_row[:, :].rearrange("p (m c r) -> p m c r", m=2, c=2)
                dve.tensor_tensor(over[:, :, :], row[:, 0, :, 0:8], row[:, 1, :, 0:8], ALU.mult).then_inc(row_ok, 1)
                dve.wait_ge(row_ok, 2)
                dve.tensor_scalar(over[:, :, :], over[:, :, :], SAFE_SQUARE, None, ALU.is_gt).then_inc(row_ok, 1)
                dve.wait_ge(row_ok, 3)
                dve.tensor_reduce(k["unsafe"][:, :], over[:, :, :], AX.XY, ALU.max).then_inc(row_ok, 1)

            @block.tensor
            def _(pe):
                def turn(i, j):
                    pe.wait_ge(norm["xn_ok"], i + 1)
                    wait_past(pe, t_lo_ok, DC * i)
                    for t in range(TB):
                        for c in range(DC):
                            last = pe.transpose(ps_t[:, c, t * P:(t + 1) * P],
                                                xn[:, j, t, c * P:(c + 1) * P], k["ident"][:, :])
                    last.then_inc(t_ok, 1)

                def norms(i, j):
                    pe.wait_ge(part1_ok, 4 * i + 4)
                    pe.wait_ge(n_used, i + 1)
                    for c in range(4):
                        last = pe.matmul(ps_n[32 * c:32 * c + 8, :], k["head_sel"][:, :], square[:, j, c],
                                         start=True, stop=True)
                    last.then_inc(n_ok, 1)

                def body(i, j, n):
                    pe.wait_ge(t_lo_ok, DC * i + DC)
                    for c in range(4):
                        wait_past(pe, rest_ok, 4 * i + c - 3)
                        w, o = c // DC, (c % DC) * P
                        for d in range(DC):
                            last = mm3(pe, ps_qk[:, c], (w_hi[:, w, d, o:o + P], w_lo[:, w, d, o:o + P]),
                                       (xnT_hi[:, j, d], xnT_lo[:, j, d]), d == 0, d == DC - 1)
                        last.then_inc(qk_ok, 1)
                        if c % 2:
                            g = c // 2
                            wait_past(pe, v_used, 2 * i + g)
                            for t in range(2):
                                o = (2 * g + t) * P
                                for d in range(DC):
                                    last = mm3(pe, ps_v[:, t], (xnT_hi[:, j, d, o:o + P], xnT_lo[:, j, d, o:o + P]),
                                               (w_hi[:, 2, d], w_lo[:, 2, d]), d == 0, d == DC - 1)
                            last.then_inc(v_ok, 1)
                        if c == 0 and not is_first(i):
                            norms(i - 1, 1 - j)
                        if c == 2 and not is_last(i, BLOCKS):
                            turn(i + 1, 1 - j)

                turn(0, 0)
                pe.wait_ge(w_split, 2)
                over_blocks(pe, BLOCKS, body)
                norms(BLOCKS - 1, 1)
                pe.wait_ge(top_ok, 1)
                pe.transpose(ps_n[0:1, 0:P], norm_top[:, :], k["ident"][:, :]).then_inc(topT_ok, 1)


def load_stacks(eng, io, g, b, Q, K, sem):
    for slots, dst, m in ((Q_SLOTS, Q, 0), (K_SLOTS, K, 1)):
        for n, part in enumerate(slots):
            src = io["qk"][part, b, m, bass.ds(g, 1)].rearrange("o (h d) t -> d (o h) t", d=DH)
            eng.dma_start(dst[DH * n:DH * n + DH], src).then_inc(sem, 16)


def phase_shift(k):
    nc, io = k["nc"], k["io"]
    QT = SEQ // P
    with ExitStack() as mem:
        def sb(name, shape, dt):
            return mem.enter_context(nc.sbuf_tensor(name, shape, dt))

        Q, K = sb("Q_max", [P, HG, SEQ], BF16), sb("K_max", [P, HG, SEQ], BF16)
        mask = sb("wide_mask", [P, 2 * SEQ - P], BF16)
        masked = sb("masked_scores", [P, SEQ], F32)
        top = sb("top", [P, HG * QT], F32)
        neg = sb("neg_top", [HG * QT, P], F32)
        left = sb("left", [HG * QT, 2, P], F32)
        parts = sb("shift_part", [HG * QT, 3, P], BF16)
        ps_s = mem.enter_context(nc.psum_tensor("ps_max", [P, SEQ], F32))
        ps_t = mem.enter_context(nc.psum_tensor("ps_top", [HG * QT, P], F32))
        loaded, scores_ok, mask_ok, masked_ok, top_ok, turned_ok, neg_ok, split_ok, stored, parts_free = sems(
            k, "shift", "loaded scores_ok mask_ok masked_ok top_ok turned_ok neg_ok split_ok stored parts_free")
        EACH = HG * QT

        with nc.Block() as block:

            def where_unsafe(eng):
                return eng.If(eng.value_load(k["unsafe"][0:1, 0:1], min_val=0, max_val=1) > 0)

            @block.sync
            def _(sp):
                with where_unsafe(sp):
                    load_stacks(sp, io, 0, 0, Q[:, :, :], K[:, :, :], loaded)
                    with sp.Fori(0, GROUPS - 1) as g:
                        for b in range(BATCH):
                            hold(sp, k, scores_ok, EACH * (BATCH * g + b + 1))
                            load_stacks(sp, io, g + b, 1 - b, Q[:, :, :], K[:, :, :], loaded)
                    sp.wait_ge(scores_ok, EACH * (UNITS - 1))
                    load_stacks(sp, io, GROUPS - 1, 1, Q[:, :, :], K[:, :, :], loaded)
                    sp.wait_ge(loaded, 16 * 12 * UNITS)

            @block.gpsimd
            def _(pool):
                with where_unsafe(pool):
                    pool.memset(mask[:, :], 0.0).then_inc(mask_ok, 1)
                    pool.wait_ge(mask_ok, 1)
                    pool.affine_select(out=mask[:, :], in_=mask[:, :], compare_op=ALU.is_ge, fill=-3.0e38,
                                       base=SEQ - P, pattern=[[-1, 2 * SEQ - P]], channel_multiplier=1
                                       ).then_inc(mask_ok, 1)
                    with pool.Fori(0, UNITS) as u:
                        hold(pool, k, split_ok, 3 * u + 3)
                        for n in range(3):
                            pool.dma_start(
                                io["shift"].rearrange("m g b h (t p) -> m (g b) (h t) p", p=P)[n, bass.ds(u, 1)]
                                .rearrange("o r p -> (o r) p"), parts[:, n, :]).then_inc(stored, 16)
                        pool.wait_ge(stored, 48 * u + 48)
                        pool.sem_inc(parts_free, 1)

            @block.vector
            def _(dve):
                with where_unsafe(dve):
                    dve.sem_inc(masked_ok, 1)
                    dve.sem_inc(parts_free, 1)
                    dve.sem_inc(top_ok, 1)
                    dve.wait_ge(mask_ok, 2)
                    with dve.Fori(0, UNITS) as u:
                        for h in range(HG):
                            with dve.Fori(0, QT) as t:
                                at = EACH * u + QT * h + t
                                dve.wait_ge(scores_ok, at + 1)
                                dve.wait_ge(top_ok, at + 1)
                                dve.tensor_tensor(masked[:, :], ps_s[:, :], mask[:, bass.ds(SEQ - P - P * t, SEQ)],
                                                  ALU.add).then_inc(masked_ok, 1)
                                dve.wait_ge(masked_ok, at + 2)
                                dve.tensor_reduce(top[:, bass.ds(QT * h + t, 1)], masked[:, :], AX.X, ALU.max
                                                  ).then_inc(top_ok, 1)
                        dve.wait_ge(turned_ok, u + 1)
                        dve.tensor_scalar(neg[:, :], ps_t[:, :], -1.0, None, ALU.mult).then_inc(neg_ok, 1)
                        dve.wait_ge(neg_ok, 3 * u + 1)
                        dve.wait_ge(parts_free, u + 1)
                        rest = neg[:, :]
                        for n in range(3):
                            dve.tensor_copy(parts[:, n], rest).then_inc(split_ok, 1)
                            if n < 2:
                                dve.wait_ge(split_ok, 3 * u + n + 1)
                                dve.tensor_tensor(left[:, n], rest, parts[:, n], ALU.subtract).then_inc(neg_ok, 1)
                                dve.wait_ge(neg_ok, 3 * u + n + 2)
                                rest = left[:, n]

            @block.tensor
            def _(pe):
                with where_unsafe(pe):
                    with pe.Fori(0, UNITS) as u:
                        hold(pe, k, loaded, 192 * u + 192)
                        for h in range(HG):
                            with pe.Fori(0, QT) as t:
                                at = EACH * u + QT * h + t
                                pe.wait_ge(masked_ok, at + 1)
                                for c in range(0, SEQ, BT):
                                    last = pe.matmul(ps_s[:, c:c + BT], Q[0:SHIFT_ROWS, h, bass.ds(P * t, P)],
                                                     K[0:SHIFT_ROWS, h, c:c + BT], start=True, stop=True)
                                last.then_inc(scores_ok, 1)
                        hold(pe, k, top_ok, EACH * u + EACH + 1)
                        pe.transpose(ps_t[:, :], top[:, :], k["ident"][:, :]).then_inc(turned_ok, 1)


def phase_attention(k):
    nc, io = k["nc"], k["io"]
    SLICES = SEQ // BT
    TILE_LIST = [(q, t, max(0, (t - TB * q) * P)) for q in range(SLICES) for t in range(TB * (q + 1))]
    NT = len(TILE_LIST)
    LAST = [max(g for g, (q, _, _) in enumerate(TILE_LIST) if q == s) for s in range(SLICES)]
    DIAG = [g for g, (q, t, _) in enumerate(TILE_LIST) if t >= TB * q]
    SCORE_BUFS, PROB_BUFS = 3, 4
    LAG = 2
    LOADS = 13

    with ExitStack() as mem:
        def sb(name, shape, dt):
            return mem.enter_context(nc.sbuf_tensor(name, shape, dt))

        Q, K = ((k["first_stacks"][n], sb(name, [P, HG, SEQ], BF16)) for n, name in enumerate(("Q_odd", "K_odd")))
        V = sb("V_unit", [P, 2, SEQ // P, HG, DH + 1], F32)
        probs = sb("probs", [P, PROB_BUFS, HG, BT], F32)
        sums = sb("weighted", [P, 2, BT], F32)
        inv = sb("inv_denominator", [P, 2, TB, HG], F32)
        result = sb("attention_rows", [P, 2, TB, HG, DH], F32)
        ps_s = mem.enter_context(nc.psum_tensor("ps_s", [P, SCORE_BUFS, 2, BT], F32))
        ps_o = mem.enter_context(nc.psum_tensor("ps_o", [P, 2, BT], F32))

        loaded = k["loaded"]
        stored = sems(k, "rows_stored", "even odd")
        ones_ok, zero_ok, v_ok, scores_ok, exp_ok, mask_ok, pv_ok, sums_ok, turned_ok, inv_ok, result_ok = sems(
            k, "attention", "ones_ok zero_ok v_ok scores_ok exp_ok mask_ok pv_ok sums_ok turned_ok inv_ok result_ok")

        with nc.Block() as block:

            def load_shifts(eng, u, j):
                src = io["shift"].rearrange("m g b h t -> m (g b) h t")[:, bass.ds(u, 1)]
                eng.dma_start(Q[j][SHIFT_ROWS:KROWS], src.rearrange("m o h t -> m (o h) t")).then_inc(loaded[j], 16)

            def load(eng, u, g, j):
                load_stacks(eng, io, g, j, Q[j], K[j], loaded[j])
                load_shifts(eng, u, j)

            @block.sync
            def _(sp):
                load_shifts(sp, 0, 0)
                load(sp, 1, 0, 1)

                def store(u, j, n):
                    for q in range(SLICES):
                        hold(sp, k, result_ok, SLICES * u + q + 1 + 2)
                        to = io["attended"].rearrange("g b (s t p) c -> (g b) s p t c", p=P, t=TB)
                        sp.dma_start(to[bass.ds(u, 1), q].rearrange("o p t c -> p (o t) c"),
                                     result[:, q % 2].rearrange("p t h d -> p t (h d)")).then_inc(stored[q % 2], 16)

                with sp.Fori(0, UNITS // 2 - 1) as n:
                    for j in range(2):
                        u = 2 * n + j
                        store(u, j, n)
                        hold(sp, k, scores_ok, 2 * NT * u + 2 * NT)
                        load(sp, u + 2, n + 1, j)
                for j in range(2):
                    store(UNITS - 2 + j, j, UNITS // 2 - 1)
                for j in range(2):
                    sp.wait_ge(stored[j], 16 * (SLICES // 2 * UNITS + 1))

            @block.gpsimd
            def _(pool):
                pool.memset(K[1][SHIFT_ROWS:P], 1.0).then_inc(ones_ok, 1)
                pool.wait_ge(ones_ok, 1)
                with pool.Fori(0, UNITS // 2) as n:
                    for j in range(2):
                        u = 2 * n + j
                        for g in DIAG:
                            off = TILE_LIST[g][2]
                            block_of = probs[:, g % PROB_BUFS, :, off:off + P]
                            hold(pool, k, exp_ok, 2 * NT * u + 2 * g + 2 + 2)
                            pool.affine_select(out=block_of, in_=block_of, compare_op=ALU.is_ge, fill=0.0, base=0,
                                               pattern=[[0, HG], [1, P]], channel_multiplier=-1).then_inc(mask_ok, 1)

            @block.scalar
            def _(act):
                act.sem_inc(exp_ok, 2)
                with act.Fori(0, UNITS // 2) as n:
                    for j in range(2):
                        u = 2 * n + j
                        for g, (q, t, off) in enumerate(TILE_LIST):
                            for p in range(2):
                                s = 2 * g + p
                                if p == 0:
                                    act.wait_ge(pv_ok, NT * u + g + 1)
                                act.wait_ge(scores_ok, 2 * NT * u + s + 1)
                                act.activation(probs[:, g % PROB_BUFS, 2 * p:2 * p + 2, off:BT],
                                               ps_s[:, s % SCORE_BUFS, :, off:BT], ACT.Exp).then_inc(exp_ok, 1)

            @block.vector
            def _(dve):
                dve.memset(ps_o[:, :, :], 0.0).then_inc(zero_ok, 1)
                dve.sem_inc(result_ok, 2)
                dve.sem_inc(stored[0], 16)
                dve.sem_inc(stored[1], 16)

                def take_v(u, j):
                    dve.tensor_copy(V[:, j], k["V"].rearrange("p g (b t) h d -> p (g b) t h d", b=BATCH)[:, bass.ds(u, 1)]
                                    ).then_inc(v_ok, 1)

                def unit(u, j, n):
                    for q in range(SLICES):
                        dve.wait_ge(pv_ok, NT * u + LAST[q] + 1 + PROB_BUFS)
                        dve.tensor_copy(sums[:, q % 2], ps_o[:, q % 2]).then_inc(sums_ok, 1)
                        dve.wait_ge(turned_ok, SLICES * u + q + 1)
                        turned = ps_o[:, q % 2].rearrange("p (t h c) -> p t h c", t=TB, h=HG)
                        dve.reciprocal(inv[:, q % 2], turned[:, :, :, DH]).then_inc(inv_ok, 1)
                        dve.wait_ge(inv_ok, SLICES * u + q + 1)
                        dve.wait_ge(stored[q % 2], 16 * (SLICES // 2 * u + q // 2 + 1))
                        dve.tensor_tensor(result[:, q % 2], turned[:, :, :, 0:DH],
                                          inv[:, q % 2].unsqueeze(3).to_broadcast([P, TB, HG, DH]),
                                          ALU.mult).then_inc(result_ok, 1)

                take_v(0, 0)
                take_v(1, 1)
                with dve.Fori(0, UNITS // 2 - 1) as n:
                    for j in range(2):
                        unit(2 * n + j, j, n)
                        take_v(2 * n + j + 2, j)
                for j in range(2):
                    unit(UNITS - 2 + j, j, UNITS // 2 - 1)

            @block.tensor
            def _(pe):
                pe.sem_inc(pv_ok, PROB_BUFS)
                pe.wait_ge(zero_ok, 1)

                def scores(u, j, g):
                    q, t, off = TILE_LIST[g]
                    for p in range(2):
                        s = 2 * g + p
                        before = s - SCORE_BUFS if s >= SCORE_BUFS else max(
                            x for x in range(2 * NT) if x % SCORE_BUFS == s % SCORE_BUFS) - 2 * NT
                        pe.wait_ge(exp_ok, 2 * NT * u + before + 1 + 2)
                        for h in range(2):
                            last = pe.matmul(ps_s[:, s % SCORE_BUFS, h, off:BT],
                                             K[j][0:KROWS, 2 * p + h, t * P:(t + 1) * P],
                                             Q[j][0:KROWS, 2 * p + h, q * BT + off:(q + 1) * BT],
                                             start=True, stop=True)
                        last.then_inc(scores_ok, 1)

                def weigh(u, j, g):
                    q, t, off = TILE_LIST[g]
                    if t == 0:
                        pe.wait_ge(result_ok, SLICES * u + q + 1)
                    pe.wait_ge(exp_ok, 2 * NT * u + 2 * g + 2 + 2)
                    if g in DIAG:
                        pe.wait_ge(mask_ok, len(DIAG) * u + DIAG.index(g) + 1)
                    for h in range(HG):
                        last = pe.matmul(ps_o[32 * h:32 * h + DH + 1, q % 2, off:BT], V[:, j, t, h, :],
                                         probs[:, g % PROB_BUFS, h, off:BT],
                                         start=(t == 0), stop=(g == LAST[q]))
                    last.then_inc(pv_ok, 1)

                def turn(u, q):
                    pe.wait_ge(sums_ok, SLICES * u + q + 1)
                    for t in range(TB):
                        last = pe.transpose(ps_o[:, q % 2, t * P:(t + 1) * P], sums[:, q % 2, t * P:(t + 1) * P],
                                            k["ident"][:, :])
                    last.then_inc(turned_ok, 1)

                with pe.Fori(0, UNITS // 2) as n:
                    steps = [(j, g) for j in range(2) for g in range(NT)]
                    for at in range(len(steps) + LAG + 2):
                        if at < len(steps):
                            j, g = steps[at]
                            if g == 0:
                                pe.wait_ge(loaded[j], 16 * LOADS * n + 16 * LOADS)
                                if j:
                                    pe.wait_ge(ones_ok, 1)
                                pe.wait_ge(v_ok, 2 * n + j + 1)
                            scores(2 * n + j, j, g)
                        if 0 <= at - LAG < len(steps):
                            j, g = steps[at - LAG]
                            weigh(2 * n + j, j, g)
                        if at - LAG - 2 >= 0:
                            j, g = steps[at - LAG - 2]
                            if g in LAST:
                                turn(2 * n + j, LAST.index(g))


def live(i):
    return not isinstance(i, int) or 0 <= i < BLOCKS


def over_steps(eng, step):
    for i in range(2):
        step(i, i % 2, i // 2)
    with eng.Fori(1, BLOCKS // 2 - 1) as n:
        for j in range(2):
            step(2 * n + j, j, n)
    for i in range(BLOCKS - 2, BLOCKS + 2):
        step(i, i % 2, i // 2)


def phase_tokens(k):
    nc, io = k["nc"], k["io"]
    FULL = [P, TB, EXPERTS, EXPERTS]
    RANKS, PLACES, CHOSEN = 12, 6, 7
    with ExitStack() as mem:
        def sb(name, shape, dt):
            return mem.enter_context(nc.sbuf_tensor(name, shape, dt))

        def ps(name, shape, dt=F32):
            return mem.enter_context(nc.psum_tensor(name, shape, dt))

        w_hi, w_lo = sb("wo_hi", [P, DC, D], F32R), sb("wo_lo", [P, DC, D], F32R)
        r_raw = sb("router_raw", [P, DC, EXPERTS], F32)
        warm = sb("table_warmer", [P, 1], F32)
        router = sb("router_parts", [P, DC, 2, EXPERTS], F32R)
        rows = sb("attended_rows", [P, 2, TB, GROUPS, HG * DH], F32)
        aT_hi, aT_lo = sb("aT_hi", [P, DC, BT], F32R), sb("aT_lo", [P, DC, BT], F32R)
        xn = sb("xn2", [P, 2, TB, D], F32)
        xT_hi, xT_lo = sb("xn2T_hi", [P, 2, DC, BT], F32R), sb("xn2T_lo", [P, 2, DC, BT], F32R)
        lower = sb("lower_index", [P, EXPERTS, EXPERTS], BF16)
        higher = sb("higher_index", [P, EXPERTS, EXPERTS], BF16)
        high_score = sb("router_scores_high", [P, TB, EXPERTS], F32)
        score = sb("router_scores", [P, TB, EXPERTS], F32)
        beats, ties = sb("beats", FULL, BF16), sb("ties", FULL, BF16)
        rank = sb("rank", [P, TB, EXPERTS], F32)
        is_rank = sb("is_rank", [P, TOP_K, TB, EXPERTS], F32)
        chosen = sb("chosen", [P, TB, EXPERTS], BF16)
        before = sb("before", [P, P], BF16)
        ones = sb("ones_square", [P, P], BF16)
        region_int = sb("region_int", [P, EXPERTS], I32)
        region = sb("region", [P, EXPERTS], F32)
        base = sb("next_row", [P, EXPERTS], F32)
        place = sb("place", [P, TB, EXPERTS], F32)
        picked = sb("picked", [P, TOP_K, TB, EXPERTS], F32)
        place_of = sb("place_of", [P, TOP_K, TB], F32)
        score_of = sb("score_of", [P, TOP_K, TB], F32)
        gate = sb("gate", [P, TOP_K, TB], F32)
        scaled = sb("scaled_rows", [P, TOP_K * TB, D], F32)
        count = sb("count", [P, EXPERTS], F32)
        padded = sb("padded_int", [P, EXPERTS], I32)
        room = sb("room", [P, EXPERTS], F32)
        ends = sb("ends", [P, EXPERTS], F32)
        unused = sb("unused_rows", [P, EXPERTS], F32)
        zeros = sb("zero_row", [P, D], F32)
        start_int = sb("tile_start_int", [1, SLOT_TILES], I32)
        tile_start = sb("tile_start", [1, SLOT_TILES], F32)
        expert = sb("tile_expert_f", [1, SLOT_TILES], F32)
        tile_row = sb("tile_row_f", [1, SLOT_TILES], F32)
        end_row = sb("end_row", [1, EXPERTS], I32)
        wi_hi, wi_lo = sb("w_in_hi", [P, DC, FF], F32R), sb("w_in_lo", [P, DC, FF], F32R)
        wg_hi, wg_lo = sb("w_swiglu_hi", [P, DC, FF], F32R), sb("w_swiglu_lo", [P, DC, FF], F32R)
        wo_hi, wo_lo = sb("w_out_hi", [P, FC, D], F32R), sb("w_out_lo", [P, FC, D], F32R)
        silu = sb("silu", [P, 2, BT], F32)
        h = sb("h_shared", [P, 2, BT], F32)
        w_raw = silu[:, 0, :].rearrange("p (c n) -> p c n", c=DC)
        s_raws = (h[:, :, :], scaled[:, 0:4, :].rearrange("p s d -> p (s d)").rearrange("p (c n) -> p c n", c=DC),
                  scaled[:, 4:8, :])
        moved, out_row, moved_sum = (silu[:, :, :].rearrange("p n t -> p (n t)")[:, at:at + size] for at, size in (
            (0, TOP_K * TILES * (EXPERTS - 1)), (512, TOP_K * TILES), (512 + TOP_K * TILES, TOP_K * TILES)))
        moved = moved.rearrange("p (s e) -> p s e", e=EXPERTS - 1)
        passed_end, skipped = (a[0:1, :, :].rearrange("p n t -> p (n t)")[:, 0:SLOT_TILES * EXPERTS].rearrange(
            "p (s e) -> p s e", e=EXPERTS) for a in (silu, h))
        h_hi, h_lo = sb("h_hi", [P, FC, BT], F32R), sb("h_lo", [P, FC, BT], F32R)

        ps_t, ps_y = ps("ps_turned", [P, DC, BT]), ps("ps_rows", [P, TB, D])
        ps_m, ps_g = ps("ps_mid", [P, BT]), ps("ps_gated", [P, BT])
        ps_r = ps("ps_router", [P, TB, 2, EXPERTS])
        ps_b = ps("ps_places", [P, TB + 1, EXPERTS])

        norm = layer_norm(k, mem, "ln2")
        a_turn, x_turn = turner(k, "a_turn", ps_t), turner(k, "x2_turn", ps_t)
        w_in, w_split, y_ok, added_ok, r_ok, r_used = sems(k, "out_projection", "w_in w_split y_ok added_ok r_ok r_used")
        rows_in = sems(k, "rows_in", "even odd")
        made, rank_step, chosen_ok, counted, place_step, gate_ok, scaled_ok = sems(
            k, "route", "made rank_step chosen_ok counted place_step gate_ok scaled_ok")
        table_step, spare_ok, pad_ok, pads_out = sems(k, "table", "table_step spare_ok pad_ok pads_out")
        scattered = sem(k, "scattered")
        s_in, s_high, s_split = sems(k, "shared", "w_in w_high w_split")
        mid_ok, gated_ok, silu_ok, h_ok, hi_ok, lo_ok, s_ok, s_used = sems(
            k, "shared", "mid_ok gated_ok silu_ok h_ok hi_ok lo_ok s_ok s_used")

        with nc.Block() as block:

            @block.sync
            def _(sp):
                def load(i):
                    b, t0 = i * BT // SEQ, i * BT % SEQ
                    for g in range(GROUPS):
                        sp.dma_start(rows[:, i % 2, :, g, :],
                                     io["attended"][g, b, t0:t0 + BT, :].rearrange("(t p) c -> p t c", p=P)
                                     ).then_inc(rows_in[i % 2], 16)

                sp.dma_start(w_raw[:, :, :], io["wo"].rearrange("(c p) n -> p c n", p=P)).then_inc(w_in, 16)
                load(0)
                sp.dma_start(r_raw[:, :, :], io["router"].rearrange("(c p) n -> p c n", p=P)).then_inc(w_in, 16)
                load(1)
                for name, raw in zip(("w_in_shared", "w_swiglu", "w_out_shared"), s_raws):
                    sp.dma_start(raw, io[name].rearrange("(c p) n -> p c n", p=P)).then_inc(s_in, 16)
                sp.wait_ge(made, 1)
                sp.dma_start(io["slots_in"][EXPERTS * REGION:SLOTS, :].rearrange("(n p) d -> p n d", p=P),
                             zeros[:, :].unsqueeze(1).to_broadcast([P, EXPERTS, D])).then_inc(spare_ok, 16)
                for i in range(2, BLOCKS):
                    sp.wait_ge(a_turn["ps_ok"], i - 1)
                    load(i)
                    if i == 3:
                        for name, w in (("w_in_e", k["we_in"]), ("w_swiglu_e", k["we_swiglu"])):
                            for e in range(EXPERTS):
                                sp.dma_start(w[:, e].bitcast(F32), io[name][e].rearrange("(c p) f -> p c f", p=P)
                                             ).then_inc(k["experts_in"], 16)
                sp.wait_ge(pad_ok, 1)
                for e in range(EXPERTS):
                    at = sp.value_load(end_row[0:1, e:e + 1], min_val=e * REGION, max_val=e * REGION + TOK)
                    sp.dma_start(io["slots_in"][bass.ds(at, P), :], zeros[:, :]).then_inc(pads_out, 16)
                sp.wait_ge(spare_ok, 16)
                sp.wait_ge(pads_out, 16 * EXPERTS)

            @block.gpsimd
            def _(pool):
                pool.memset(zeros[:, :], 0.0).then_inc(made, 1)
                pool.memset(lower[:, :, :], 1.0).then_inc(made, 1)
                pool.memset(higher[:, :, :], 1.0).then_inc(made, 1)
                pool.memset(before[:, :], 1.0).then_inc(made, 1)
                pool.memset(ones[:, :], 1.0).then_inc(made, 1)
                pool.iota(region_int[:, :], pattern=[[REGION, EXPERTS]], base=0, channel_multiplier=0).then_inc(made, 1)
                pool.iota(start_int[:, :], pattern=[[P, SLOT_TILES]], base=0,
                          channel_multiplier=0).then_inc(made, 1)
                pool.wait_ge(made, 7)
                pool.affine_select(out=lower[:, :, :], in_=lower[:, :, :], compare_op=ALU.is_gt, fill=0.0, base=0,
                                   pattern=[[1, EXPERTS], [-1, EXPERTS]], channel_multiplier=0).then_inc(made, 1)
                pool.affine_select(out=higher[:, :, :], in_=higher[:, :, :], compare_op=ALU.is_ge, fill=0.0, base=0,
                                   pattern=[[-1, EXPERTS], [1, EXPERTS]], channel_multiplier=0).then_inc(made, 1)
                pool.affine_select(out=before[:, :], in_=before[:, :], compare_op=ALU.is_gt, fill=0.0, base=0,
                                   pattern=[[1, P]], channel_multiplier=-1).then_inc(made, 1)

                def low(b, f):
                    pool.wait_ge(hi_ok, FC * b + f + 1)
                    pool.tensor_tensor(h_lo[:, f], h[:, f % 2], h_hi[:, f].bitcast(F32), ALU.subtract
                                       ).then_inc(lo_ok, 1)

                def scatter(b, s):
                    r, t = s % TOP_K, s // TOP_K
                    pool.wait_ge(scaled_ok, TOP_K * TB * b + s + 1)
                    pool.indirect_dma_start(
                        out=io["slots_in"],
                        out_offset=bass.IndirectOffsetOnAxis(ap=k["slot"][:, r, TB * b + t:TB * b + t + 1], axis=0),
                        in_=scaled[:, s, :], in_offset=None).then_inc(scattered, 16)

                for b in range(BLOCKS + 1):
                    left = list(range(TOP_K * TB)) if b else []
                    if b:
                        pool.wait_ge(place_step, PLACES * b)
                    for s in left[:-2]:
                        scatter(b - 1, s)
                    for f in range(FC):
                        if b < BLOCKS:
                            low(b, f)
                        if f < 2 and b:
                            scatter(b - 1, left[f - 2])
                pool.wait_ge(scattered, 16 * TOP_K * TILES)

            @block.scalar
            def _(act):
                def gates(b):
                    act.wait_ge(rank_step, RANKS * b + RANKS)
                    wait_past(act, scaled_ok, at_least(TOP_K * TB * b))
                    act.activation(gate[:, :, :], score_of[:, :, :], ACT.Sigmoid).then_inc(gate_ok, 1)

                def step(i, j, n):
                    if live(i - 1):
                        high_parts(act, x_turn, i - 1, lambda c: xT_hi[:, 1 - j, c])
                    if live(i):
                        norm_root(act, norm, i, j)
                        act.activation(warm[:, :], k["eps"][:, :], ACT.Silu)
                    if live(i + 1):
                        act.wait_ge(y_ok, 2 * i + 2)
                        high_parts(act, a_turn, i + 1, lambda c: aT_hi[:, c])
                    if live(i - 1):
                        for f in range(FC):
                            at = FC * (i - 1) + f
                            act.wait_ge(mid_ok, at + 1)
                            wait_past(act, h_ok, at_least(at - 1))
                            act.activation(silu[:, f % 2], ps_m[:, :], ACT.Silu).then_inc(silu_ok, 1)
                            act.wait_ge(h_ok, at + 1)
                            act.activation(h_hi[:, f], h[:, f % 2], ACT.Copy).then_inc(hi_ok, 1)
                        gates(i - 1)

                high_parts(act, a_turn, 0, lambda c: aT_hi[:, c])
                act.wait_ge(s_in, 48)
                for raw, hi in zip(s_raws, (wi_hi, wg_hi, wo_hi)):
                    act.activation(hi[:, :, :], raw, ACT.Copy).then_inc(s_high, 1)
                over_steps(act, step)

            @block.vector
            def _(dve):
                def a_low(i):
                    low_parts(dve, a_turn, i, lambda c: aT_lo[:, c], lambda c: aT_hi[:, c])

                def add_rows(i, sem, at, used):
                    for g in range(2):
                        dve.wait_ge(sem, at + g + 1)
                        x = k["X"][:, bass.ds(TB * i + 2 * g, 2), :]
                        dve.tensor_tensor(x, x, ps_y[:, 2 * g:2 * g + 2, :], ALU.add).then_inc(used, 1)

                def rank_block(b):
                    local = 0

                    def link(op):
                        nonlocal local
                        local += 1
                        op.then_inc(rank_step, 1)
                        dve.wait_ge(rank_step, RANKS * b + local)

                    dve.wait_ge(r_ok, b + 1)
                    link(dve.tensor_copy(high_score[:, :, :], ps_r[:, :, 0, :]))
                    link(dve.tensor_tensor(score[:, :, :], high_score[:, :, :], ps_r[:, :, 1, :], ALU.add))
                    own = score[:, :, :].unsqueeze(3).to_broadcast(FULL)
                    rival = score[:, :, :].unsqueeze(2).to_broadcast(FULL)
                    dve.tensor_tensor(beats[:, :, :, :], rival, own, ALU.is_gt)
                    link(dve.tensor_tensor(ties[:, :, :, :], rival, own, ALU.is_ge))
                    dve.tensor_tensor(beats[:, :, :, :], beats[:, :, :, :],
                                      higher[:, :, :].unsqueeze(1).to_broadcast(FULL), ALU.mult)
                    link(dve.tensor_tensor(ties[:, :, :, :], ties[:, :, :, :],
                                           lower[:, :, :].unsqueeze(1).to_broadcast(FULL), ALU.mult))
                    link(dve.tensor_tensor(beats[:, :, :, :], beats[:, :, :, :], ties[:, :, :, :], ALU.add))
                    link(dve.tensor_reduce(rank[:, :, :], beats[:, :, :, :], AX.X, ALU.add))
                    wait_past(dve, counted, b)
                    link(dve.tensor_scalar(chosen[:, :, :], rank[:, :, :], float(TOP_K), None, ALU.is_lt))
                    assert local == CHOSEN

                def chosen_scores(b):
                    local = CHOSEN

                    def link(op):
                        nonlocal local
                        local += 1
                        op.then_inc(rank_step, 1)
                        dve.wait_ge(rank_step, RANKS * b + local)

                    for r in range(TOP_K):
                        link(dve.tensor_scalar(is_rank[:, r], rank[:, :, :], float(r), None, ALU.is_equal))
                    for r in range(TOP_K):
                        link(dve.tensor_tensor(picked[:, r], is_rank[:, r], score[:, :, :], ALU.mult))
                    wait_past(dve, gate_ok, b)
                    link(dve.tensor_reduce(score_of[:, :, :], picked[:, :, :, :], AX.X, ALU.add))
                    assert local == RANKS

                def place_block(b):
                    local = 0

                    def link(op):
                        nonlocal local
                        local += 1
                        op.then_inc(place_step, 1)
                        dve.wait_ge(place_step, PLACES * b + local)

                    dve.wait_ge(counted, b + 1)
                    link(dve.tensor_tensor(place[:, :, :], ps_b[:, 0:TB, :],
                                           base[:, :].unsqueeze(1).to_broadcast([P, TB, EXPERTS]), ALU.add))
                    link(dve.tensor_tensor(base[:, :], base[:, :], ps_b[:, TB, :], ALU.add))
                    for r in range(TOP_K):
                        link(dve.tensor_tensor(picked[:, r], is_rank[:, r], place[:, :, :], ALU.mult))
                    link(dve.tensor_reduce(place_of[:, :, :], picked[:, :, :, :], AX.X, ALU.add))
                    link(dve.tensor_copy(k["slot"][:, :, bass.ds(TB * b, TB)], place_of[:, :, :]))
                    assert local == PLACES

                def scale_rows(b, j):
                    dve.wait_ge(gate_ok, b + 1)
                    wait_past(dve, scattered, 16 * TOP_K * TB * b)
                    for s in range(TOP_K * TB):
                        r, t = s % TOP_K, s // TOP_K
                        dve.tensor_scalar(scaled[:, s, :], xn[:, j, t, :], gate[:, r, t:t + 1], None,
                                          ALU.mult).then_inc(scaled_ok, 1)

                table = 0

                def link(op):
                    nonlocal table
                    table += 1
                    op.then_inc(table_step, 1)
                    dve.wait_ge(table_step, table)

                def make_tables():
                    dve.tensor_copy(end_row[:, :], base[0:1, :]).then_inc(pad_ok, 1)
                    link(dve.tensor_tensor(count[:, :], base[:, :], region[:, :], ALU.subtract))
                    link(dve.tensor_scalar(padded[:, :], count[:, :], float(P - 1), None, ALU.add))
                    link(dve.tensor_scalar(padded[:, :], padded[:, :], -P, None, ALU.bitwise_and))
                    link(dve.tensor_copy(room[:, :], padded[:, :]))
                    link(dve.tensor_scalar(unused[:, :], room[:, :], -1.0, float(REGION), ALU.mult, ALU.add))
                    slots = k["slot"][:, :, :].rearrange("p r t -> p (r t)")
                    slot_shape = [P, TOP_K * TILES, EXPERTS - 1]
                    link(dve.tensor_copy(out_row[:, :], slots))
                    link(dve.tensor_tensor(moved[:, :, :], out_row[:, :].unsqueeze(2).to_broadcast(slot_shape),
                                           region[:, 1:EXPERTS].unsqueeze(1).to_broadcast(slot_shape), ALU.is_ge))
                    link(dve.tensor_tensor(moved[:, :, :], moved[:, :, :],
                                           unused[:, 0:EXPERTS - 1].unsqueeze(1).to_broadcast(slot_shape), ALU.mult))
                    link(dve.tensor_reduce(moved_sum[:, :], moved[:, :, :], AX.X, ALU.add))
                    link(dve.tensor_tensor(out_row[:, :], out_row[:, :], moved_sum[:, :], ALU.subtract))
                    link(dve.tensor_copy(k["out_slot"][:, :, :].rearrange("p r t -> p (r t)"), out_row[:, :]))
                    link(dve.tensor_tensor_scan(ends[:, :], room[:, :], zeros[:, 0:EXPERTS], 0.0, ALU.add, ALU.add))
                    dve.wait_ge(lo_ok, FC * BLOCKS)
                    table_shape = [1, SLOT_TILES, EXPERTS]
                    link(dve.tensor_tensor(passed_end[:, :, :], tile_start[:, :].unsqueeze(2).to_broadcast(table_shape),
                                           ends[0:1, :].unsqueeze(1).to_broadcast(table_shape), ALU.is_ge))
                    link(dve.tensor_reduce(expert[:, :], passed_end[:, :, :], AX.X, ALU.add))
                    link(dve.tensor_scalar(k["tile_expert"][:, :], expert[:, :], float(EXPERTS - 1), None, ALU.min))
                    link(dve.tensor_tensor(skipped[:, :, :], passed_end[:, :, :],
                                           unused[0:1, :].unsqueeze(1).to_broadcast(table_shape), ALU.mult))
                    link(dve.tensor_reduce(tile_row[:, :], skipped[:, :, :], AX.X, ALU.add))
                    link(dve.tensor_tensor(tile_row[:, :], tile_row[:, :], tile_start[:, :], ALU.add))
                    link(dve.tensor_scalar(k["tile_place"][:, :], tile_row[:, :], 1.0 / P, None, ALU.mult))

                def step(i, j, n):
                    if live(i):
                        add_rows(i, y_ok, 2 * i, added_ok)
                    if live(i - 1):
                        low_parts(dve, x_turn, i - 1, lambda c: xT_lo[:, 1 - j, c], lambda c: xT_hi[:, 1 - j, c])
                    if live(i):
                        hold(dve, k, added_ok, 2 * i + 2)
                        norm_measure(dve, norm, i, j)
                    if live(i - 2) and not is_last(i - 2, BLOCKS):
                        scale_rows(i - 2, j)
                    if isinstance(i, int) and i == BLOCKS + 1:
                        make_tables()
                    if live(i - 2):
                        add_rows(i - 2, s_ok, 2 * (i - 2), s_used)
                    if live(i + 1):
                        a_low(i + 1)
                    if live(i):
                        norm_apply(dve, norm, i, j, lambda t: xn[:, j, t:t + 1, :])
                    if live(i - 1):
                        for f in range(FC):
                            at = FC * (i - 1) + f
                            dve.wait_ge(silu_ok, at + 1)
                            dve.wait_ge(gated_ok, at + 1)
                            wait_past(dve, lo_ok, at_least(at - 1))
                            dve.tensor_tensor(h[:, f % 2], silu[:, f % 2], ps_g[:, :], ALU.mult).then_inc(h_ok, 1)
                            if f == 0:
                                rank_block(i - 1)
                            if f == 1:
                                chosen_scores(i - 1)
                        place_block(i - 1)
                        if is_last(i - 1, BLOCKS):
                            scale_rows(i - 1, 1 - j)
                    if isinstance(i, int) and i == 0:
                        for n, (raw, hi, lo) in enumerate(zip(s_raws, (wi_hi, wg_hi, wo_hi), (wi_lo, wg_lo, wo_lo))):
                            dve.wait_ge(s_high, n + 1)
                            dve.tensor_tensor(lo[:, :, :], raw, hi[:, :, :].bitcast(F32), ALU.subtract
                                              ).then_inc(s_split, 1)

                dve.sem_inc(s_used, 2)
                dve.wait_ge(w_in, 32)
                split_weights(dve, w_raw[:, :, :], w_hi[:, :, :], w_lo[:, :, :], w_split, 0)
                split_weights(dve, r_raw[:, :, :], router[:, :, 0, :], router[:, :, 1, :], w_split, 2)
                a_low(0)
                dve.wait_ge(made, 10)
                dve.tensor_copy(region[:, :], region_int[:, :])
                dve.tensor_copy(base[:, :], region_int[:, :])
                link(dve.tensor_copy(tile_start[:, :], start_int[:, :]))
                over_steps(dve, step)

            @block.tensor
            def _(pe):
                def turn_a(i, j, n):
                    pe.wait_ge(rows_in[j], 16 * GROUPS * (n + 1))
                    wait_past(pe, x_turn["lo_ok"], at_least(DC * (i - 1)))
                    turn_block(pe, a_turn, i, lambda t, c: rows[:, j, t, 2 * c:2 * c + 2, :].rearrange("p g c -> p (g c)"))

                def project(i, j):
                    pe.wait_ge(a_turn["lo_ok"], DC * i + DC)
                    for g in range(2):
                        wait_past(pe, s_used, at_least(2 * (i - 3) + g + 1 + 2))
                        wait_past(pe, added_ok, at_least(2 * (i - 1) + g + 1))
                        for t in (2 * g, 2 * g + 1):
                            for d in range(DC):
                                o = t * P
                                last = mm3(pe, ps_y[:, t], (aT_hi[:, d, o:o + P], aT_lo[:, d, o:o + P]),
                                           (w_hi[:, d], w_lo[:, d]), d == 0, d == DC - 1)
                        last.then_inc(y_ok, 1)

                def turn_x(i, j):
                    pe.wait_ge(norm["xn_ok"], i + 1)
                    if live(i + 1):
                        pe.wait_ge(a_turn["lo_ok"], DC * (i + 1) + DC)
                    turn_block(pe, x_turn, i, lambda t, c: xn[:, j, t, c * P:(c + 1) * P])

                def scores(i, j):
                    pe.wait_ge(x_turn["lo_ok"], DC * i + DC)
                    wait_past(pe, rank_step, at_least(RANKS * (i - 1) + 2))
                    for t in range(TB):
                        for d in range(DC):
                            at = slice(t * P, (t + 1) * P)
                            pe.matmul(ps_r[:, t], xT_hi[:, j, d, at], router[:, d], start=(d == 0), stop=False)
                            last = pe.matmul(ps_r[:, t, 0], xT_lo[:, j, d, at], router[:, d, 0], start=False,
                                             stop=(d == DC - 1))
                    last.then_inc(r_ok, 1)

                def count_rows(b):
                    pe.wait_ge(rank_step, RANKS * b + CHOSEN)
                    wait_past(pe, place_step, at_least(PLACES * (b - 1) + 2))
                    for t in range(TB + 1):
                        for u in range(min(t, TB - 1) + 1 if t < TB else TB):
                            last = pe.matmul(ps_b[:, t], before[:, :] if u == t else ones[:, :], chosen[:, u],
                                             start=(u == 0), stop=(u == min(t, TB - 1)))
                    last.then_inc(counted, 1)

                def expand(i, j, f):
                    at = FC * i + f
                    x = [(xT_hi[:, j, d], xT_lo[:, j, d]) for d in range(DC)]
                    for dst, hi, lo, used, sem in ((ps_m, wi_hi, wi_lo, silu_ok, mid_ok),
                                                   (ps_g, wg_hi, wg_lo, h_ok, gated_ok)):
                        wait_past(pe, used, at)
                        for d in range(DC):
                            last = mm3(pe, dst[:, :], (hi[:, d, f * P:(f + 1) * P], lo[:, d, f * P:(f + 1) * P]),
                                       x[d], d == 0, d == DC - 1)
                        last.then_inc(sem, 1)

                def contract(i):
                    pe.wait_ge(lo_ok, FC * i + FC)
                    for g in range(2):
                        if live(i + 2):
                            pe.wait_ge(added_ok, 2 * (i + 2) + g + 1)
                        else:
                            pe.wait_ge(s_used, 2 * (i - 1) + g + 1 + 2)
                        for t in (2 * g, 2 * g + 1):
                            for f in range(FC):
                                last = mm3(pe, ps_y[:, t], (h_hi[:, f, t * P:(t + 1) * P], h_lo[:, f, t * P:(t + 1) * P]),
                                           (wo_hi[:, f], wo_lo[:, f]), f == 0, f == FC - 1)
                        last.then_inc(s_ok, 1)

                def step(i, j, n):
                    if live(i):
                        project(i, j)
                    if live(i - 1):
                        turn_x(i - 1, 1 - j)
                    if live(i - 2):
                        contract(i - 2)
                    if live(i + 1):
                        turn_a(i + 1, 1 - j, n + j)
                    if live(i - 1):
                        scores(i - 1, 1 - j)
                        if isinstance(i, int) and i == 1:
                            pe.wait_ge(s_split, 3)
                        for f in range(FC):
                            expand(i - 1, 1 - j, f)
                        count_rows(i - 1)

                turn_a(0, 0, 0)
                pe.wait_ge(w_split, 4)
                over_steps(pe, step)


def phase_experts(k):
    nc, io = k["nc"], k["io"]
    with ExitStack() as mem:
        def sb(name, shape, dt):
            return mem.enter_context(nc.sbuf_tensor(name, shape, dt))

        def ps(name, shape, dt=F32):
            return mem.enter_context(nc.psum_tensor(name, shape, dt))

        wi_lo, wg_lo = k["we_in"], k["we_swiglu"]
        wi_hi, wg_hi = sb("we_in_hi", [P, EXPERTS, DC, FF], F32R), sb("we_swiglu_hi", [P, EXPERTS, DC, FF], F32R)
        wo = sb("we_out", [P, EXPERTS, FC, D], F32)
        rows = sb("slot_rows", [P, 2, D], F32)
        xT_hi, xT_lo = sb("slot_xT_hi", [P, DC, P], F32R), sb("slot_xT_lo", [P, DC, P], F32R)
        silu = sb("slot_silu", [P, FF], F32)
        h = sb("slot_h", [P, FF], F32)
        hT = sb("slot_hT", [P, FC, P], F32)
        y = sb("slot_y", [P, 2, D], F32)
        ps_x, ps_h, ps_y = ps("ps_xT", [P, DC, P]), ps("ps_hT", [P, FC, P]), ps("ps_slot_y", [P, D])
        ps_m, ps_g = ps("ps_slot_mid", [P, 2, FF]), ps("ps_slot_gated", [P, 2, FF])
        w_in = sem(k, "experts_w_in")
        rows_in, y_out = sems(k, "slot_rows_in", "even odd"), sems(k, "slot_y_out", "even odd")
        x_ok, x_high, x_low, mid_ok, gated_ok, silu_ok, h_ok, hps_ok, hT_ok, yps_ok, y_ok = sems(
            k, "slot", "x_ok x_high x_low mid_ok gated_ok silu_ok h_ok hps_ok hT_ok yps_ok y_ok")
        w_high, w_low = sems(k, "experts_split", "high low")
        halves = [(hi[:, e], lo[:, e]) for e in range(EXPERTS) for hi, lo in ((wi_hi, wi_lo), (wg_hi, wg_lo))]

        def low_weights(eng, own):
            for n, (hi, lo) in enumerate(halves):
                if (n % 3 == 2) == own:
                    eng.wait_ge(w_high, n + 1)
                    eng.tensor_tensor(lo, lo.bitcast(F32), hi.bitcast(F32), ALU.subtract).then_inc(w_low, 1)


        with nc.Block() as block:

            @block.sync
            def _(sp):
                src = io["slots_in"].rearrange("(s p) d -> s p d", p=P)

                def load(i, j):
                    at = sp.value_load(k["tile_place"][0:1, bass.ds(i, 1)], min_val=0, max_val=SLOTS // P - 1)
                    sp.dma_start(rows[:, j, :], src[bass.ds(at, 1)].rearrange("o p d -> p (o d)")
                                 ).then_inc(rows_in[j], 16)

                load(0, 0)
                load(1, 1)
                for e in range(EXPERTS):
                    sp.dma_start(wo[:, e], io["w_out_e"][e].rearrange("(c p) f -> p c f", p=P)).then_inc(w_in, 16)
                with sp.Fori(0, SLOT_TILES // 2 - 1) as n:
                    for j in range(2):
                        hold(sp, k, x_ok, 2 * n + j + 1)
                        load(2 * n + j + 2, j)

            @block.gpsimd
            def _(pool):
                low_weights(pool, True)
                dst = io["slots_out"].rearrange("(s p) d -> s p d", p=P)

                def store(i, j, n):
                    hold(pool, k, y_ok, i + 1)
                    pool.dma_start(dst[bass.ds(i, 1)].rearrange("o p d -> p (o d)"), y[:, j, :]).then_inc(y_out[j], 16)

                with pool.Fori(0, SLOT_TILES // 2) as n:
                    for j in range(2):
                        store(2 * n + j, j, n)
                for j in range(2):
                    pool.wait_ge(y_out[j], 16 * (SLOT_TILES // 2))

            @block.scalar
            def _(act):
                def turned(i, j):
                    act.wait_ge(x_ok, i + 1)
                    wait_past(act, gated_ok, i)
                    act.activation(xT_hi[:, :, :], ps_x[:, :, :], ACT.Copy).then_inc(x_high, 1)

                def result(i, j, n):
                    act.wait_ge(yps_ok, i + 1)
                    wait_past(act, y_out[j], 16 * n)
                    act.activation(y[:, j], ps_y[:, :], ACT.Copy).then_inc(y_ok, 1)

                def body(i, j, n):
                    act.wait_ge(mid_ok, i + 1)
                    wait_past(act, h_ok, i)
                    act.activation(silu[:, :], ps_m[:, j], ACT.Silu).then_inc(silu_ok, 1)
                    if not is_last(i, SLOT_TILES):
                        turned(i + 1, 1 - j)
                    if not is_first(i):
                        result(i - 1, 1 - j, n - (1 - j))

                act.wait_ge(k["experts_in"], 16 * 2 * EXPERTS)
                for hi, lo in halves:
                    act.activation(hi, lo.bitcast(F32), ACT.Copy).then_inc(w_high, 1)
                turned(0, 0)
                over_blocks(act, SLOT_TILES, body)
                result(SLOT_TILES - 1, 1, SLOT_TILES // 2 - 1)

            @block.vector
            def _(dve):
                def turned(i, j):
                    dve.wait_ge(hps_ok, i + 1)
                    wait_past(dve, yps_ok, i)
                    dve.tensor_copy(hT[:, :, :], ps_h[:, :, :]).then_inc(hT_ok, 1)

                def x_rest(i, j):
                    dve.wait_ge(x_high, i + 1)
                    dve.tensor_tensor(xT_lo[:, :, :], ps_x[:, :, :], xT_hi[:, :, :].bitcast(F32), ALU.subtract).then_inc(x_low, 1)

                def body(i, j, n):
                    if not is_first(i):
                        turned(i - 1, 1 - j)
                    dve.wait_ge(silu_ok, i + 1)
                    dve.wait_ge(gated_ok, i + 1)
                    dve.tensor_tensor(h[:, :], silu[:, :], ps_g[:, j], ALU.mult).then_inc(h_ok, 1)
                    if not is_last(i, SLOT_TILES):
                        x_rest(i + 1, 1 - j)

                low_weights(dve, False)
                x_rest(0, 0)
                over_blocks(dve, SLOT_TILES, body)
                turned(SLOT_TILES - 1, 1)

            @block.tensor
            def _(pe):
                def expert_of(i):
                    return pe.value_load(k["tile_expert"][0:1, bass.ds(i, 1)],
                                         min_val=0, max_val=EXPERTS - 1)

                def turn_x(i, j, n):
                    pe.wait_ge(rows_in[j], 16 * n + 16)
                    wait_past(pe, x_low, i)
                    for c in range(DC):
                        last = pe.transpose(ps_x[:, c], rows[:, j, c * P:(c + 1) * P], k["ident"][:, :])
                    last.then_inc(x_ok, 1)

                def expand(i, j, e, dst, hi, lo, sem):
                    for d in range(DC):
                        last = mm3(pe, dst[:, j], (xT_hi[:, d], xT_lo[:, d]),
                                   (hi[:, bass.ds(e, 1), d, :], lo[:, bass.ds(e, 1), d, :]), d == 0, d == DC - 1)
                    last.then_inc(sem, 1)

                def turn_h(i, j):
                    pe.wait_ge(h_ok, i + 1)
                    wait_past(pe, hT_ok, i)
                    for f in range(FC):
                        last = pe.transpose(ps_h[:, f], h[:, f * P:(f + 1) * P], k["ident"][:, :])
                    last.then_inc(hps_ok, 1)

                def contract(i, j):
                    e = expert_of(i)
                    if is_first(i):
                        pe.wait_ge(w_in, 16 * EXPERTS)
                    pe.wait_ge(hT_ok, i + 1)
                    wait_past(pe, y_ok, i)
                    for f in range(FC):
                        last = pe.matmul(ps_y[:, :], hT[:, f], wo[:, bass.ds(e, 1), f, :],
                                         start=(f == 0), stop=(f == FC - 1))
                    last.then_inc(yps_ok, 1)

                def body(i, j, n):
                    e = expert_of(i)
                    pe.wait_ge(x_low, i + 1)
                    wait_past(pe, h_ok, at_least(i - 1))
                    expand(i, j, e, ps_m, wi_hi, wi_lo, mid_ok)
                    if not is_first(i):
                        turn_h(i - 1, 1 - j)
                    expand(i, j, e, ps_g, wg_hi, wg_lo, gated_ok)
                    if not is_last(i, SLOT_TILES):
                        turn_x(i + 1, 1 - j, n + j)
                    if not is_first(i):
                        contract(i - 1, 1 - j)

                turn_x(0, 0, 0)
                pe.wait_ge(w_low, len(halves))
                over_blocks(pe, SLOT_TILES, body)
                turn_h(SLOT_TILES - 1, 1)
                contract(SLOT_TILES - 1, 1)


SEQ_TILES = SEQ // P
SEQ_BLOCKS = SEQ // BT


def phase_keys(k, b):
    nc, io = k["nc"], k["io"]
    with ExitStack() as mem:
        def sb(name, shape, dt):
            return mem.enter_context(nc.sbuf_tensor(name + str(b), shape, dt))

        def ps(name, shape, dt=F32):
            return mem.enter_context(nc.psum_tensor(name + str(b), shape, dt))

        w_raw = sb("kv_raw", [P, DC, 2 * D], F32)
        w_hi, w_lo = sb("kv_hi", [P, DC, 2 * D], F32R), sb("kv_lo", [P, DC, 2 * D], F32R)
        back = None if b else sb("back", [P, 2, TOP_K, TB, D], F32)
        xn = sb("xn3", [P, SEQ_BLOCKS, TB, D], F32)
        ps_t, ps_k, ps_v = ps("ps_x3", [P, DC, BT]), ps("ps_k3", [P, DC, BT]), ps("ps_v3", [P, TB, D])
        if b:
            size, gamma = sb("abs_sum", [P, 2], F32), sb("gamma", [P, 2], F32)
            absolute, ones = sb("absolute", [P, D * D_FF // P], F32), sb("ones_f32", [P, P], F32)
            ps_g = ps("ps_gamma", [P, 2])
            v_raw = sb("v3_raw", [P, 2, 2, D], F32)
        norm = layer_norm(k, mem, f"ln3_{b}")
        x_turn = turner(k, f"x3_turn{b}", ps_t)
        w_in, w_split, sum_ok, k_ok, k_hi, k_lo, v_ok, v_hi, v_lo = sems(
            k, f"keys{b}", "w_in w_split sum_ok k_ok k_hi k_lo v_ok v_hi v_lo")
        back_in = [sems(k, f"back_in{b}_{n}", "even odd") for n in range(TOP_K)]
        mlp_in, size_ok, summed, ones_ok, gamma_ok = sems(k, f"ternary{b}", "mlp_in size_ok summed ones_ok gamma_ok")
        T0 = b * SEQ_TILES

        def v_rest(eng, i):
            for g in range(2):
                eng.wait_ge(v_hi, 2 * i + g + 1)
                t = TB * i + 2 * g
                full = v_raw[:, g] if b else ps_v[:, 2 * g:2 * g + 2, :]
                eng.tensor_tensor(k["v_lo"][:, t:t + 2, :], full, k["v_hi"][:, t:t + 2, :].bitcast(F32), ALU.subtract).then_inc(v_lo, 1)

        with nc.Block() as block:

            @block.sync
            def _(sp):
                sp.dma_start(w_raw[:, :, :], io["w_kv"].rearrange("(c p) n -> p c n", p=P)).then_inc(w_in, 16)
                if b:
                    for m, name in enumerate(("w1", "w2")):
                        sp.dma_start(k["mlp_raw"][m], io[name].rearrange("(c p) n -> p c n", p=P)).then_inc(mlp_in, 16)

            @block.gpsimd
            def _(pool):
                def residual(i):
                    x = k["X"][:, T0 + TB * i:T0 + TB * i + TB, :]
                    pool.wait_ge(norm["xn_ok"], i + 1)
                    pool.tensor_tensor(x, x, xn[:, i], ALU.add).then_inc(k["residual_ok"], 1)

                if b:
                    pool.memset(ones[:, :], 1.0).then_inc(ones_ok, 1)
                for i in range(SEQ_BLOCKS):
                    if b:
                        residual(i)
                        v_rest(pool, i)
                        continue
                    if i >= 2:
                        pool.wait_ge(sum_ok, 2 * i - 2)
                    for r in range(TOP_K):
                        for t in range(TB):
                            T = T0 + TB * i + t
                            pool.indirect_dma_start(
                                out=back[:, i % 2, r, t, :], out_offset=None, in_=io["slots_out"],
                                in_offset=bass.IndirectOffsetOnAxis(ap=k["out_slot"][:, r, T:T + 1], axis=0)
                            ).then_inc(back_in[r][i % 2], 16)
                if not b:
                    for i in range(SEQ_BLOCKS):
                        residual(i)

            @block.scalar
            def _(act):
                def q_high(i):
                    high_parts(act, x_turn, i, lambda c: k["qT_hi"][:, c, i * BT:(i + 1) * BT])

                norm_root(act, norm, 0, 0)
                q_high(0)
                norm_root(act, norm, 1, 1)
                for i in range(SEQ_BLOCKS):
                    for c in range(DC):
                        act.wait_ge(k_ok, DC * i + c + 1)
                        act.activation(k["kT_hi"][:, c, i * BT:(i + 1) * BT], ps_k[:, c], ACT.Copy).then_inc(k_hi, 1)
                    if i + 1 < SEQ_BLOCKS:
                        q_high(i + 1)
                    if not b and i + 2 < SEQ_BLOCKS:
                        norm_root(act, norm, i + 2, i % 2)
                    for g in range(2):
                        act.wait_ge(v_ok, 2 * i + g + 1)
                        t = TB * i + 2 * g
                        if b:
                            if i:
                                act.wait_ge(v_lo, 2 * (i - 1) + g + 1)
                            act.activation(v_raw[:, g], ps_v[:, 2 * g:2 * g + 2, :], ACT.Copy)
                        act.activation(k["v_hi"][:, t:t + 2, :], ps_v[:, 2 * g:2 * g + 2, :], ACT.Copy).then_inc(v_hi, 1)
                    if b and i + 2 < SEQ_BLOCKS:
                        norm_root(act, norm, i + 2, i % 2)
                if b:
                    act.wait_ge(mlp_in, 32)
                    for m in range(2):
                        if m:
                            act.wait_ge(size_ok, m)
                        act.activation(absolute[:, :], k["mlp_raw"][m].rearrange("p c n -> p (c n)"), ACT.Abs,
                                       accum_out=size[:, m:m + 1]).then_inc(size_ok, 1)

            @block.vector
            def _(dve):
                def normed(i):
                    j = i % 2
                    x = k["X"][:, T0 + TB * i:T0 + TB * i + TB, :]
                    if not b:
                        for r in range(TOP_K):
                            dve.wait_ge(back_in[r][j], 16 * TB * (i // 2 + 1))
                            dve.tensor_tensor(x, x, back[:, j, r], ALU.add).then_inc(sum_ok, 1)
                            dve.wait_ge(sum_ok, 2 * i + r + 1)
                    norm_measure(dve, norm, i, j, T0)
                    norm_apply(dve, norm, i, j, lambda t: xn[:, i, t:t + 1, :], T0)

                def split():
                    dve.wait_ge(w_in, 16)
                    split_weights(dve, w_raw[:, :, :], w_hi[:, :, :], w_lo[:, :, :], w_split, 0)

                def q_low(i):
                    low_parts(dve, x_turn, i, lambda c: k["qT_lo"][:, c, i * BT:(i + 1) * BT],
                              lambda c: k["qT_hi"][:, c, i * BT:(i + 1) * BT])

                if not b:
                    split()
                normed(0)
                if b:
                    split()
                q_low(0)
                normed(1)
                for i in range(SEQ_BLOCKS):
                    at = slice(i * BT, (i + 1) * BT)
                    for c in range(DC):
                        dve.wait_ge(k_hi, DC * i + c + 1)
                        dve.tensor_tensor(k["kT_lo"][:, c, at], ps_k[:, c], k["kT_hi"][:, c, at].bitcast(F32),
                                          ALU.subtract).then_inc(k_lo, 1)
                    if i + 1 < SEQ_BLOCKS:
                        q_low(i + 1)
                    if i + 2 < SEQ_BLOCKS:
                        normed(i + 2)
                    if not b:
                        v_rest(dve, i)

                if b:
                    dve.wait_ge(summed, 1)
                    dve.tensor_scalar(gamma[:, :], ps_g[:, :], 1.0 / (D * D_FF), EPS, ALU.mult, ALU.add).then_inc(gamma_ok, 1)
                    dve.wait_ge(gamma_ok, 1)
                    for n, sign in enumerate((0.5, -0.5)):
                        dve.tensor_scalar(k["half_gamma"][:, n, :], gamma[:, :], sign, None, ALU.mult).then_inc(gamma_ok, 1)

            @block.tensor
            def _(pe):
                def turn(i):
                    pe.wait_ge(norm["xn_ok"], i + 1)
                    turn_block(pe, x_turn, i, lambda t, c: xn[:, i, t, c * P:(c + 1) * P])

                turn(0)
                pe.wait_ge(w_split, 2)
                for i in range(SEQ_BLOCKS):
                    pe.wait_ge(x_turn["lo_ok"], DC * i + DC)
                    for c in range(DC):
                        wait_past(pe, k_lo, DC * (i - 1) + c + 1)
                        for d in range(DC):
                            at = slice(i * BT, (i + 1) * BT)
                            last = mm3(pe, ps_k[:, c], (w_hi[:, d, c * P:(c + 1) * P], w_lo[:, d, c * P:(c + 1) * P]),
                                       (k["qT_hi"][:, d, at], k["qT_lo"][:, d, at]), d == 0, d == DC - 1)
                        last.then_inc(k_ok, 1)
                    if i + 1 < SEQ_BLOCKS:
                        turn(i + 1)
                    for g in range(2):
                        wait_past(pe, v_hi if b else v_lo, 2 * (i - 1) + g + 1)
                        for t in (2 * g, 2 * g + 1):
                            for d in range(DC):
                                at = slice(i * BT + t * P, i * BT + (t + 1) * P)
                                last = mm3(pe, ps_v[:, t], (k["qT_hi"][:, d, at], k["qT_lo"][:, d, at]),
                                           (w_hi[:, d, D:2 * D], w_lo[:, d, D:2 * D]), d == 0, d == DC - 1)
                        last.then_inc(v_ok, 1)
                if b:
                    pe.wait_ge(ones_ok, 1)
                    pe.wait_ge(size_ok, 2)
                    pe.matmul(ps_g[:, :], ones[:, :], size[:, :], start=True, stop=True).then_inc(summed, 1)


CUTS = SEQ_TILES // 4
CUT = D * D_FF // P // CUTS


def phase_attend(k, b):
    nc, io = k["nc"], k["io"]
    with ExitStack() as mem:
        def sb(name, shape, dt):
            return mem.enter_context(nc.sbuf_tensor(name + str(b), shape, dt))

        def ps(name, shape, dt=F32):
            return mem.enter_context(nc.psum_tensor(name + str(b), shape, dt))

        chunk_top = sb("chunk_max", [P, SEQ_TILES, SEQ_BLOCKS], F32)
        chunk_total = sb("chunk_sum", [P, SEQ_TILES, SEQ_BLOCKS], F32)
        top = sb("row_max", [P, SEQ_TILES], F32)
        neg_top = sb("neg_row_max", [P, SEQ_TILES], F32)
        total = sb("row_sum", [P, SEQ_TILES], F32)
        inv = sb("inv_row_sum", [P, SEQ_TILES], F32)
        probs = sb("probs3", [P, 2, SEQ], F32)
        pT_hi, pT_lo = sb("pT_hi", [P, 2, TB, P], F32R), sb("pT_lo", [P, 2, TB, P], F32R)
        back = None if b else sb("next_back", [P, TOP_K, SEQ_TILES, D], F32)
        ps_s, ps_t, ps_o = ps("ps_s3", [P, SEQ]), ps("ps_p3", [P, 2, TB, P]), ps("ps_o3", [P, 2, BT])
        s_ok, masked_ok, chunk_ok, top_ok, neg_ok, exp_ok = sems(
            k, f"attend{b}", "s_ok masked_ok chunk_ok top_ok neg_ok exp_ok")
        t_ok, hi_ok, lo_ok, pv_ok, total_ok, inv_ok, used_ok = sems(
            k, f"attend{b}", "t_ok hi_ok lo_ok pv_ok total_ok inv_ok used_ok")
        below = sb("below", [P, CUT], F32) if b else None
        cut_ok = sem(k, f"ternary_cut{b}")
        back_in, summed = sems(k, f"next_rows{b}", "back_in summed")
        T0 = b * SEQ_TILES
        PARTS = [(q, g, min(TB, q + 1 - g)) for q in range(SEQ_TILES) for g in range(0, q + 1, TB)]
        OF = [[n for n, part in enumerate(PARTS) if part[0] == q] for q in range(SEQ_TILES)]

        with nc.Block() as block:

            if not b:
                @block.gpsimd
                def _(pool):
                    for r in range(TOP_K):
                        for t in range(SEQ_TILES):
                            T = T0 + SEQ_TILES + t
                            pool.indirect_dma_start(
                                out=back[:, r, t, :], out_offset=None, in_=io["slots_out"],
                                in_offset=bass.IndirectOffsetOnAxis(ap=k["out_slot"][:, r, T:T + 1], axis=0)
                            ).then_inc(back_in, 16)
                    pool.wait_ge(back_in, 16 * TOP_K * SEQ_TILES)
                    for i in range(SEQ_BLOCKS):
                        x = k["X"][:, T0 + SEQ_TILES + TB * i:T0 + SEQ_TILES + TB * i + TB, :]
                        for r in range(TOP_K):
                            pool.tensor_tensor(x, x, back[:, r, TB * i:TB * i + TB, :], ALU.add).then_inc(summed, 1)
                            pool.wait_ge(summed, TOP_K * i + r + 1)

            @block.vector
            def _(dve):
                def ternary(n):
                    m, at = n // 2 // CUTS, n // 2 % CUTS * CUT
                    raw = k["mlp_raw"][m].rearrange("p c n -> p (c n)")[:, at:at + CUT]
                    out = k["mlp_ternary"][m].rearrange("p c n -> p (c n)")[:, at:at + CUT]
                    if n:
                        dve.wait_ge(cut_ok, n)
                    if n % 2 == 0:
                        op = dve.tensor_scalar(below[:, :], raw, k["half_gamma"][:, 1, m:m + 1], None, ALU.is_lt)
                    else:
                        op = dve.scalar_tensor_tensor(out=out, in0=raw, scalar=k["half_gamma"][:, 0, m:m + 1],
                                                      in1=below[:, :], op0=ALU.is_gt, op1=ALU.subtract)
                    op.then_inc(cut_ok, 1)

                def soften(q):
                    for n in OF[q]:
                        _, g, m = PARTS[n]
                        dve.wait_ge(s_ok, n + 1)
                        if n == OF[q][-1]:
                            diag = ps_s[:, q * P:(q + 1) * P]
                            dve.tensor_tensor(diag, diag, k["causal"][:, :], ALU.add).then_inc(masked_ok, 1)
                            dve.wait_ge(masked_ok, q + 1)
                        dve.tensor_reduce(chunk_top[:, q, g // TB:g // TB + 1], ps_s[:, g * P:(g + m) * P], AX.X,
                                          ALU.max).then_inc(chunk_ok, 1)
                    dve.wait_ge(chunk_ok, OF[q][-1] + 1)
                    dve.tensor_reduce(top[:, q:q + 1], chunk_top[:, q, 0:len(OF[q])], AX.X, ALU.max).then_inc(top_ok, 1)
                    dve.wait_ge(top_ok, q + 1)
                    dve.tensor_scalar(neg_top[:, q:q + 1], top[:, q:q + 1], -1.0, None, ALU.mult).then_inc(neg_ok, 1)

                def lows(n):
                    dve.wait_ge(hi_ok, n + 1)
                    m = PARTS[n][2]
                    dve.tensor_tensor(pT_lo[:, n % 2, 0:m], ps_t[:, n % 2, 0:m], pT_hi[:, n % 2, 0:m].bitcast(F32),
                                      ALU.subtract).then_inc(lo_ok, 1)

                soften(0)
                for q in range(SEQ_TILES):
                    for n in OF[q][:2]:
                        lows(n)
                    if q + 1 < SEQ_TILES:
                        soften(q + 1)
                    for n in OF[q][2:]:
                        lows(n)
                    if b:
                        ternary(q)
                    dve.wait_ge(exp_ok, OF[q][-1] + 1)
                    dve.tensor_reduce(total[:, q:q + 1], chunk_total[:, q, 0:len(OF[q])], AX.X, ALU.add
                                      ).then_inc(total_ok, 1)
                    dve.wait_ge(total_ok, q + 1)
                    dve.reciprocal(inv[:, q:q + 1], total[:, q:q + 1]).then_inc(inv_ok, 1)
                    dve.wait_ge(pv_ok, OF[q][-1] + 1)
                    dve.wait_ge(inv_ok, q + 1)
                    x = k["X"][:, T0 + q, :]
                    dve.scalar_tensor_tensor(out=x, in0=ps_o[:, q % 2, 0:D], scalar=inv[:, q:q + 1], in1=x,
                                             op0=ALU.mult, op1=ALU.add).then_inc(used_ok, 1)

            @block.scalar
            def _(act):
                def weigh(n):
                    q, g, m = PARTS[n]
                    if n == OF[q][0]:
                        act.wait_ge(neg_ok, q + 1)
                        if q >= 2:
                            act.wait_ge(t_ok, OF[q - 2][-1] + 1)
                    act.activation(probs[:, q % 2, g * P:(g + m) * P], ps_s[:, g * P:(g + m) * P], ACT.Exp,
                                   bias=neg_top[:, q:q + 1], accum_out=chunk_total[:, q, g // TB:g // TB + 1]
                                   ).then_inc(exp_ok, 1)

                def high(n):
                    m = PARTS[n][2]
                    act.wait_ge(t_ok, n + 1)
                    if n >= 2:
                        act.wait_ge(pv_ok, n - 1)
                    act.activation(pT_hi[:, n % 2, 0:m], ps_t[:, n % 2, 0:m], ACT.Copy).then_inc(hi_ok, 1)

                weigh(0)
                for q in range(SEQ_TILES):
                    following = list(OF[q + 1]) if q + 1 < SEQ_TILES else []
                    for n in OF[q][:2]:
                        high(n)
                    for at in range(max(len(following), len(OF[q]) - 2)):
                        if at < len(following):
                            weigh(following[at])
                        if at + 2 < len(OF[q]):
                            high(OF[q][at + 2])

            @block.tensor
            def _(pe):
                def score(q):
                    for n in OF[q]:
                        _, g, m = PARTS[n]
                        if q and n - OF[q][0] < len(OF[q - 1]):
                            pe.wait_ge(exp_ok, OF[q - 1][n - OF[q][0]] + 1)
                        for d in range(DC):
                            at = slice(q * P, (q + 1) * P)
                            to = slice(g * P, (g + m) * P)
                            last = mm3(pe, ps_s[:, to], (k["qT_hi"][:, d, at], k["qT_lo"][:, d, at]),
                                       (k["kT_hi"][:, d, to], k["kT_lo"][:, d, to]), d == 0, d == DC - 1)
                        last.then_inc(s_ok, 1)

                def turn(n):
                    q, g, m = PARTS[n]
                    pe.wait_ge(exp_ok, n + 1)
                    if n >= 2:
                        pe.wait_ge(lo_ok, n - 1)
                    for t in range(m):
                        last = pe.transpose(ps_t[:, n % 2, t], probs[:, q % 2, (g + t) * P:(g + t + 1) * P],
                                            k["ident"][:, :])
                    last.then_inc(t_ok, 1)

                def weigh(n):
                    q, g, m = PARTS[n]
                    pe.wait_ge(lo_ok, n + 1)
                    if g == 0 and q >= 2:
                        pe.wait_ge(used_ok, q - 1)
                    for t in range(m):
                        last = mm3(pe, ps_o[:, q % 2, 0:D], (pT_hi[:, n % 2, t], pT_lo[:, n % 2, t]),
                                   (k["v_hi"][:, g + t], k["v_lo"][:, g + t]), g + t == 0, g + t == q)
                    last.then_inc(pv_ok, 1)

                score(0)
                for q in range(SEQ_TILES):
                    for n in OF[q][:2]:
                        turn(n)
                    if q + 1 < SEQ_TILES:
                        score(q + 1)
                    for n in OF[q]:
                        weigh(n)
                        if n + 2 in OF[q]:
                            turn(n + 2)


def phase_mlp(k):
    nc, io = k["nc"], k["io"]
    FC4 = D_FF // P
    with ExitStack() as mem:
        def sb(name, shape, dt):
            return mem.enter_context(nc.sbuf_tensor(name, shape, dt))

        def ps(name, shape, dt=F32):
            return mem.enter_context(nc.psum_tensor(name, shape, dt))

        w1, w2 = k["mlp_ternary"]
        b1 = sb("b1_columns", [P, FC4], F32)
        b2 = sb("b2_rows", [P, D], F32)
        xn = sb("xn4", [P, 2, TB, D], F32)
        xT_hi, xT_lo = sb("x4T_hi", [P, 2, DC, BT], F32R), sb("x4T_lo", [P, 2, DC, BT], F32R)
        h = sb("h4", [P, 2, BT], F32)
        h_hi, h_lo = sb("h4_hi", [P, 2, FC4, BT], F32R), sb("h4_lo", [P, 2, FC4, BT], F32R)
        y = sb("y4", [P, 2, TB, D], F32)
        ps_t, ps_h, ps_y = ps("ps_x4", [P, DC, BT]), ps("ps_h4", [P, 3, BT]), ps("ps_y4", [P, TB, D])
        norm = layer_norm(k, mem, "ln4")
        x_turn = turner(k, "x4_turn", ps_t)
        b_in, res_ok = sems(k, "mlp", "b_in res_ok")
        hps_ok, hi_ok, h_ok, lo_ok, yps_ok, y_ok = sems(k, "mlp", "hps_ok hi_ok h_ok lo_ok yps_ok y_ok")
        y_out = sems(k, "y_out", "even odd")

        with nc.Block() as block:

            @block.sync
            def _(sp):
                sp.dma_start(b1[:, :], io["b1"]).then_inc(b_in, 16)
                sp.dma_start(b2[:, :], io["b2"].to_broadcast([P, D])).then_inc(b_in, 16)
                out = io["out"].rearrange("(n p) d -> p n d", p=P)
                for i in range(BLOCKS):
                    sp.wait_ge(y_ok, 2 * i + 2)
                    sp.dma_start(out[:, TB * i:TB * i + TB, :], y[:, i % 2]).then_inc(y_out[i % 2], 16)
                for j in range(2):
                    sp.wait_ge(y_out[j], 16 * (BLOCKS // 2))

            @block.gpsimd
            def _(pool):
                def body(i, j, n):
                    for f in range(FC4):
                        at = FC4 * i + f
                        pool.wait_ge(h_ok, at + 1)
                        pool.tensor_tensor(h_lo[:, j, f], h[:, f % 2], h_hi[:, j, f].bitcast(F32), ALU.subtract
                                           ).then_inc(lo_ok, 1)

                over_blocks(pool, BLOCKS, body)

            @block.scalar
            def _(act):
                norm_root(act, norm, 0, 0)
                high_parts(act, x_turn, 0, lambda c: xT_hi[:, 0, c])
                act.wait_ge(b_in, 32)

                def body(i, j, n):
                    if not is_last(i, BLOCKS):
                        norm_root(act, norm, i + 1, 1 - j)
                    wait_past(act, yps_ok, at_least(2 * (i - 1)))
                    for f in range(FC4):
                        act.wait_ge(hps_ok, FC4 * i + f + 1)
                        act.activation(h_hi[:, j, f], ps_h[:, f % 3], ACT.Relu, bias=b1[:, f:f + 1]).then_inc(hi_ok, 1)
                        if f == 6 and not is_last(i, BLOCKS):
                            high_parts(act, x_turn, i + 1, lambda c: xT_hi[:, 1 - j, c])

                over_blocks(act, BLOCKS, body)

            @block.vector
            def _(dve):
                norm_measure(dve, norm, 0, 0)
                norm_apply(dve, norm, 0, 0, lambda t: xn[:, 0, t:t + 1, :])

                def x_low(i, j):
                    low_parts(dve, x_turn, i, lambda c: xT_lo[:, j, c], lambda c: xT_hi[:, j, c])

                def result(i, j, n, g):
                    if g == 0:
                        wait_past(dve, y_out[j], 16 * n)
                    dve.wait_ge(res_ok, i + 1)
                    dve.wait_ge(yps_ok, 2 * i + g + 1)
                    dve.tensor_tensor(y[:, j, 2 * g:2 * g + 2], ps_y[:, 2 * g:2 * g + 2],
                                      k["X"][:, bass.ds(TB * i + 2 * g, 2), :], ALU.add).then_inc(y_ok, 1)

                def body(i, j, n):
                    if not is_last(i, BLOCKS):
                        norm_measure(dve, norm, i + 1, 1 - j)
                    for f in range(FC4):
                        at = FC4 * i + f
                        dve.wait_ge(hi_ok, at + 1)
                        wait_past(dve, lo_ok, at - 1)
                        dve.tensor_scalar(h[:, f % 2], ps_h[:, f % 3], b1[:, f:f + 1], 0.0, ALU.add, ALU.max
                                          ).then_inc(h_ok, 1)
                        if f == 1:
                            x = k["X"][:, bass.ds(TB * i, TB), :]
                            dve.tensor_tensor(x, x, b2[:, :].unsqueeze(1).to_broadcast([P, TB, D]), ALU.add
                                              ).then_inc(res_ok, 1)
                        if f == 3 and not is_last(i, BLOCKS):
                            norm_apply(dve, norm, i + 1, 1 - j, lambda t: xn[:, 1 - j, t:t + 1, :])
                        if f == 5 and not is_first(i):
                            result(i - 1, 1 - j, n - (1 - j), 0)
                        if f == 6 and not is_last(i, BLOCKS):
                            x_low(i + 1, 1 - j)
                    if not is_first(i):
                        result(i - 1, 1 - j, n - (1 - j), 1)

                x_low(0, 0)
                dve.wait_ge(b_in, 32)
                over_blocks(dve, BLOCKS, body)
                for g in range(2):
                    result(BLOCKS - 1, 1, BLOCKS // 2 - 1, g)

            @block.tensor
            def _(pe):
                def turn(i, j):
                    pe.wait_ge(norm["xn_ok"], i + 1)
                    turn_block(pe, x_turn, i, lambda t, c: xn[:, j, t, c * P:(c + 1) * P])

                def contract(i, j, part):
                    t, half = part // 2, part % 2
                    if t % 2 == 0 and half == 0:
                        wait_past(pe, y_ok, at_least(2 * (i - 1) + t // 2 + 1))
                    for f in range(half * FC4 // 2, (half + 1) * FC4 // 2):
                        if part == 0 or t == 0:
                            pe.wait_ge(lo_ok, FC4 * i + f + 1)
                        pe.matmul(ps_y[:, t], h_hi[:, j, f, t * P:(t + 1) * P], w2[:, f], start=(f == 0), stop=False)
                        last = pe.matmul(ps_y[:, t], h_lo[:, j, f, t * P:(t + 1) * P], w2[:, f], start=False,
                                         stop=(f == FC4 - 1))
                    if t % 2 and half:
                        last.then_inc(yps_ok, 1)

                def body(i, j, n):
                    pe.wait_ge(x_turn["lo_ok"], DC * i + DC)
                    for f in range(FC4):
                        wait_past(pe, h_ok, FC4 * i + f - (1 if f < 2 else 2))
                        for d in range(DC):
                            w = w1[:, d, f * P:(f + 1) * P]
                            pe.matmul(ps_h[:, f % 3], w, xT_hi[:, j, d], start=(d == 0), stop=False)
                            last = pe.matmul(ps_h[:, f % 3], w, xT_lo[:, j, d], start=False, stop=(d == DC - 1))
                        last.then_inc(hps_ok, 1)
                        if not is_first(i):
                            contract(i - 1, 1 - j, f)
                        if f == 5 and not is_last(i, BLOCKS):
                            turn(i + 1, 1 - j)

                turn(0, 0)
                over_blocks(pe, BLOCKS, body)
                for part in range(2 * TB):
                    contract(BLOCKS - 1, 1, part)


def program(nc, io):
    io = dict(io)

    def scratch(name, shape, dt):
        return nc.dram_tensor(name, shape, dt, kind="Internal").ap()

    io["qk"] = scratch("qk_parts", (3, BATCH, 2, GROUPS, HG * DH, SEQ), BF16)
    io["shift"] = scratch("shift_parts", (3, GROUPS, BATCH, HG, SEQ), BF16)
    io["attended"] = scratch("attended", (GROUPS, BATCH, SEQ, HG * DH), F32)
    io["slots_in"] = scratch("slots_in", (SLOTS, D), F32)
    io["slots_out"] = scratch("slots_out", (OUT_SLOTS, D), F32)
    with ExitStack() as ctx:
        k = {"nc": nc, "io": io}
        k["passed"], k["residual_ok"] = (ctx.enter_context(nc.semaphore(name)) for name in ("passed", "residual_ok"))
        k["X"] = ctx.enter_context(nc.sbuf_tensor("X", [P, TILES, D], F32))
        k["ident"] = ctx.enter_context(nc.sbuf_tensor("ident", [P, P], F32))
        k["causal"] = ctx.enter_context(nc.sbuf_tensor("causal", [P, P], F32))
        k["head_sel"] = ctx.enter_context(nc.sbuf_tensor("head_sel", [P, P // DH], BF16))
        k["eps"] = ctx.enter_context(nc.sbuf_tensor("eps", [P, 1], F32))
        k["unsafe"] = ctx.enter_context(nc.sbuf_tensor("unsafe", [1, 1], I32))
        k["slot"] = ctx.enter_context(nc.sbuf_tensor("slot", [P, TOP_K, TILES], I32))
        k["out_slot"] = ctx.enter_context(nc.sbuf_tensor("out_slot", [P, TOP_K, TILES], I32))
        k["tile_expert"] = ctx.enter_context(nc.sbuf_tensor("tile_expert", [1, SLOT_TILES], I32))
        k["tile_place"] = ctx.enter_context(nc.sbuf_tensor("tile_place", [1, SLOT_TILES], I32))
        with ExitStack() as mem, semaphores(k):
            k["V"] = mem.enter_context(nc.sbuf_tensor("V", [P, GROUPS, TILES, HG, DH + 1], F32))
            k["first_stacks"] = [mem.enter_context(nc.sbuf_tensor(name, [P, HG, SEQ], BF16)) for name in ("Q_even", "K_even")]
            k["loaded"] = sems(k, "unit_loaded", "even odd")
            phase_constants(k)
            phase_qkv(k)
            phase_shift(k)
            phase_attention(k)
        with ExitStack() as mem, semaphores(k):
            k["we_in"] = mem.enter_context(nc.sbuf_tensor("we_in", [P, EXPERTS, DC, FF], F32R))
            k["we_swiglu"] = mem.enter_context(nc.sbuf_tensor("we_swiglu", [P, EXPERTS, DC, FF], F32R))
            k["experts_in"] = sem(k, "experts_in")
            phase_tokens(k)
            phase_experts(k)
        k["mlp_ternary"] = [ctx.enter_context(nc.sbuf_tensor("w1_ternary", [P, DC, D_FF], F32R))[:, :, :],
                            ctx.enter_context(nc.sbuf_tensor("w2_ternary", [P, D_FF // P, D], F32R))[:, :, :]]
        with semaphores(k):
            for b in range(BATCH):
              with ExitStack() as mem:
                  def sb(name, shape, dt=F32R):
                      return mem.enter_context(nc.sbuf_tensor(name + str(b), shape, dt))

                  k["qT_hi"], k["qT_lo"] = sb("q3T_hi", [P, DC, SEQ]), sb("q3T_lo", [P, DC, SEQ])
                  k["kT_hi"], k["kT_lo"] = sb("k3T_hi", [P, DC, SEQ]), sb("k3T_lo", [P, DC, SEQ])
                  k["v_hi"], k["v_lo"] = sb("v3_hi", [P, SEQ_TILES, D]), sb("v3_lo", [P, SEQ_TILES, D])
                  if b == BATCH - 1:
                      k["mlp_raw"] = [sb("w1_raw", [P, DC, D_FF], F32)[:, :, :], sb("w2_raw", [P, D_FF // P, D], F32)[:, :, :]]
                      k["half_gamma"] = sb("half_gamma", [P, 2, 2], F32)
                  phase_keys(k, b)
                  phase_attend(k, b)
            phase_mlp(k)


def kernel(**inputs):
    import numpy as np
    import concourse.bacc as bacc
    from concourse.bass_utils import run_bass_kernel_spmd

    given = {name: np.asarray(a) for name, a in inputs.items()}
    arrays = {
        "x": given["L0_attn_in_features"].reshape(TOK, D),
        "wq": given["L0_attn_q_proj_weight"].T, "wk": given["L0_attn_k_proj_weight"].T,
        "wv": given["L0_attn_v_proj_weight"].T, "wo": given["L0_attn_o_proj_weight"].T,
        "router": given["L0_ffn_router_DE"],
        "w_in_shared": given["L0_ffn_w_in_shared_FD"].T, "w_swiglu": given["L0_ffn_w_swiglu_FD"].T,
        "w_out_shared": given["L0_ffn_w_out_shared_DF"].T,
        "w_in_e": given["L0_ffn_w_in_eDF"], "w_swiglu_e": given["L0_ffn_w_swiglu_eDF"],
        "w_out_e": given["L0_ffn_w_out_eFD"],
        "w_kv": given["L1_attn_W"].T,
        "w1": given["L1_ffn_W1"].T, "b1": given["L1_ffn_b1"].reshape(-1, P).T,
        "w2": given["L1_ffn_W2"].T, "b2": given["L1_ffn_b2"].reshape(1, D),
    }
    arrays = {name: np.ascontiguousarray(a) for name, a in arrays.items()}
    nc = bacc.Bacc("TRN2", target_bir_lowering=False, num_devices=1)
    io = {name: nc.dram_tensor(name, a.shape, mybir.dt.from_np(a.dtype), kind="ExternalInput").ap()
          for name, a in arrays.items()}
    io["out"] = nc.dram_tensor("out", (TOK, D), F32, kind="ExternalOutput").ap()
    program(nc, io)
    result = run_bass_kernel_spmd(nc, [arrays], core_ids=[0])
    return result.results[0]["out"].reshape(BATCH, SEQ, D)
```
